# Optimizing a Trainium2 kernel written in Bass

```python
import numpy as np
import jax
import jax.numpy as jnp

def _softmax(x, axis=-1):
    return jax.nn.softmax(x, axis=axis)

def _gelu(x):
    return jax.nn.gelu(x, approximate=True)

def _silu(x):
    return jax.nn.silu(x)

def _sigmoid(x):
    return jax.nn.sigmoid(x)

def _layernorm(x, axis=-1, eps=1e-05):
    m = jnp.mean(x, axis=axis, keepdims=True)
    v = jnp.var(x, axis=axis, keepdims=True)
    return (x - m) / jnp.sqrt(v + eps)

def _scatter_add(tgt, idx, src, axis=0):
    return tgt.at[idx].add(src)

def _segment_sum(src, seg, n):
    return jax.ops.segment_sum(src, seg, n)
kernel_name = 'mk_lm_tower_d2_tok_ids512_r4_8be05c'

def setup_inputs(seed: int=0):
    np.random.seed(seed)
    _w = jnp.asarray

    def _rec_inputs():
        import jax
        import jax.numpy as jnp
        _rk = jax.random.key(seed)
        x = jax.random.randint(jax.random.fold_in(_rk, 1), (4, 512), 0, 12564, jnp.int32)
        return x
    x = _rec_inputs()

    def _L0_tok_setup():
        import jax, jax.numpy as jnp
        import numpy as np
        VOCAB = 50257
        SEQ = 512
        EMB = 128
        BATCH = 8
        key = jax.random.key(seed)
        k1, k2, k3 = jax.random.split(key, 3)
        tokens = jax.random.randint(k1, (BATCH, SEQ), 0, VOCAB, dtype=jnp.int64 if jax.config.jax_enable_x64 else jnp.int32)
        W_emb = jax.random.normal(k2, (EMB, VOCAB), dtype=jnp.float32)
        W_pos = jax.random.normal(k3, (SEQ, EMB), dtype=jnp.float32)
        return {'tokens': tokens, 'W_emb': W_emb, 'W_pos': W_pos}
    _L0_tok_all = _L0_tok_setup()
    _L0_tok_in = {k: v for k, v in _L0_tok_all.items() if k in ('W_emb', 'W_pos')}
    del _L0_tok_all

    def _L0_attn_setup():
        import jax, jax.numpy as jnp
        import numpy as np
        B, N, D, H, E = (4, 512, 128, 8, 8192)
        HD = D // H

        def _edge_col_bias(edge_index, edge_attr, eb_w, eb_b, n):
            eb = edge_attr @ eb_w.T + eb_b
            src, tgt = (edge_index[0], edge_index[1])
            valid = (src >= 0) & (src < n) & (tgt >= 0) & (tgt < n)
            order = jnp.where(valid, jnp.arange(edge_index.shape[1]), -1)
            tgt_safe = jnp.where(valid, tgt, 0)
            last = jnp.full((n,), -1, dtype=order.dtype).at[tgt_safe].max(order)
            hit = last >= 0
            gathered = eb[jnp.maximum(last, 0)]
            col_bias = jnp.where(hit[:, None], gathered, 0.0)
            return col_bias
        key = jax.random.key(seed)
        ks = jax.random.split(key, 12)
        s = 0.02
        inp = {'x': jax.random.normal(ks[0], (B, N, D), dtype=jnp.float32), 'edge_index': jax.random.randint(ks[1], (2, E), 0, N, dtype=jnp.int64), 'edge_attr': jax.random.normal(ks[2], (E, 3), dtype=jnp.float32), 'q_w': jax.random.normal(ks[3], (D, D), dtype=jnp.float32) * s, 'q_b': jnp.zeros((D,), jnp.float32), 'k_w': jax.random.normal(ks[4], (D, D), dtype=jnp.float32) * s, 'k_b': jnp.zeros((D,), jnp.float32), 'v_w': jax.random.normal(ks[5], (D, D), dtype=jnp.float32) * s, 'v_b': jnp.zeros((D,), jnp.float32), 'o_w': jax.random.normal(ks[6], (D, D), dtype=jnp.float32) * s, 'o_b': jnp.zeros((D,), jnp.float32), 'eb_w': jax.random.normal(ks[7], (H, 3), dtype=jnp.float32) * s, 'eb_b': jnp.zeros((H,), jnp.float32)}
        return inp
    _L0_attn_all = _L0_attn_setup()
    _L0_attn_in = {k: v for k, v in _L0_attn_all.items() if k in ('edge_index', 'edge_attr', 'q_w', 'q_b', 'k_w', 'k_b', 'v_w', 'v_b', 'o_w', 'o_b', 'eb_w', 'eb_b')}
    del _L0_attn_all

    def _L0_ffn_setup():
        import jax, jax.numpy as jnp
        import numpy as np
        B, S, D, E, O = (256, 64, 128, 16, 128)
        key = jax.random.key(seed)
        k_x, k_wg, k_bg, k_we, k_be = jax.random.split(key, 5)
        scale_g = 1.0 / np.sqrt(D)
        scale_e = 1.0 / np.sqrt(D)
        return {'x': jax.random.normal(k_x, (B, S, D), dtype=jnp.float32), 'Wg': jax.random.uniform(k_wg, (D, E), jnp.float32, -scale_g, scale_g), 'bg': jax.random.uniform(k_bg, (E,), jnp.float32, -scale_g, scale_g), 'We': jax.random.uniform(k_we, (E, D, O), jnp.float32, -scale_e, scale_e), 'be': jax.random.uniform(k_be, (E, O), jnp.float32, -scale_e, scale_e)}
    _L0_ffn_all = _L0_ffn_setup()
    _L0_ffn_in = {k: v for k, v in _L0_ffn_all.items() if k in ('Wg', 'bg', 'We', 'be')}
    del _L0_ffn_all

    def _L1_attn_setup():
        import jax, jax.numpy as jnp
        import numpy as np
        D_MODEL = 128
        D_STATE = 16
        D_CONV = 4
        EXPAND = 2
        D_INNER = EXPAND * D_MODEL
        DT_RANK = (D_MODEL + 15) // 16

        def _mamba_block(x, W_in, conv_w, conv_b, W_xproj, W_dt, b_dt, A_log, D, W_out, gamma, beta):
            Bsz, L, _ = x.shape
            d_inner, d_state = A_log.shape
            dt_rank = W_dt.shape[0]
            d_conv = conv_w.shape[1]
            xz = jnp.einsum('bld,de->ble', x, W_in)
            xi, z = jnp.split(xz, 2, axis=-1)
            xc = jnp.swapaxes(xi, 1, 2)
            kernel = conv_w[:, None, :]
            xc = jax.lax.conv_general_dilated(xc, kernel, window_strides=(1,), padding=[(d_conv - 1, 0)], dimension_numbers=('NCH', 'OIH', 'NCH'), feature_group_count=d_inner)
            xc = jax.nn.silu(xc + conv_b[None, :, None])
            xc = jnp.swapaxes(xc, 1, 2)
            dbl = jnp.einsum('bld,de->ble', xc, W_xproj)
            dtr = dbl[..., :dt_rank]
            Bm = dbl[..., dt_rank:dt_rank + d_state]
            Cm = dbl[..., dt_rank + d_state:]
            dt = jax.nn.softplus(jnp.einsum('blr,rd->bld', dtr, W_dt) + b_dt)
            A = -jnp.exp(A_log)

            def step(h, inp):
                dt_t, B_t, C_t, x_t = inp
                dA = jnp.exp(dt_t[..., None] * A)
                h = h * dA + (dt_t * x_t)[..., None] * B_t[:, None, :]
                y_t = jnp.einsum('bds,bs->bd', h, C_t)
                return (h, y_t)
            h0 = jnp.zeros((Bsz, d_inner, d_state), x.dtype)
            xs = (jnp.swapaxes(dt, 0, 1), jnp.swapaxes(Bm, 0, 1), jnp.swapaxes(Cm, 0, 1), jnp.swapaxes(xc, 0, 1))
            _, ys = jax.lax.scan(step, h0, xs)
            y = jnp.swapaxes(ys, 0, 1)
            y = y + xc * D
            y = y * jax.nn.silu(z)
            out = jnp.einsum('bld,dm->blm', y, W_out)
            h2 = out + x
            mu = jnp.mean(h2, axis=-1, keepdims=True)
            var = jnp.mean((h2 - mu) ** 2, axis=-1, keepdims=True)
            return (h2 - mu) / jnp.sqrt(var + 1e-05) * gamma + beta
        key = jax.random.key(seed)
        ks = jax.random.split(key, 10)
        B, L = (2, 512)
        s = 0.02
        inp = {'x': jax.random.normal(ks[0], (B, L, D_MODEL), jnp.float32), 'W_in': jax.random.normal(ks[1], (D_MODEL, 2 * D_INNER), jnp.float32) * s, 'conv_w': jax.random.normal(ks[2], (D_INNER, D_CONV), jnp.float32) * s, 'conv_b': jnp.zeros((D_INNER,), jnp.float32), 'W_xproj': jax.random.normal(ks[3], (D_INNER, DT_RANK + 2 * D_STATE), jnp.float32) * s, 'W_dt': jax.random.normal(ks[4], (DT_RANK, D_INNER), jnp.float32) * s, 'b_dt': jax.random.normal(ks[5], (D_INNER,), jnp.float32) * s, 'A_log': jnp.tile(jnp.log(jnp.arange(1, D_STATE + 1, dtype=jnp.float32))[None, :], (D_INNER, 1)), 'D': jnp.ones((D_INNER,), jnp.float32), 'W_out': jax.random.normal(ks[6], (D_INNER, D_MODEL), jnp.float32) * s, 'gamma': jnp.ones((D_MODEL,), jnp.float32), 'beta': jnp.zeros((D_MODEL,), jnp.float32)}
        return inp
    _L1_attn_all = _L1_attn_setup()
    _L1_attn_in = {k: v for k, v in _L1_attn_all.items() if k in ('W_in', 'conv_w', 'conv_b', 'W_xproj', 'W_dt', 'b_dt', 'A_log', 'D', 'W_out', 'gamma', 'beta')}
    del _L1_attn_all

    def _L1_ffn_setup():
        import jax, jax.numpy as jnp
        import numpy as np
        D, H, E, B, S = (128, 512, 16, 8, 2048)
        MAX_GROUP_SIZE = 1024
        MIN_CAPACITY = 8
        CAPACITY_FACTOR = 1.0

        def _group_dims(num_tokens, num_experts):
            num_groups = -(-num_tokens // MAX_GROUP_SIZE)
            while num_tokens % num_groups != 0 or num_groups % num_experts != 0:
                num_groups += 1
            return (num_tokens // num_groups, num_groups)
        key = jax.random.key(seed)
        ks = jax.random.split(key, 6)
        s = 0.02
        return {'x': jax.random.normal(ks[0], (B, S, D), jnp.float32), 'gate_w': jax.random.normal(ks[1], (D, E), jnp.float32) * s, 'w1': jax.random.normal(ks[2], (E, D, H), jnp.float32) * s, 'b1': jnp.zeros((E, H), jnp.float32), 'w2': jax.random.normal(ks[3], (E, H, D), jnp.float32) * s, 'b2': jnp.zeros((E, D), jnp.float32), 'sw1': jax.random.normal(ks[4], (D, H), jnp.float32) * s, 'sb1': jnp.zeros((H,), jnp.float32), 'sw2': jax.random.normal(ks[5], (H, D), jnp.float32) * s, 'sb2': jnp.zeros((D,), jnp.float32)}
    _L1_ffn_all = _L1_ffn_setup()
    _L1_ffn_in = {k: v for k, v in _L1_ffn_all.items() if k in ('gate_w', 'w1', 'b1', 'w2', 'b2', 'sw1', 'sb1', 'sw2', 'sb2')}
    del _L1_ffn_all
    return {'x': x, 'L0_tok_W_emb': _L0_tok_in['W_emb'], 'L0_tok_W_pos': _L0_tok_in['W_pos'], 'L0_attn_edge_index': _L0_attn_in['edge_index'], 'L0_attn_edge_attr': _L0_attn_in['edge_attr'], 'L0_attn_q_w': _L0_attn_in['q_w'], 'L0_attn_q_b': _L0_attn_in['q_b'], 'L0_attn_k_w': _L0_attn_in['k_w'], 'L0_attn_k_b': _L0_attn_in['k_b'], 'L0_attn_v_w': _L0_attn_in['v_w'], 'L0_attn_v_b': _L0_attn_in['v_b'], 'L0_attn_o_w': _L0_attn_in['o_w'], 'L0_attn_o_b': _L0_attn_in['o_b'], 'L0_attn_eb_w': _L0_attn_in['eb_w'], 'L0_attn_eb_b': _L0_attn_in['eb_b'], 'L0_ffn_Wg': _L0_ffn_in['Wg'], 'L0_ffn_bg': _L0_ffn_in['bg'], 'L0_ffn_We': _L0_ffn_in['We'], 'L0_ffn_be': _L0_ffn_in['be'], 'L1_attn_W_in': _L1_attn_in['W_in'], 'L1_attn_conv_w': _L1_attn_in['conv_w'], 'L1_attn_conv_b': _L1_attn_in['conv_b'], 'L1_attn_W_xproj': _L1_attn_in['W_xproj'], 'L1_attn_W_dt': _L1_attn_in['W_dt'], 'L1_attn_b_dt': _L1_attn_in['b_dt'], 'L1_attn_A_log': _L1_attn_in['A_log'], 'L1_attn_D': _L1_attn_in['D'], 'L1_attn_W_out': _L1_attn_in['W_out'], 'L1_attn_gamma': _L1_attn_in['gamma'], 'L1_attn_beta': _L1_attn_in['beta'], 'L1_ffn_gate_w': _L1_ffn_in['gate_w'], 'L1_ffn_w1': _L1_ffn_in['w1'], 'L1_ffn_b1': _L1_ffn_in['b1'], 'L1_ffn_w2': _L1_ffn_in['w2'], 'L1_ffn_b2': _L1_ffn_in['b2'], 'L1_ffn_sw1': _L1_ffn_in['sw1'], 'L1_ffn_sb1': _L1_ffn_in['sb1'], 'L1_ffn_sw2': _L1_ffn_in['sw2'], 'L1_ffn_sb2': _L1_ffn_in['sb2']}

def reference(x, L0_tok_W_emb, L0_tok_W_pos, L0_attn_edge_index, L0_attn_edge_attr, L0_attn_q_w, L0_attn_q_b, L0_attn_k_w, L0_attn_k_b, L0_attn_v_w, L0_attn_v_b, L0_attn_o_w, L0_attn_o_b, L0_attn_eb_w, L0_attn_eb_b, L0_ffn_Wg, L0_ffn_bg, L0_ffn_We, L0_ffn_be, L1_attn_W_in, L1_attn_conv_w, L1_attn_conv_b, L1_attn_W_xproj, L1_attn_W_dt, L1_attn_b_dt, L1_attn_A_log, L1_attn_D, L1_attn_W_out, L1_attn_gamma, L1_attn_beta, L1_ffn_gate_w, L1_ffn_w1, L1_ffn_b1, L1_ffn_w2, L1_ffn_b2, L1_ffn_sw1, L1_ffn_sb1, L1_ffn_sw2, L1_ffn_sb2):
    import jax
    import jax.numpy as jnp

    def _L0_tok_ref(tokens, W_emb, W_pos):
        import jax, jax.numpy as jnp
        import numpy as np
        VOCAB = 50257
        SEQ = 512
        EMB = 128
        BATCH = 8
        tok_emb = jnp.take(W_emb.T, tokens, axis=0)
        return tok_emb + W_pos

    def _L0_attn_ref(x, edge_index, edge_attr, q_w, q_b, k_w, k_b, v_w, v_b, o_w, o_b, eb_w, eb_b):
        import jax, jax.numpy as jnp
        import numpy as np
        B, N, D, H, E = (4, 512, 128, 8, 8192)
        HD = D // H

        def _edge_col_bias(edge_index, edge_attr, eb_w, eb_b, n):
            eb = edge_attr @ eb_w.T + eb_b
            src, tgt = (edge_index[0], edge_index[1])
            valid = (src >= 0) & (src < n) & (tgt >= 0) & (tgt < n)
            order = jnp.where(valid, jnp.arange(edge_index.shape[1]), -1)
            tgt_safe = jnp.where(valid, tgt, 0)
            last = jnp.full((n,), -1, dtype=order.dtype).at[tgt_safe].max(order)
            hit = last >= 0
            gathered = eb[jnp.maximum(last, 0)]
            col_bias = jnp.where(hit[:, None], gathered, 0.0)
            return col_bias
        b, n, d = x.shape
        q = (x @ q_w.T + q_b).reshape(b, n, H, HD)
        k = (x @ k_w.T + k_b).reshape(b, n, H, HD)
        v = (x @ v_w.T + v_b).reshape(b, n, H, HD)
        scores = jnp.einsum('bnhd,bmhd->bhnm', q, k) / jnp.sqrt(jnp.float32(HD))
        col_bias = _edge_col_bias(edge_index, edge_attr, eb_w, eb_b, n)
        scores = scores + col_bias.T[None, :, None, :]
        attn = jax.nn.softmax(scores, axis=-1)
        out = jnp.einsum('bhnm,bmhd->bnhd', attn, v).reshape(b, n, d)
        return out @ o_w.T + o_b

    def _L0_ffn_ref(x, Wg, bg, We, be):
        import jax, jax.numpy as jnp
        import numpy as np
        B, S, D, E, O = (256, 64, 128, 16, 128)
        scores = jax.nn.softmax(jnp.mean(x, axis=1) @ Wg + bg, axis=-1)
        idx = jnp.argmax(scores, axis=-1)
        gate = jnp.take_along_axis(scores, idx[:, None], axis=-1)
        W_sel = We[idx]
        b_sel = be[idx]
        y = jnp.einsum('bsd,bdo->bso', x, W_sel) + b_sel[:, None, :]
        return gate[:, :, None] * y

    def _L1_attn_ref(x, W_in, conv_w, conv_b, W_xproj, W_dt, b_dt, A_log, D, W_out, gamma, beta):
        import jax, jax.numpy as jnp
        import numpy as np
        D_MODEL = 128
        D_STATE = 16
        D_CONV = 4
        EXPAND = 2
        D_INNER = EXPAND * D_MODEL
        DT_RANK = (D_MODEL + 15) // 16

        def _mamba_block(x, W_in, conv_w, conv_b, W_xproj, W_dt, b_dt, A_log, D, W_out, gamma, beta):
            Bsz, L, _ = x.shape
            d_inner, d_state = A_log.shape
            dt_rank = W_dt.shape[0]
            d_conv = conv_w.shape[1]
            xz = jnp.einsum('bld,de->ble', x, W_in)
            xi, z = jnp.split(xz, 2, axis=-1)
            xc = jnp.swapaxes(xi, 1, 2)
            kernel = conv_w[:, None, :]
            xc = jax.lax.conv_general_dilated(xc, kernel, window_strides=(1,), padding=[(d_conv - 1, 0)], dimension_numbers=('NCH', 'OIH', 'NCH'), feature_group_count=d_inner)
            xc = jax.nn.silu(xc + conv_b[None, :, None])
            xc = jnp.swapaxes(xc, 1, 2)
            dbl = jnp.einsum('bld,de->ble', xc, W_xproj)
            dtr = dbl[..., :dt_rank]
            Bm = dbl[..., dt_rank:dt_rank + d_state]
            Cm = dbl[..., dt_rank + d_state:]
            dt = jax.nn.softplus(jnp.einsum('blr,rd->bld', dtr, W_dt) + b_dt)
            A = -jnp.exp(A_log)

            def step(h, inp):
                dt_t, B_t, C_t, x_t = inp
                dA = jnp.exp(dt_t[..., None] * A)
                h = h * dA + (dt_t * x_t)[..., None] * B_t[:, None, :]
                y_t = jnp.einsum('bds,bs->bd', h, C_t)
                return (h, y_t)
            h0 = jnp.zeros((Bsz, d_inner, d_state), x.dtype)
            xs = (jnp.swapaxes(dt, 0, 1), jnp.swapaxes(Bm, 0, 1), jnp.swapaxes(Cm, 0, 1), jnp.swapaxes(xc, 0, 1))
            _, ys = jax.lax.scan(step, h0, xs)
            y = jnp.swapaxes(ys, 0, 1)
            y = y + xc * D
            y = y * jax.nn.silu(z)
            out = jnp.einsum('bld,dm->blm', y, W_out)
            h2 = out + x
            mu = jnp.mean(h2, axis=-1, keepdims=True)
            var = jnp.mean((h2 - mu) ** 2, axis=-1, keepdims=True)
            return (h2 - mu) / jnp.sqrt(var + 1e-05) * gamma + beta
        return _mamba_block(x, W_in, conv_w, conv_b, W_xproj, W_dt, b_dt, A_log, D, W_out, gamma, beta)

    def _L1_ffn_ref(x, gate_w, w1, b1, w2, b2, sw1, sb1, sw2, sb2):
        import jax, jax.numpy as jnp
        import numpy as np
        D, H, E, B, S = (128, 512, 16, 8, 2048)
        MAX_GROUP_SIZE = 1024
        MIN_CAPACITY = 8
        CAPACITY_FACTOR = 1.0

        def _group_dims(num_tokens, num_experts):
            num_groups = -(-num_tokens // MAX_GROUP_SIZE)
            while num_tokens % num_groups != 0 or num_groups % num_experts != 0:
                num_groups += 1
            return (num_tokens // num_groups, num_groups)
        Bn, Sn, Dn = x.shape
        En = gate_w.shape[1]
        T = Bn * Sn
        group_size, num_groups = _group_dims(T, En)
        cap = max(int(round(CAPACITY_FACTOR * group_size * num_groups / En)), MIN_CAPACITY)
        xg = x.reshape(num_groups, group_size, Dn)
        logits = jnp.einsum('gsd,de->gse', xg, gate_w)
        probs = jax.nn.softmax(logits, axis=-1)
        flat_probs = probs.transpose(2, 0, 1).reshape(En, T)
        scores, tok_idx = jax.lax.top_k(flat_probs, cap)
        xf = x.reshape(T, Dn)
        toks = xf[tok_idx]
        h = jax.nn.gelu(jnp.einsum('ecd,edh->ech', toks, w1) + b1[:, None, :])
        y = jnp.einsum('ech,ehd->ecd', h, w2) + b2[:, None, :]
        y = y * scores[..., None]
        routed = jnp.zeros_like(xf).at[tok_idx.reshape(-1)].add(y.reshape(-1, Dn))
        shared = jax.nn.gelu(xf @ sw1 + sb1) @ sw2 + sb2
        out = (routed + shared).reshape(Bn, Sn, Dn)
        return out
    h = _L0_tok_ref(x, L0_tok_W_emb, L0_tok_W_pos)
    h = h + _L0_attn_ref(_layernorm(h, axis=-1), L0_attn_edge_index, L0_attn_edge_attr, L0_attn_q_w, L0_attn_q_b, L0_attn_k_w, L0_attn_k_b, L0_attn_v_w, L0_attn_v_b, L0_attn_o_w, L0_attn_o_b, L0_attn_eb_w, L0_attn_eb_b)
    h = h + _L0_ffn_ref(_layernorm(h, axis=-1), L0_ffn_Wg, L0_ffn_bg, L0_ffn_We, L0_ffn_be)
    h = h + _L1_attn_ref(_layernorm(h, axis=-1), L1_attn_W_in, L1_attn_conv_w, L1_attn_conv_b, L1_attn_W_xproj, L1_attn_W_dt, L1_attn_b_dt, L1_attn_A_log, L1_attn_D, L1_attn_W_out, L1_attn_gamma, L1_attn_beta)
    h = h + _L1_ffn_ref(_layernorm(h, axis=-1), L1_ffn_gate_w, L1_ffn_w1, L1_ffn_b1, L1_ffn_w2, L1_ffn_b2, L1_ffn_sw1, L1_ffn_sb1, L1_ffn_sw2, L1_ffn_sb2)
    return h

_drawn_inputs = setup_inputs


def setup_inputs(seed=0):
    import zlib

    import numpy as np

    out = dict(_drawn_inputs(seed))
    spreads = {'L0_attn_q_b': (0.0, 0.8),
     'L0_attn_k_b': (0.0, 2.0),
     'L0_attn_v_b': (0.0, 0.323),
     'L0_attn_o_b': (0.0, 0.1),
     'L0_attn_eb_b': (0.0, 2.0),
     'L1_attn_conv_b': (0.0, 0.8),
     'L1_attn_D': (1.0, 0.6),
     'L1_attn_gamma': (1.0, 0.2),
     'L1_attn_beta': (0.0, 0.1),
     'L1_ffn_b1': (0.0, 0.8),
     'L1_ffn_b2': (0.0, 0.8),
     'L1_ffn_sb1': (0.0, 0.8),
     'L1_ffn_sb2': (0.0, 0.1)}
    factors = {'L0_attn_edge_attr': 8.0,
     'L0_attn_q_w': 8.0,
     'L0_attn_k_w': 8.0,
     'L0_attn_v_w': 8.0,
     'L0_attn_eb_w': 8.0,
     'L0_ffn_Wg': 2.832,
     'L0_ffn_be': 8.0,
     'L1_attn_W_in': 8.0,
     'L1_attn_conv_w': 8.0,
     'L1_attn_W_xproj': 8.0,
     'L1_attn_W_dt': 8.0,
     'L1_attn_b_dt': 8.0,
     'L1_attn_A_log': 8.0,
     'L1_attn_W_out': 8.0,
     'L1_ffn_gate_w': 8.0,
     'L1_ffn_w1': 8.0,
     'L1_ffn_w2': 8.0,
     'L1_ffn_sw1': 2.674}
    for name, (base, spread) in spreads.items():
        noise = np.random.default_rng([zlib.crc32(name.encode()), seed]).standard_normal(out[name].shape)
        drawn = base * np.exp(spread * noise) if base else spread * noise
        out[name] = jnp.asarray(drawn.astype(out[name].dtype))
    for name, factor in factors.items():
        out[name] = (out[name] * factor).astype(out[name].dtype)
    return out
```

```python
from contextlib import ExitStack

import numpy as np

import concourse.bass as bass
from concourse import mybir

F32 = mybir.dt.float32
BF16 = mybir.dt.bfloat16
I32 = mybir.dt.int32
U32 = mybir.dt.uint32
ACT = mybir.ActivationFunctionType
ALU = mybir.AluOpType
AX = mybir.AxisListType

P = 128
B, N, D = 4, 512, 128
T = B * N
NT = T // P
TB = N // P
H, HD = 8, 16
G = 4
NG = H // G
EDGES = 8192
EPS = 1e-5
EXPERTS0 = 16
DI, DS, DR, DC = 256, 16, 8, 4
NH = DI // P
E1, HID = 16, 512
CAP = T // E1
HC = HID // P
FAR = 5000.0
Q_PART = (0, 0, 1, 0, 2, 1)
K_PART = (0, 1, 0, 2, 0, 1)
NTERM = len(Q_PART)
ROW_CB = NTERM * HD
ROW_MAX = ROW_CB + 3
ROWS_A, ROWS_B = ROW_MAX, ROW_MAX + 3
UNITS = B * H
LAG = 10
SPAN = 1024
NSPAN = T // SPAN
ROUTE = D + E1
BITS = 30
AHEAD = 4
A1, B1 = 16, 8


def slots():
    out = []
    for u in range(UNITS + LAG + 10):
        now = []
        v = u - LAG
        if u < UNITS:
            now.append(("scores", u))
        if u % H == 0 and 0 < u <= UNITS:
            now.append(("turn_max", u // H - 1))
        if 0 <= v < UNITS:
            now.append(("probs", v))
        if v >= 5 and (v - 5) % G == 0 and (v - 5) // G < B * NG:
            now.append(("pv", (v - 5) // G))
        if v >= 6 and (v - 6) % G == 0 and (v - 6) // G < B * NG:
            now.append(("turn_out", (v - 6) // G))
        if v >= 12 and (v - 12) % H == 0 and (v - 12) // H < B:
            now.append(("turn_back", (v - 12) // H))
        if v >= 13 and (v - 13) % H == 0 and (v - 13) // H < B:
            now.append(("project", (v - 13) // H))
        if v >= 15 and (v - 15) % H == 0 and (v - 15) // H < B:
            now.append(("norm", (v - 15) // H))
        out.append(now)
    return out


SLOTS = slots()
BANK_USES = ("turn_max", "turn_out", "turn_back", "project", "norm")
BANK_USE = {piece: k for k, piece in enumerate(p for now in SLOTS for p in now if p[0] in BANK_USES)}


def tower_kernel(nc, ids, emb, pos, edges, wanted, attrs, ebw, ident, identb, ones,
                 wq, wk, wv, wo, qb, kb, vb, ob,
                 lane, wg0, bg0, we0, be0,
                 w_in, conv_w, conv_b, w_x, c_pick, w_dt, b_dt, a_log, d_skip, w_out, gamma, beta,
                 gate_w, w1, b1, w2, b2, sw1, sb1, sw2, sb2,
                 same_expert, bit_values, before, onesb, run_start, a_iota, b_iota, tile_of, own_expert,
                 out):
    ctx = ExitStack()
    with ctx:
        def sb(name, shape, dt=F32, stack=ctx):
            return stack.enter_context(nc.sbuf_tensor(name, shape, dt))

        def sem(name):
            return ctx.enter_context(nc.semaphore(name))

        def dram(name, shape, dt=F32):
            return nc.dram_tensor(name, shape, dt, kind="Internal").ap()

        h = sb("h", [P, NT, D])
        xn = sb("xn", [P, NT, D])
        xT = sb("xT", [P, T])
        stats = sb("stats", [P, NT, 6])
        mv = sb("mv", [P, NT, 2])
        rstd = sb("rstd", [P, NT])
        vare = sb("vare", [P, NT])
        minus_half = sb("minus_half", [P, TB])
        id_f = sb("id_f", [P, P])
        id_b = sb("id_b", [P, P], BF16)

        ones_f = sb("ones_f", [P, P])
        lane_sb = sb("lane_sb", [P, 1])
        pooled = sb("pooled", [P, B])
        wg_sb = sb("wg_sb", [P, EXPERTS0])
        bg_sb = sb("bg_sb", [B, EXPERTS0])
        win_sb = sb("win_sb", [P, 2 * DI])
        cw_sb = sb("cw_sb", [P, NH, DC])
        cvb_sb = sb("cvb_sb", [P, NH])
        wx_sb = sb("wx_sb", [P, NH, P])
        pick_sb = sb("pick_sb", [P, DS, P], BF16)
        wdt_sb = sb("wdt_sb", [DR, DI])
        bdt_sb = sb("bdt_sb", [P, NH])
        a_sb = sb("a_sb", [P, NH, DS])
        ds_sb = sb("ds_sb", [P, NH])
        wout_sb = sb("wout_sb", [P, NH, D])
        gamma_sb = sb("gamma_sb", [P, D])
        beta_sb = sb("beta_sb", [P, D])

        ps = ctx.enter_context(nc.psum_tensor("ps", [P, 8, 512], F32))

        att = ExitStack()
        ids_sb = sb("ids_sb", [P, NT], I32, att)
        pos_sb = sb("pos_sb", [P, TB, D], F32, att)
        edge_sb = sb("edge_sb", [P, 2, EDGES // P], I32, att)
        edge_f = sb("edge_f", [P, 8, EDGES // P], F32, att)
        want_sb = sb("want_sb", [P, 8], F32, att)
        last = sb("last", [P, 8], U32, att)
        last_f = sb("last_f", [P, TB], F32, att)
        hit = sb("hit", [P, TB], F32, att)
        last_i = sb("last_i", [P, TB], I32, att)
        edge_a = sb("edge_a", [P, TB, 3], F32, att)
        ebw_sb = sb("ebw_sb", [P, 4, H], F32, att)
        cb = sb("cb", [P, 2, TB, H], F32, att)
        cb_part = sb("cb_part", [P, 3, H, TB], BF16, att)
        cb_rest = sb("cb_rest", [P, H, TB], F32, att)
        cb_row = sb("cb_row", [3 * H * TB, P], BF16, att)
        wq_sb = sb("wq_sb", [P, P], F32, att)
        wk_sb = sb("wk_sb", [P, P], F32, att)
        wv_sb = sb("wv_sb", [P, P], F32, att)
        wo_sb = sb("wo_sb", [P, P], F32, att)
        qb_sb = sb("qb_sb", [P, 1], F32, att)
        qb4 = sb("qb4", [P, 1], F32, att)
        kb_sb = sb("kb_sb", [P, 1], F32, att)
        vb_sb = sb("vb_sb", [P, D], F32, att)
        ob_sb = sb("ob_sb", [1, D], F32, att)
        qk = sb("qk", [P, 2, 2, N], F32, att)
        qk_rest = sb("qk_rest", [P, 2, N], F32, att)
        qk_part = sb("qk_part", [P, 2, 2, 3, N], BF16, att)
        q_stack = sb("q_stack", [P, 3, H, N], BF16, att)
        k_stack = sb("k_stack", [P, 3, H, N], BF16, att)
        v_aug = sb("v_aug", [P, NT, H, 2 * HD], F32, att)
        nmax = sb("nmax", [P, 2, H * TB], F32, att)
        nmax_rest = sb("nmax_rest", [P, H * TB], F32, att)
        nmax_part = sb("nmax_part", [P, 2, 3, H * TB], BF16, att)
        nmax_row = sb("nmax_row", [3 * H * TB, 2, P], BF16, att)
        probs_mem = sb("probs_mem", [P, 2 * G * TB * N], F32, att)
        probs = probs_mem[:].rearrange("p (a g t n) -> p a g t n", a=2, g=G, t=TB)
        keys = probs_mem[:, 0:EDGES + 8]
        oT = sb("oT", [P, 2, N], F32, att)
        r_den = sb("r_den", [P, TB, G], F32, att)
        o_nat = sb("o_nat", [P, TB, H, HD], F32, att)
        onT = sb("onT", [P, N], F32, att)
        att.close()

        mam = ExitStack()
        small = sb("small", [B, 96], F32, mam)
        top_i = sb("top_i", [B, 8], U32, mam)
        pick_b = sb("pick_b", [P, 2 * B], F32, mam)
        off_w = sb("off_w", [P, B], I32, mam)
        off_b = sb("off_b", [P, B], I32, mam)
        w_sel = sb("w_sel", [P, 2, B, D], F32, mam)
        b_sel = sb("b_sel", [P, 2, B, D], F32, mam)
        xi = sb("xi", [P, NH, B, N + DC - 1], F32, mam)
        sz = sb("sz", [P, NH, T], F32, mam)
        xc = sb("xc", [P, NH, T], F32, mam)
        dt = sb("dt", [P, NH, T], F32, mam)
        dtx = sb("dtx", [P, NH, T], F32, mam)
        dbl = sb("dbl", [32, T], F32, mam)
        c_stack = sb("c_stack", [P, T], BF16, mam)
        c_rest = sb("c_rest", [P, 2, N], F32, mam)
        c_mid = sb("c_mid", [P, 2, N], BF16, mam)
        a_neg = sb("a_neg", [P, NH, DS], F32, mam)
        d_diag = sb("d_diag", [P, NH, P], F32, mam)
        decay = sb("decay", [P, 4, SPAN], F32, mam)
        drive = sb("drive", [P, 4, SPAN], F32, mam)
        state = sb("state", [P, 2, SPAN], F32, mam)
        read_out = sb("read_out", [P, 2, SPAN], F32, mam)
        conv = read_out[:].rearrange("p k (j n) -> p (k j) n", n=N)
        b_row = sb("b_row", [P, 2, SPAN], F32, mam)
        mam.close()

        moe = ExitStack()
        w1_sb = sb("w1_sb", [P, E1, HID], F32, moe)
        w2_sb = sb("w2_sb", [P, E1, HC, D], F32, moe)
        b1_sb = sb("b1_sb", [P, E1, HC], F32, moe)
        b2_sb = sb("b2_sb", [1, E1, D], F32, moe)
        sw1_sb = sb("sw1_sb", [P, HID], F32, moe)
        sw2_sb = sb("sw2_sb", [P, HC, D], F32, moe)
        sb1_sb = sb("sb1_sb", [P, HC], F32, moe)
        sb2_sb = sb("sb2_sb", [1, D], F32, moe)
        gw_sb = sb("gw_sb", [P, E1], F32, moe)
        same_sb = sb("same_sb", [P, P], F32, moe)
        bits_sb = sb("bits_sb", [P, BITS], I32, moe)
        before_sb = sb("before_sb", [P, P], BF16, moe)
        onesb_sb = sb("onesb_sb", [P, P], BF16, moe)
        start_sb = sb("start_sb", [P, E1 * NT], F32, moe)
        ai_sb = sb("ai_sb", [P, A1], BF16, moe)
        bi_sb = sb("bi_sb", [P, B1], BF16, moe)
        tile_sb = sb("tile_sb", [P, E1 * NT, B1], BF16, moe)
        own_sb = sb("own_sb", [P, B1], F32, moe)
        logit = sb("logit", [P, NT, E1], F32, moe)
        prob = sb("prob", [P, NT, E1], F32, moe)
        rowmax = sb("rowmax", [P, 3, NT], F32, moe)
        prob_x = sb("prob_x", [P, 2 * P], F32, moe)
        hits_x = sb("hits_x", [P, 2 * P], F32, moe)
        thr = sb("thr", [P, 1], I32, moe)
        cand = sb("cand", [P, 1], I32, moe)
        enough = sb("enough", [P, 1], I32, moe)
        count = sb("count", [P, 1], F32, moe)
        thr_b = sb("thr_b", [P, P], F32, moe)
        thr_n = sb("thr_n", [P, E1], F32, moe)
        need = sb("need", [P, E1], F32, moe)
        over = sb("over", [P, E1, NT], BF16, moe)
        even = sb("even", [P, E1, NT], BF16, moe)
        run = sb("run", [P, 2, E1, NT], F32, moe)
        run_b = sb("run_b", [P, 2, E1, NT], BF16, moe)
        picked = sb("picked", [P, 3, E1, NT], F32, moe)
        picked_b = sb("picked_b", [P, E1, NT], BF16, moe)
        slot_i = sb("slot_i", [P, 3, E1, NT], I32, moe)
        slot_b = sb("slot_b", [P, 2, E1, NT], BF16, moe)
        hot_a = sb("hot_a", [P, NT, E1, A1], BF16, moe)
        hot_b = sb("hot_b", [P, E1 * NT, B1], BF16, moe)
        val_b = sb("val_b", [P, E1, NT, 2, B1], BF16, moe)
        diag = sb("diag", [P, B1, 2 * B1], F32, moe)
        idx_v = sb("idx_v", [P, 2, 2 * B1], F32, moe)
        idx_i = sb("idx_i", [P, 2, B1], I32, moe)
        idx_t = sb("idx_t", [P, E1], I32, moe)
        rows = sb("rows", [P, E1, ROUTE], F32, moe)
        rowsT = sb("rowsT", [P, 2, P], F32, moe)
        hid = sb("hid", [P, 2, HC, P], F32, moe)
        pre = sb("pre", [P, 2, HC, P], F32, moe)
        shid = sb("shid", [P, 2, HC, N], F32, moe)
        routed = sb("routed", [P, E1, D], F32, moe)
        moe.close()

        key_d = dram("key_d", [EDGES])
        part_d = dram("part_d", [B, P, 2, 3, N], BF16)

        b_d = dram("b_d", [DS, T])
        route_d = dram("route_d", [T, ROUTE])
        idx_d = dram("idx_d", [E1 * CAP], I32)

        ids_in, pos_in, edges_in, proj_in, const_in, ebw_in = (
            sem(n) for n in ("ids_in", "pos_in", "edges_in", "proj_in", "const_in", "ebw_in"))
        emb_in = [sem(f"emb_in{b}") for b in range(B)]
        keys_out, keys_in, attr_in = sem("keys_out"), sem("keys_in"), sem("attr_in")
        key_done, last_done = sem("key_done"), sem("last_done")
        minus_half_set = sem("minus_half_set")
        dve_step, act_step, pool_step = sem("dve_step"), sem("act_step"), sem("pool_step")
        ln_mv, ln_rstd, ln_done = sem("ln_mv"), sem("ln_rstd"), sem("ln_done")
        turned, xT_done = sem("turned"), sem("xT_done")
        qkv_full, v_read = sem("qkv_full"), sem("v_read")
        part_cast, part_rest, parts_done = sem("part_cast"), sem("part_rest"), sem("parts_done")
        parts_out = [sem(f"parts_out{b}") for b in range(B)]
        stack_in = [sem(f"stack_in{b}") for b in range(B)]
        ones_in, row_in = sem("ones_in"), sem("row_in")
        cb_parts, cb_turned, cb_rows, cb_in = sem("cb_parts"), sem("cb_turned"), sem("cb_rows"), sem("cb_in")
        scores_full, scores_read = sem("scores_full"), sem("scores_read")
        max_parts = sem("max_parts")
        max_in = [sem(f"max_in{b}") for b in range(B)]
        expo_full, expo_read = sem("expo_full"), sem("expo_read")
        pv_full, pv_read = sem("pv_full"), sem("pv_read")
        bank_full, bank_read = sem("bank_full"), sem("bank_read")
        out_done = sem("out_done")
        lane_in, ffn_in, mamba_in, moe_in, moe_w_in = (
            sem(n) for n in ("lane_in", "ffn_in", "mamba_in", "moe_in", "moe_w_in"))
        gate_full, gate_exp, gate_diag, gate_rows, gate_off, sel_in, sel_done, y0_full = (
            sem(n) for n in ("gate_full", "gate_exp", "gate_diag", "gate_rows", "gate_off", "sel_in",
                             "sel_done", "y0_full"))
        gate_arg = sem("gate_arg")
        turned3, xT3_done = sem("turned3"), sem("xT3_done")
        pads_set, xz_full, xi_done, z_done = sem("pads_set"), sem("xz_full"), sem("xi_done"), sem("z_done")
        conv_done, xc_done = sem("conv_done"), sem("xc_done")
        dbl_full, dbl_done, c_cast, c_read0, c_done = (
            sem(n) for n in ("dbl_full", "dbl_done", "c_cast", "c_read0", "c_done"))
        b_out = sem("b_out")
        dt_full, dt_abs, dt_relu, dt_log, dt_done, dtx_done = (
            sem(n) for n in ("dt_full", "dt_abs", "dt_relu", "dt_log", "dt_done", "dtx_done"))
        a_done, diag_done, edge_zero = sem("a_done"), sem("diag_done"), sem("edge_zero")
        row_b_in = [sem(f"row_b_in{j}") for j in range(2)]
        c_full, c_used, b_used = sem("c_full"), sem("c_used"), sem("b_used")
        decay_full, drive_full, scanned, read_full, y_added = (
            sem(n) for n in ("decay_full", "drive_full", "scanned", "read_full", "y_added"))
        y_full, y_done = sem("y_full"), sem("y_done")
        out1_full, post_h2, h3_done = sem("out1_full"), sem("post_h2"), sem("h3_done")
        turned4, xT4_done = sem("turned4"), sem("xT4_done")
        logits_full, shifted, exped, probs_done, probs_turned, prob_x_done = (
            sem(n) for n in ("logits_full", "shifted", "exped", "probs_done", "probs_turned", "prob_x_done"))
        route_out = sem("route_out")
        counted, summed, bit_step = sem("counted"), sem("summed"), sem("bit_step")
        thr_ready, thr_turned = sem("thr_ready"), sem("thr_turned")
        runs_done, ranks_full = sem("runs_done"), sem("ranks_full")
        hot_done, idx_full, idx_done, idx_out, idx_in = (
            sem(n) for n in ("hot_done", "idx_full", "idx_done", "idx_out", "idx_in"))
        shid_full, shid_done, sy_full, base_done, base_out = (
            sem(n) for n in ("shid_full", "shid_done", "sy_full", "base_done", "base_out"))
        rows_in = [sem(f"rows_in{e}") for e in range(AHEAD)]
        rows_turned, rowsT_done, eh_full, pre_done, eh_done, ey_full, routed_done = (
            sem(n) for n in ("rows_turned", "rowsT_done", "eh_full", "pre_done", "eh_done", "ey_full",
                             "routed_done"))
        added = sem("added")

        block = ctx.enter_context(nc.Block())

        def tile_cols(i):
            return slice(i * P, (i + 1) * P)

        @block.sync
        def _(sp):
            sp.dma_start(ids_sb[:], ids).then_inc(ids_in, 16)
            sp.dma_start(edge_sb[:], edges).then_inc(edges_in, 16)
            sp.dma_start(pos_sb[:], pos).then_inc(pos_in, 16)
            sp.dma_start(id_f[:], ident).then_inc(const_in, 16)
            sp.dma_start(id_b[:], identb).then_inc(const_in, 16)
            for dst, src in ((wq_sb, wq), (wk_sb, wk), (wv_sb, wv), (wo_sb, wo), (qb_sb, qb), (kb_sb, kb),
                             (vb_sb, vb), (ob_sb, ob)):
                sp.dma_start(dst[:], src).then_inc(proj_in, 16)
            sp.dma_start(q_stack[ROW_CB:ROW_MAX], ones).then_inc(row_in, 16)
            sp.dma_start(k_stack[ROW_MAX:ROWS_B], ones).then_inc(row_in, 16)
            sp.dma_start(lane_sb[:], lane).then_inc(lane_in, 16)
            sp.dma_start(wg_sb[:], wg0).then_inc(ffn_in, 16)
            sp.dma_start(bg_sb[:], bg0).then_inc(ffn_in, 16)
            sp.dma_start(want_sb[:], wanted).then_inc(ebw_in, 16)
            sp.dma_start(ebw_sb[:], ebw).then_inc(ebw_in, 16)
            sp.dma_start(keys[:, EDGES:], wanted).then_inc(ebw_in, 16)
            sp.wait_ge(key_done, 1)
            sp.dma_start(key_d.rearrange("(p c) -> p c", p=P), edge_f[:, 7, :]).then_inc(keys_out, 16)
            sp.wait_ge(keys_out, 16)
            sp.dma_start(keys[:, 0:EDGES], key_d.partition_broadcast(P)).then_inc(keys_in, 16)

            def stacks(b):
                sp.wait_ge(parts_done, b + 1)
                sp.dma_start(part_d[b], qk_part[:, b % 2]).then_inc(parts_out[b], 16)
                sp.wait_ge(parts_out[b], 16)
                if b >= 3:
                    sp.wait_ge(expo_full, (b - 2) * H * 2)
                for dst, side, parts in ((q_stack, 0, Q_PART), (k_stack, 1, K_PART)):
                    for c, part in enumerate(parts):
                        sp.dma_start(dst[c * HD:(c + 1) * HD, b % 3],
                                     part_d[b, :, side, part, :].rearrange("(h e) n -> e h n", e=HD)
                                     ).then_inc(stack_in[b], 16)

            for b in range(3):
                stacks(b)
            sp.wait_ge(cb_rows, 1)
            for k in range(3):
                for j in range(3):
                    sp.dma_start(k_stack[ROW_CB + j:ROW_CB + j + 1, k].rearrange("o h (t n) -> o (h t) n", n=P),
                                 cb_row[j * H * TB:(j + 1) * H * TB, :]).then_inc(cb_in, 16)

            def max_to_stack(b):
                sp.wait_ge(bank_read, BANK_USE["turn_max", b] + 1)
                for j in range(3):
                    sp.dma_start(q_stack[ROW_MAX + j:ROW_MAX + j + 1, b % 3].rearrange("o h (t n) -> o (h t) n", n=P),
                                 nmax_row[j * H * TB:(j + 1) * H * TB, b % 2, :]).then_inc(max_in[b], 16)

            for dst, src in ((win_sb, w_in), (cw_sb, conv_w), (cvb_sb, conv_b), (wx_sb, w_x), (pick_sb, c_pick),
                             (wdt_sb, w_dt), (bdt_sb, b_dt), (a_sb, a_log), (ds_sb, d_skip), (wout_sb, w_out),
                             (gamma_sb, gamma), (beta_sb, beta)):
                sp.dma_start(dst[:], src).then_inc(mamba_in, 16)
            max_to_stack(0)
            stacks(3)
            for b in range(1, B):
                max_to_stack(b)
            for b in range(B):
                sp.wait_ge(dbl_done, b + 1)
                sp.dma_start(b_d[:, b * N:(b + 1) * N], dbl[16:32, b * N:(b + 1) * N]).then_inc(b_out, 16)
            sp.wait_ge(b_out, 16 * B)
            for q in range(NSPAN):
                with sp.Fori(0, DS // 2) as i:
                    for j in range(2):
                        sp.wait_ge(b_used, i * 2 + (q * DS + j + 1))
                        sp.dma_start(b_row[:, j, :],
                                     b_d[bass.ds(i * 2 + j, 1), q * SPAN:(q + 1) * SPAN].partition_broadcast(P)
                                     ).then_inc(row_b_in[j], 16)
            sp.wait_ge(h3_done, B)
            for dst, src in ((gw_sb, gate_w), (same_sb, same_expert), (bits_sb, bit_values), (before_sb, before),
                             (onesb_sb, onesb), (start_sb, run_start), (ai_sb, a_iota), (bi_sb, b_iota),
                             (tile_sb, tile_of), (own_sb, own_expert)):
                sp.dma_start(dst[:], src).then_inc(moe_in, 16)
            for dst, src in ((sw1_sb, sw1), (sw2_sb, sw2), (sb1_sb, sb1), (sb2_sb, sb2), (b1_sb, b1), (b2_sb, b2),
                             (w1_sb, w1), (w2_sb, w2)):
                sp.dma_start(dst[:], src).then_inc(moe_w_in, 16)
            sp.wait_ge(ln_done, 5 * B)
            route_v = route_d.rearrange("(i p) c -> p i c", p=P)
            sp.dma_start(route_v[:, :, 0:D], xn[:]).then_inc(route_out, 16)
            sp.wait_ge(probs_done, 1)
            sp.dma_start(route_v[:, :, D:], prob[:]).then_inc(route_out, 16)
            sp.wait_ge(idx_done, 2)
            sp.dma_start(idx_d.rearrange("(g q b) -> q g b", g=2, b=B1), idx_i[:]).then_inc(idx_out, 16)
            sp.wait_ge(idx_out, 16)
            with nc.allow_non_contiguous_dma(reason="2048 token numbers"):
                sp.dma_start(idx_t[:], idx_d.rearrange("(e s) -> s e", e=E1)).then_inc(idx_in, 16)
            sp.wait_ge(base_done, B)
            sp.dma_start(out.rearrange("(i p) d -> p i d", p=P), h[:]).then_inc(base_out, 16)
            sp.wait_ge(added, 16 * E1)
            sp.wait_ge(base_out, 16)

        @block.gpsimd
        def _(pool):
            pool.memset(minus_half[:], -0.5).then_inc(minus_half_set, 1)
            pool.memset(ones_f[:], 1.0).then_inc(minus_half_set, 1)
            pool.wait_ge(ids_in, 16)
            roots = [0]

            def gather_tokens(b):
                for i in range(b * TB, (b + 1) * TB):
                    pool.indirect_dma_start(h[:, i, :], None, emb,
                                            bass.IndirectOffsetOnAxis(ids_sb[:, i:i + 1], 0)).then_inc(emb_in[b], 16)

            def root():
                k = roots[0]
                b = k % B
                pool.wait_ge(ln_mv, k + 1)
                nc.gpsimd.tensor_scalar(vare[:, b * TB:(b + 1) * TB], mv[:, b * TB:(b + 1) * TB, 1], EPS, None,
                                        ALU.add).then_inc(pool_step, 1)
                pool.wait_ge(pool_step, k + 1)
                if k == 0:
                    pool.wait_ge(minus_half_set, 2)
                nc.gpsimd.tensor_tensor(rstd[:, b * TB:(b + 1) * TB], vare[:, b * TB:(b + 1) * TB],
                                        minus_half[:], ALU.pow).then_inc(ln_rstd, 1)
                roots[0] += 1

            gather_tokens(0)
            gather_tokens(1)
            root()
            gather_tokens(2)
            root()
            gather_tokens(3)
            root()
            root()
            pool.memset(v_aug[:], 1.0).then_inc(ones_in, 1)
            pool.wait_ge(last_done, 1)
            for t in range(TB):
                pool.indirect_dma_start(edge_a[:, t, :], None, attrs,
                                        bass.IndirectOffsetOnAxis(last_i[:, t:t + 1], 0)).then_inc(attr_in, 16)
            for b in range(B):
                root()
            pool.wait_ge(gate_off, 1)
            for b in range(B):
                pool.indirect_dma_start(w_sel[:, 0, b, :], None, we0,
                                        bass.IndirectOffsetOnAxis(off_w[:, b:b + 1], 0)).then_inc(sel_in, 16)
                pool.indirect_dma_start(b_sel[:, 0, b, :], None, be0,
                                        bass.IndirectOffsetOnAxis(off_b[:, b:b + 1], 0)).then_inc(sel_in, 16)
            for b in range(B):
                root()
                if b == 0:
                    pool.memset(xi[:, :, :, 0:DC - 1], 0.0).then_inc(pads_set, 1)
                    pool.memset(decay[:].rearrange("p j (b n) -> p j b n", n=N)[:, :, :, 0:1], 0.0
                                ).then_inc(edge_zero, 1)
            pool.sem_inc(b_used, 2)
            pool.wait_ge(dtx_done, NH)
            for q in range(NSPAN):
                with pool.Fori(0, DS // 2) as i:
                    for j in range(2):
                        pool.wait_ge(row_b_in[j], i * 16 + (q * DS // 2 + 1) * 16)
                        for half in range(NH):
                            n = 2 * j + half
                            pool.wait_ge(scanned, i * 4 + (q * 2 * DS + n + 1))
                            ins = nc.gpsimd.tensor_tensor(drive[:, n, :], dtx[:, half, q * SPAN:(q + 1) * SPAN],
                                                          b_row[:, j, :], ALU.mult).then_inc(drive_full, 1)
                        pool.wait_ge(drive_full, i * 4 + (q * 2 * DS + 2 * j + 2))
                        pool.sem_inc(b_used, 1)
            for b in range(2 * B):
                root()
            pool.wait_ge(idx_in, 16)
            pool.wait_ge(route_out, 32)

            def gather_rows(e):
                if e >= AHEAD:
                    pool.wait_ge(rows_turned, e - AHEAD + 1)
                pool.indirect_dma_start(rows[:, e, :], None, route_d,
                                        bass.IndirectOffsetOnAxis(idx_t[:, e:e + 1], 0)).then_inc(rows_in[e % AHEAD], 16)

            def add_rows(e):
                pool.wait_ge(routed_done, e + 1)
                if e:
                    pool.wait_ge(added, 16 * e)
                else:
                    pool.wait_ge(base_out, 16)
                pool.indirect_dma_start(out, bass.IndirectOffsetOnAxis(idx_t[:, e:e + 1], 0), routed[:, e, :], None,
                                        compute_op=ALU.add).then_inc(added, 16)

            for e in range(E1 + AHEAD):
                if e < E1:
                    gather_rows(e)
                if e >= AHEAD:
                    add_rows(e - AHEAD)

        @block.scalar
        def _(act):
            steps = [0]

            def link(ins):
                steps[0] += 1
                ins.then_inc(act_step, 1)
                act.wait_ge(act_step, steps[0])

            act.wait_ge(proj_in, 128)
            link(nc.scalar.mul(qb4[:], qb_sb[:], 1.0 / HD ** 0.5))

            for b in range(B):
                act.wait_ge(turned, b + 1)
                nc.scalar.copy(xT[:, b * N:(b + 1) * N], ps[:, 6 + b % 2, :]).then_inc(xT_done, 1)
                act.wait_ge(qkv_full, b + 1)
                if b >= 2:
                    act.wait_ge(parts_done, b - 1)
                nc.scalar.activation(qk[:, b % 2, 0, :], ps[:, 3 * (b % 2), :], ACT.Identity, bias=qb4[:],
                                     scale=1.0 / HD ** 0.5)
                link(nc.scalar.activation(qk[:, b % 2, 1, :], ps[:, 3 * (b % 2) + 1, :], ACT.Identity,
                                          bias=kb_sb[:]))
                if b >= 2:
                    act.wait_ge(parts_out[b - 2], 16)
                nc.scalar.copy(qk_part[:, b % 2, :, 0, :], qk[:, b % 2]).then_inc(part_cast, 1)
                act.wait_ge(part_rest, b + 1)
                nc.scalar.copy(qk_part[:, b % 2, :, 1, :], qk_rest[:]).then_inc(part_cast, 1)
            act.wait_ge(cb_turned, 1)
            nc.scalar.copy(cb_row[:], ps[0:3 * H * TB, 7, 0:P // 2].bitcast(BF16)).then_inc(cb_rows, 1)
            for now in SLOTS:
                for piece in now:
                    kind, k = piece
                    if kind in ("turn_max", "turn_back", "norm"):
                        act.wait_ge(bank_full, BANK_USE[piece] + 1)
                    if kind == "turn_max":
                        if k >= 2:
                            act.wait_ge(max_in[k - 2], 48)
                        nc.scalar.copy(nmax_row[:, k % 2, :],
                                       ps[0:3 * H * TB, 7, 0:P // 2].bitcast(BF16)).then_inc(bank_read, 1)
                    if kind == "probs":
                        g, hh = k // G, k % G
                        if hh == 0 and g >= 2:
                            act.wait_ge(pv_full, g - 1)
                        for m in range(2):
                            act.wait_ge(expo_full, 2 * k + m + 1)
                            nc.scalar.activation(probs[:, g % 2, hh, 2 * m:2 * m + 2, :],
                                                 ps[:, 2 + 2 * m:4 + 2 * m, :], ACT.Exp).then_inc(expo_read, 1)
                    if kind == "pv":
                        act.wait_ge(pv_full, k + 1)
                        nc.scalar.copy(oT[:, k % 2, :], ps[:, 6, :]).then_inc(pv_read, 1)
                    if kind == "turn_back":
                        nc.scalar.copy(onT[:], ps[:, 7, :]).then_inc(bank_read, 1)
                    if kind == "norm":
                        nc.scalar.activation(xT[:, k * N:(k + 1) * N], ps[:, 7, :], ACT.Copy,
                                             accum_out=pooled[:, k:k + 1]).then_inc(bank_read, 1)
            act.wait_ge(gate_full, 2)
            nc.scalar.activation(small[:, 32:48], small[:, 16:32], ACT.Exp, bias=small[:, 80:81],
                                 accum_out=small[:, 81:82]).then_inc(gate_exp, 1)
            for b in range(B):
                act.wait_ge(turned3, b + 1)
                nc.scalar.copy(xT[:, b * N:(b + 1) * N], ps[:, b, :]).then_inc(xT3_done, 1)
            for b in range(B):
                act.wait_ge(xz_full, b + 1)
                k0 = 4 * ((b + 1) % 2)
                for half in range(NH):
                    ins = nc.scalar.copy(xi[:, half, b, DC - 1:], ps[:, k0 + half, :])
                ins.then_inc(xi_done, 1)
                for half in range(NH):
                    ins = nc.scalar.activation(sz[:, half, b * N:(b + 1) * N], ps[:, k0 + NH + half, :], ACT.Silu)
                ins.then_inc(z_done, 1)
            for b in range(B):
                for half in range(NH):
                    act.wait_ge(conv_done, NH * b + half + 1)
                    nc.scalar.activation(xc[:, half, b * N:(b + 1) * N], conv[:, (half * 2 + 1), :], ACT.Silu,
                                         bias=cvb_sb[:, half:half + 1]).then_inc(xc_done, 1)
                act.wait_ge(dbl_full, b + 1)
                nc.scalar.copy(dbl[:, b * N:(b + 1) * N], ps[0:32, b, :]).then_inc(dbl_done, 1)
                nc.scalar.copy(c_stack[:, b * N:(b + 1) * N], ps[:, b, :]).then_inc(c_cast, 1)
            for b in range(B):
                for half in range(NH):
                    k = NH * b + half
                    act.wait_ge(dt_full, k + 1)
                    nc.scalar.activation(dt[:, half, b * N:(b + 1) * N], ps[:, 4 + k % 4, :], ACT.Abs,
                                         bias=bdt_sb[:, half:half + 1]).then_inc(dt_abs, 1)
            act.wait_ge(dt_abs, NH * B)
            for half in range(NH):
                link(nc.scalar.activation(dt[:, half, :], dt[:, half, :], ACT.Exp, scale=-1.0))
            act.wait_ge(mamba_in, 16 * 12)
            link(nc.scalar.activation(a_neg[:], a_sb[:], ACT.Exp))
            link(nc.scalar.mul(a_neg[:], a_neg[:], -1.0))
            for half in range(NH):
                nc.scalar.activation(dt[:, half, :], dt[:, half, :], ACT.Ln, bias=1.0).then_inc(dt_log, 1)
            act.wait_ge(dt_done, NH)
            act.wait_ge(edge_zero, 1)
            for q in range(NSPAN):
                with act.Fori(0, DS // 2) as i:
                    for n in range(4):
                        j, half = n // 2, n % 2
                        act.wait_ge(scanned, i * 4 + (q * 2 * DS + n + 1))
                        nc.scalar.activation(
                            decay[:, n, :].rearrange("p (b n) -> p b n", n=N)[:, :, 1:],
                            dt[:, half, q * SPAN:(q + 1) * SPAN].rearrange("p (b n) -> p b n", n=N)[:, :, 1:],
                            ACT.Exp, scale=a_neg[:, half, bass.ds(i * 2 + j, 1)]).then_inc(decay_full, 1)
            for b in range(B):
                act.wait_ge(turned4, b + 1)
                nc.scalar.copy(xT[:, b * N:(b + 1) * N], ps[:, b, :]).then_inc(xT4_done, 1)
            act.wait_ge(shifted, 1)
            nc.scalar.activation(prob[:], logit[:], ACT.Exp).then_inc(exped, 1)
            act.wait_ge(moe_w_in, 16 * 8)
            for b in range(B):
                for c in range(HC):
                    act.wait_ge(shid_full, HC * b + c + 1)
                    if b >= 2 and c == 0:
                        act.wait_ge(sy_full, b - 1)
                    nc.scalar.activation(shid[:, b % 2, c, :], ps[:, 1 + (HC * b + c) % 3, :], ACT.Gelu_apprx_tanh,
                                         bias=sb1_sb[:, c:c + 1]).then_inc(shid_done, 1)
            for e in range(E1):
                act.wait_ge(rows_turned, e + 1)
                nc.scalar.copy(rowsT[:, e % 2, :], ps[:, 4 * (e % 2), 0:P]).then_inc(rowsT_done, 1)
                act.wait_ge(pre_done, e + 1)
                if e >= 2:
                    act.wait_ge(ey_full, e - 1)
                nc.scalar.activation(hid[:, e % 2], pre[:, e % 2], ACT.Gelu_apprx_tanh).then_inc(eh_done, 1)

        @block.vector
        def _(dve):
            steps = [0]
            norms = [0]

            def link(ins):
                steps[0] += 1
                ins.then_inc(dve_step, 1)
                dve.wait_ge(dve_step, steps[0])

            def norm_stats(b, src):
                for i in range(b * TB, (b + 1) * TB):
                    ins = nc.vector.bn_stats(stats[:, i, :], src[:, i, :])
                link(ins)
                for i in range(b * TB, (b + 1) * TB):
                    ins = nc.vector.bn_aggr(mv[:, i, :], stats[:, i, :])
                ins.then_inc(ln_mv, 1)

            def normalise(b, src):
                norms[0] += 1
                dve.wait_ge(ln_rstd, norms[0])
                for i in range(b * TB, (b + 1) * TB):
                    ins = nc.vector.tensor_scalar(xn[:, i, :], src[:, i, :], mv[:, i, 0:1], rstd[:, i:i + 1],
                                                  ALU.subtract, ALU.mult)
                ins.then_inc(ln_done, 1)

            dve.wait_ge(edges_in, 16)
            src, tgt = edge_f[:, 0, :], edge_f[:, 1, :]
            link(nc.vector.tensor_copy(edge_f[:, 0:2, :], edge_sb[:]))
            link(nc.vector.tensor_scalar(edge_f[:, 2, :], src, 0.0, None, ALU.is_ge))
            link(nc.vector.scalar_tensor_tensor(edge_f[:, 3, :], src, float(N), edge_f[:, 2, :], ALU.is_lt, ALU.mult))
            link(nc.vector.scalar_tensor_tensor(edge_f[:, 4, :], tgt, 0.0, edge_f[:, 3, :], ALU.is_ge, ALU.mult))
            link(nc.vector.scalar_tensor_tensor(edge_f[:, 5, :], tgt, float(N), edge_f[:, 4, :], ALU.is_lt, ALU.mult))
            link(nc.vector.scalar_tensor_tensor(edge_f[:, 6, :], tgt, -FAR, edge_f[:, 5, :], ALU.add, ALU.mult))
            nc.vector.tensor_scalar(edge_f[:, 7, :], edge_f[:, 6, :], FAR, None, ALU.add).then_inc(key_done, 1)

            dve.wait_ge(pos_in, 16)
            for b in range(B + 1):
                if b < B:
                    dve.wait_ge(emb_in[b], 16 * TB)
                    link(nc.vector.tensor_tensor(h[:, b * TB:(b + 1) * TB, :], h[:, b * TB:(b + 1) * TB, :],
                                                 pos_sb[:], ALU.add))
                    norm_stats(b, h)
                if b:
                    normalise(b - 1, h)

            dve.wait_ge(keys_in, 16)
            dve.wait_ge(ebw_in, 48)
            link(nc.vector.max_index(last[:], want_sb[:], keys))
            link(nc.vector.tensor_copy(last_f[:], last[:, 0:TB]))
            nc.vector.tensor_scalar(hit[:], last_f[:], float(EDGES), None, ALU.is_lt)
            nc.vector.tensor_scalar(last_i[:], last_f[:], float(EDGES - 1), None, ALU.min).then_inc(last_done, 1)

            dve.wait_ge(proj_in, 128)
            dve.wait_ge(ones_in, 1)
            for b in range(B):
                dve.wait_ge(part_cast, 2 * b + 1)
                nc.vector.tensor_tensor(qk_rest[:], qk[:, b % 2], qk_part[:, b % 2, :, 0, :],
                                        ALU.subtract).then_inc(part_rest, 1)
                dve.wait_ge(qkv_full, b + 1)
                vp = ps[:, 3 * (b % 2) + 2, :].rearrange("p (t h e) -> p t h e", t=TB, h=H)
                nc.vector.tensor_tensor(v_aug[:, b * TB:(b + 1) * TB, :, 0:HD], vp,
                                        vb_sb[:].rearrange("p (o h e) -> p o h e", o=1, h=H)
                                        .to_broadcast([P, TB, H, HD]), ALU.add).then_inc(v_read, 1)
                dve.wait_ge(part_cast, 2 * b + 2)
                nc.vector.tensor_tensor(qk_part[:, b % 2, :, 2, :], qk_rest[:], qk_part[:, b % 2, :, 1, :],
                                        ALU.subtract).then_inc(parts_done, 1)
                dve.wait_ge(parts_done, b + 1)

            dve.wait_ge(attr_in, 16 * TB)
            for t in range(TB):
                ins = nc.vector.tensor_copy(cb[:, 0, t, :], ebw_sb[:, 3, :])
            link(ins)
            for f in range(3):
                for t in range(TB):
                    ins = nc.vector.scalar_tensor_tensor(cb[:, (f + 1) % 2, t, :], ebw_sb[:, f, :],
                                                         edge_a[:, t, f:f + 1], cb[:, f % 2, t, :], ALU.mult, ALU.add)
                link(ins)
            for t in range(TB):
                ins = nc.vector.tensor_scalar(cb[:, 0, t, :], cb[:, 1, t, :], hit[:, t:t + 1], None, ALU.mult)
            link(ins)
            cbv = cb[:, 0].rearrange("p t h -> p h t")
            link(nc.vector.tensor_copy(cb_part[:, 0], cbv))
            link(nc.vector.tensor_tensor(cb_rest[:], cbv, cb_part[:, 0], ALU.subtract))
            link(nc.vector.tensor_copy(cb_part[:, 1], cb_rest[:]))
            nc.vector.tensor_tensor(cb_part[:, 2], cb_rest[:], cb_part[:, 1], ALU.subtract).then_inc(cb_parts, 1)

            for now in SLOTS:
                for piece in now:
                    kind, k = piece
                    if kind == "scores":
                        b, hh = k // H, k % H
                        for t in range(TB):
                            n = TB * k + t
                            dve.wait_ge(scores_full, n + 1)
                            nc.vector.tensor_reduce(nmax[:, b % 2, hh * TB + t:hh * TB + t + 1], ps[:, n % 2, :],
                                                    AX.X, ALU.max, negate=True).then_inc(scores_read, 1)
                        if hh == H - 1:
                            dve.wait_ge(scores_read, TB * (k + 1))
                            m = nmax[:, b % 2]
                            link(nc.vector.tensor_copy(nmax_part[:, b % 2, 0], m))
                            link(nc.vector.tensor_tensor(nmax_rest[:], m, nmax_part[:, b % 2, 0], ALU.subtract))
                            link(nc.vector.tensor_copy(nmax_part[:, b % 2, 1], nmax_rest[:]))
                            nc.vector.tensor_tensor(nmax_part[:, b % 2, 2], nmax_rest[:], nmax_part[:, b % 2, 1],
                                                    ALU.subtract).then_inc(max_parts, 1)
                            dve.wait_ge(max_parts, b + 1)
                    if kind in ("turn_out", "project"):
                        dve.wait_ge(bank_full, BANK_USE[piece] + 1)
                    if kind == "turn_out":
                        g = k % NG
                        o = ps[:, 7, :].rearrange("p (t g e) -> p t g e", t=TB, g=G)
                        link(nc.vector.reciprocal(r_den[:], o[:, :, :, HD]))
                        nc.vector.tensor_tensor(
                            o_nat[:, :, g * G:(g + 1) * G, :], o[:, :, :, 0:HD],
                            r_den[:].rearrange("p t (g o) -> p t g o", o=1).to_broadcast([P, TB, G, HD]),
                            ALU.mult).then_inc(bank_read, 1)
                    if kind == "project":
                        hb = h[:, k * TB:(k + 1) * TB, :]
                        nc.vector.tensor_tensor(hb, hb, ps[:, 7, :].rearrange("p (t d) -> p t d", t=TB),
                                                ALU.add).then_inc(bank_read, 1)
                        dve.wait_ge(bank_read, BANK_USE[piece] + 1)
                        norm_stats(k, h)
                    if kind == "norm":
                        normalise(k, h)

            lg, ex, pr, top = small[:, 16:32], small[:, 32:48], small[:, 48:64], small[:, 64:72]
            dve.wait_ge(gate_full, 1)
            link(nc.vector.scalar_tensor_tensor(lg, ps[0:B, 0, 0:EXPERTS0], 1.0 / N, bg_sb[:], ALU.mult, ALU.add))
            nc.vector.tensor_reduce(small[:, 80:81], lg, AX.X, ALU.max, negate=True).then_inc(gate_full, 1)
            dve.wait_ge(gate_exp, 1)
            link(nc.vector.reciprocal(small[:, 82:83], small[:, 81:82]))
            link(nc.vector.tensor_scalar(pr, ex, small[:, 82:83], None, ALU.mult))
            link(nc.vector.max(top, pr))
            link(nc.vector.max_index(top_i[:], top, pr))
            link(nc.vector.tensor_copy(small[:, 83:84], top_i[:, 0:1]))
            nc.vector.tensor_scalar(small[:, 0:B], id_f[0:B, 0:B], small[:, 83:84], None, ALU.mult)
            nc.vector.tensor_scalar(small[:, B:2 * B], id_f[0:B, 0:B], top[:, 0:1], None,
                                    ALU.mult).then_inc(gate_diag, 1)
            dve.wait_ge(gate_rows, 1)
            dve.wait_ge(lane_in, 16)
            link(nc.vector.tensor_copy(pick_b[:], ps[:, 0, 32:32 + 2 * B]))
            nc.vector.tensor_scalar(off_w[:], pick_b[:, 0:B], float(D), lane_sb[:], ALU.mult, ALU.add)
            nc.vector.tensor_copy(off_b[:], pick_b[:, 0:B]).then_inc(gate_off, 1)
            dve.wait_ge(sel_in, 16 * 2 * B)
            for b in range(B):
                nc.vector.tensor_scalar(w_sel[:, 1, b, :], w_sel[:, 0, b, :], pick_b[:, B + b:B + b + 1], None,
                                        ALU.mult).then_inc(sel_done, 1)
            for b in range(B):
                ins = nc.vector.tensor_scalar(b_sel[:, 1, b, :], b_sel[:, 0, b, :], pick_b[:, B + b:B + b + 1], None,
                                              ALU.mult)
            link(ins)
            for b in range(B + 1):
                if b < B:
                    hb = h[:, b * TB:(b + 1) * TB, :]
                    link(nc.vector.tensor_tensor(hb, hb, b_sel[:, 1, b:b + 1, :].to_broadcast([P, TB, D]), ALU.add))
                    dve.wait_ge(y0_full, b + 1)
                    link(nc.vector.tensor_tensor(hb, hb, ps[:, b, :].rearrange("p (t d) -> p t d", t=TB), ALU.add))
                    norm_stats(b, h)
                if b:
                    normalise(b - 1, h)

            dve.wait_ge(mamba_in, 16 * 12)
            dve.wait_ge(pads_set, 1)
            for half in range(NH):
                ins = nc.vector.tensor_scalar(d_diag[:, half, :], id_f[:], ds_sb[:, half:half + 1], None, ALU.mult)
            ins.then_inc(diag_done, 1)
            for b in range(B):
                dve.wait_ge(xi_done, b + 1)
                for half in range(NH):
                    if b:
                        dve.wait_ge(xc_done, NH * (b - 1) + half + 1)
                    c0, c1 = conv[:, half * 2, :], conv[:, half * 2 + 1, :]
                    link(nc.vector.tensor_scalar(c0, xi[:, half, b, 0:N], cw_sb[:, half, 0:1], None, ALU.mult))
                    link(nc.vector.scalar_tensor_tensor(c1, xi[:, half, b, 1:1 + N], cw_sb[:, half, 1:2], c0,
                                                        ALU.mult, ALU.add))
                    link(nc.vector.scalar_tensor_tensor(c0, xi[:, half, b, 2:2 + N], cw_sb[:, half, 2:3], c1,
                                                        ALU.mult, ALU.add))
                    nc.vector.scalar_tensor_tensor(c1, xi[:, half, b, 3:3 + N], cw_sb[:, half, 3:4], c0,
                                                   ALU.mult, ALU.add).then_inc(conv_done, 1)
            for b in range(B):
                cols = slice(b * N, (b + 1) * N)
                dve.wait_ge(c_cast, b + 1)
                rest, mid = c_rest[:, b % 2, :], c_mid[:, b % 2, :]
                link(nc.vector.tensor_tensor(rest, ps[:, b, :], c_stack[:, cols], ALU.subtract))
                link(nc.vector.tensor_copy(mid, rest))
                nc.vector.tensor_copy(c_stack[64:96, cols], mid[64:96])
                nc.vector.tensor_tensor(c_stack[96:128, cols], rest[96:128], mid[96:128],
                                        ALU.subtract).then_inc(c_done, 1)
            for b in range(B):
                for half in range(NH):
                    k = NH * b + half
                    dve.wait_ge(dt_abs, k + 1)
                    nc.vector.tensor_scalar(dtx[:, half, b * N:(b + 1) * N], ps[:, 4 + k % 4, :],
                                            bdt_sb[:, half:half + 1], 0.0, ALU.add, ALU.max).then_inc(dt_relu, 1)
            dve.wait_ge(dt_relu, NH * B)
            for half in range(NH):
                dve.wait_ge(dt_log, half + 1)
                nc.vector.tensor_tensor(dt[:, half, :], dt[:, half, :], dtx[:, half, :], ALU.add).then_inc(dt_done, 1)
            dve.wait_ge(xc_done, NH * B)
            for half in range(NH):
                dve.wait_ge(dt_done, half + 1)
                nc.vector.tensor_tensor(dtx[:, half, :], dt[:, half, :], xc[:, half, :], ALU.mult).then_inc(dtx_done, 1)
            dve.sem_inc(scanned, 4)
            dve.sem_inc(c_used, 2)
            for q in range(NSPAN):
                with dve.Fori(0, DS // 2) as i:
                    for n in range(4):
                        j, half = n // 2, n % 2
                        unit = q * 2 * DS + n
                        dve.wait_ge(decay_full, i * 4 + (unit + 1))
                        dve.wait_ge(drive_full, i * 4 + (unit + 1))
                        nc.vector.tensor_tensor_scan(state[:, half, :], decay[:, n, :], drive[:, n, :], 0.0,
                                                     ALU.mult, ALU.add).then_inc(scanned, 1)
                        dve.wait_ge(scanned, i * 4 + (unit + 5))
                        if half == 0:
                            dve.wait_ge(c_full, i * 2 + (q * DS + j + 1))
                        dve.wait_ge(y_added, i * 4 + (unit + 1))
                        ins = nc.vector.tensor_tensor(read_out[:, half, :].rearrange("p (b n) -> p b n", n=N),
                                                      state[:, half, :].rearrange("p (b n) -> p b n", n=N),
                                                      ps[:, 4 + 2 * j:6 + 2 * j, :], ALU.mult)
                        ins.then_inc(read_full, 1)
                        if half == 1:
                            dve.wait_ge(read_full, i * 4 + (unit + 1))
                            dve.sem_inc(c_used, 1)
                dve.wait_ge(y_full, q + 1)
                for half in range(NH):
                    s_ = sz[:, half, q * SPAN:(q + 1) * SPAN].rearrange("p (b n) -> p b n", n=N)
                    ins = nc.vector.tensor_tensor(s_, ps[:, 2 * half:2 * half + 2, :], s_, ALU.mult)
                ins.then_inc(y_done, 1)
            for b in range(B + 1):
                if b < B:
                    xb = xn[:, b * TB:(b + 1) * TB, :]
                    dve.wait_ge(out1_full, b + 1)
                    link(nc.vector.tensor_tensor(xb, xb, ps[:, 4 + b, :].rearrange("p (t d) -> p t d", t=TB), ALU.add))
                    norm_stats(b, xn)
                if b:
                    k = b - 1
                    normalise(k, xn)
                    dve.wait_ge(ln_done, 3 * B + b)
                    xb, hb = xn[:, k * TB:b * TB, :], h[:, k * TB:b * TB, :]
                    link(nc.vector.tensor_tensor(
                        xb, xb, gamma_sb[:].rearrange("p (o d) -> p o d", o=1).to_broadcast([P, TB, D]), ALU.mult))
                    link(nc.vector.tensor_tensor(
                        hb, hb, beta_sb[:].rearrange("p (o d) -> p o d", o=1).to_broadcast([P, TB, D]), ALU.add))
                    nc.vector.tensor_tensor(hb, hb, xb, ALU.add).then_inc(h3_done, 1)
            for b in range(B + 1):
                if b < B:
                    dve.wait_ge(h3_done, b + 1)
                    norm_stats(b, h)
                if b:
                    normalise(b - 1, h)
            dve.wait_ge(logits_full, 1)
            lgp = ps[:, 4, 0:NT * E1].rearrange("p (i e) -> p i e", e=E1)

            def over_e(a):
                return a.rearrange("p (i o) -> p i o", o=1).to_broadcast([P, NT, E1])

            link(nc.vector.tensor_reduce(rowmax[:, 0, :], lgp, AX.X, ALU.max))
            nc.vector.tensor_tensor(logit[:], lgp, over_e(rowmax[:, 0, :]), ALU.subtract).then_inc(shifted, 1)
            dve.wait_ge(exped, 1)
            link(nc.vector.tensor_reduce(rowmax[:, 1, :], prob[:], AX.X, ALU.add))
            link(nc.vector.reciprocal(rowmax[:, 2, :], rowmax[:, 1, :]))
            nc.vector.tensor_tensor(prob[:], prob[:], over_e(rowmax[:, 2, :]), ALU.mult).then_inc(probs_done, 1)
            dve.wait_ge(probs_turned, 1)
            nc.vector.tensor_copy(prob_x[:], ps[:, 5, 0:2 * P]).then_inc(prob_x_done, 1)
            dve.wait_ge(prob_x_done, 1)
            dve.wait_ge(moe_in, 16 * 10)
            nc.vector.memset(thr[:], 0).then_inc(bit_step, 1)
            with dve.Fori(0, BITS) as i:
                dve.wait_ge(bit_step, i * 3 + 1)
                nc.vector.tensor_tensor(cand[:], thr[:], bits_sb[:, bass.ds(i, 1)], ALU.bitwise_or).then_inc(bit_step, 1)
                dve.wait_ge(bit_step, i * 3 + 2)
                nc.vector.tensor_scalar(hits_x[:], prob_x[:], cand[:].bitcast(F32), None, ALU.is_ge, ALU.add,
                                        accum_out=count[:]).then_inc(counted, 1)
                dve.wait_ge(summed, i + 1)
                nc.vector.scalar_tensor_tensor(enough[:], ps[:, 6, 0:1], float(CAP) - 0.5, bits_sb[:, bass.ds(i, 1)],
                                               ALU.is_gt, ALU.mult).then_inc(bit_step, 1)
                dve.wait_ge(bit_step, i * 3 + 3)
                nc.vector.tensor_tensor(thr[:], thr[:], enough[:], ALU.bitwise_or).then_inc(bit_step, 1)
            dve.wait_ge(bit_step, 3 * BITS + 1)
            nc.vector.tensor_scalar(thr_b[:], ones_f[:], thr[:].bitcast(F32), None, ALU.mult).then_inc(thr_ready, 1)
            dve.wait_ge(thr_turned, 1)
            link(nc.vector.tensor_copy(thr_n[:], ps[:, 6, P:P + E1]))
            pe_t = prob[:].rearrange("p i e -> p e i")

            def over_i(a):
                return a.rearrange("p (e o) -> p e o", o=1).to_broadcast([P, E1, NT])

            def flat(a):
                return a.rearrange("p e i -> p (e i)")

            link(nc.vector.tensor_tensor(over[:], pe_t, over_i(thr_n[:]), ALU.is_gt))
            link(nc.vector.tensor_tensor(even[:], pe_t, over_i(thr_n[:]), ALU.is_equal))

            def runs(mask, k):
                link(nc.vector.tensor_tensor_scan(flat(run[:, k]), start_sb[:], flat(mask), 0.0, ALU.mult, ALU.add))

            link(nc.vector.tensor_copy(picked[:, 2], over[:]))
            runs(over[:], 0)
            runs(even[:], 1)
            link(nc.vector.tensor_copy(run_b[:, 0], run[:, 0]))
            nc.vector.tensor_tensor(run_b[:, 1], run[:, 1], even[:], ALU.subtract).then_inc(runs_done, 1)
            dve.wait_ge(ranks_full, 1)
            link(nc.vector.tensor_scalar(need[:], ps[:, 7, 256:256 + E1], -1.0, float(CAP), ALU.mult, ALU.add))
            link(nc.vector.tensor_tensor(picked[:, 0], ps[:, 7, 0:256].rearrange("p (e i) -> p e i", e=E1),
                                         over_i(need[:]), ALU.is_lt))
            link(nc.vector.tensor_tensor(picked[:, 1], picked[:, 0], even[:], ALU.mult))
            link(nc.vector.tensor_tensor(picked[:, 0], picked[:, 1], picked[:, 2], ALU.add))
            link(nc.vector.tensor_copy(picked_b[:], picked[:, 0]))
            runs(picked_b[:], 0)
            nc.vector.tensor_tensor(run_b[:, 0], run[:, 0], picked_b[:], ALU.subtract).then_inc(runs_done, 1)
            dve.wait_ge(ranks_full, 2)
            link(nc.vector.tensor_copy(slot_i[:, 0], ps[:, 6, 256:512].rearrange("p (e i) -> p e i", e=E1)))
            nc.vector.tensor_single_scalar(slot_i[:, 1], slot_i[:, 0], 3, ALU.arith_shift_right)
            link(nc.vector.tensor_single_scalar(slot_i[:, 2], slot_i[:, 0], B1 - 1, ALU.bitwise_and))
            nc.vector.scalar_tensor_tensor(slot_b[:, 0], slot_i[:, 1], 1.0, picked[:, 0], ALU.add, ALU.mult)
            link(nc.vector.tensor_copy(slot_b[:, 1], slot_i[:, 2]))
            link(nc.vector.tensor_tensor(
                hot_b[:], bi_sb[:].rearrange("p (o b) -> p o b", o=1).to_broadcast([P, E1 * NT, B1]),
                slot_b[:, 1].rearrange("p e (i o) -> p (e i) o", o=1).to_broadcast([P, E1 * NT, B1]), ALU.is_equal))
            vb_ = val_b[:].rearrange("p e i k b -> p (e i) k b")
            nc.vector.tensor_scalar(vb_[:, :, 0, :], hot_b[:], lane_sb[:], None, ALU.mult)
            nc.vector.tensor_tensor(vb_[:, :, 1, :], hot_b[:], tile_sb[:], ALU.mult)
            nc.vector.tensor_tensor(
                hot_a[:].rearrange("p i e a -> p e i a"),
                ai_sb[:].rearrange("p (o u a) -> p o u a", o=1, u=1).to_broadcast([P, E1, NT, A1]),
                slot_b[:, 0].rearrange("p e (i o) -> p e i o", o=1).to_broadcast([P, E1, NT, A1]),
                ALU.is_equal).then_inc(hot_done, 1)
            for g in range(2):
                dve.wait_ge(idx_full, g + 1)
                link(nc.vector.tensor_tensor(
                    diag[:], ps[:, 5 + 2 * g, 0:P].rearrange("p (e k) -> p e k", e=B1),
                    own_sb[:].rearrange("p (e o) -> p e o", o=1).to_broadcast([P, B1, 2 * B1]), ALU.mult))
                link(nc.vector.tensor_reduce(idx_v[:, g, :], diag[:].rearrange("p e k -> p k e"), AX.X, ALU.add))
                nc.vector.scalar_tensor_tensor(idx_i[:, g, :], idx_v[:, g, B1:], float(P), idx_v[:, g, 0:B1],
                                               ALU.mult, ALU.add).then_inc(idx_done, 1)
            for b in range(B):
                dve.wait_ge(sy_full, b + 1)
                hb = h[:, b * TB:(b + 1) * TB, :]
                nc.vector.tensor_tensor(hb, hb, ps[:, 4 + b, :].rearrange("p (t d) -> p t d", t=TB),
                                        ALU.add).then_inc(base_done, 1)
            for e in range(E1):
                dve.wait_ge(eh_full, e + 1)
                if e >= 2:
                    dve.wait_ge(eh_done, e - 1)
                nc.vector.tensor_tensor(pre[:, e % 2], ps[:, 1 + e % 2, :].rearrange("p (c n) -> p c n", c=HC),
                                        b1_sb[:, e, :].rearrange("p (c o) -> p c o", o=1).to_broadcast([P, HC, P]),
                                        ALU.add).then_inc(pre_done, 1)
                dve.wait_ge(ey_full, e + 1)
                nc.vector.tensor_scalar(routed[:, e, :], ps[:, 3 + 2 * (e % 2), 0:P],
                                        rows[:, e, D + e:D + e + 1], None, ALU.mult).then_inc(routed_done, 1)

        @block.tensor
        def _(pe):
            mm, tr = nc.tensor.matmul, nc.tensor.transpose
            pe.wait_ge(const_in, 32)
            for b in range(B):
                pe.wait_ge(ln_done, b + 1)
                if b >= 2:
                    pe.wait_ge(xT_done, b - 1)
                for i in range(TB):
                    ins = tr(ps[:, 6 + b % 2, tile_cols(i)], xn[:, b * TB + i, :], id_f[:])
                ins.then_inc(turned, 1)
                if b == 0:
                    pe.wait_ge(proj_in, 128)
                if b >= 2:
                    pe.wait_ge(part_cast, 2 * (b - 2) + 1)
                    pe.wait_ge(v_read, b - 1)
                pe.wait_ge(xT_done, b + 1)
                cols = slice(b * N, (b + 1) * N)
                mm(ps[:, 3 * (b % 2), :], wq_sb[:], xT[:, cols], start=True, stop=True)
                mm(ps[:, 3 * (b % 2) + 1, :], wk_sb[:], xT[:, cols], start=True, stop=True)
                for i in range(TB):
                    ins = mm(ps[:, 3 * (b % 2) + 2, tile_cols(i)], xT[:, b * N + i * P:b * N + (i + 1) * P], wv_sb[:],
                             start=True, stop=True)
                ins.then_inc(qkv_full, 1)
            pe.wait_ge(cb_parts, 1)
            pe.wait_ge(xT_done, B)
            tr(ps[0:3 * H * TB, 7, 0:P // 2].bitcast(BF16), cb_part[:].rearrange("p j h t -> p (j h t)"),
               id_b[:]).then_inc(cb_turned, 1)
            pe.wait_ge(cb_in, 16 * 9)
            pe.wait_ge(row_in, 32)
            pe.wait_ge(minus_half_set, 2)
            pe.wait_ge(cb_rows, 1)
            pe.wait_ge(part_cast, 2 * B)
            pe.wait_ge(v_read, B)
            for now in SLOTS:
                for piece in now:
                    kind, k = piece
                    if kind in BANK_USES:
                        use = BANK_USE[piece]
                        if use:
                            pe.wait_ge(bank_read, use)
                    if kind == "scores":
                        b, hh = k // H, k % H
                        if hh == 0:
                            pe.wait_ge(stack_in[b], 16 * 2 * NTERM)
                        for t in range(TB):
                            n = TB * k + t
                            if n >= 2:
                                pe.wait_ge(scores_read, n - 1)
                            mm(ps[:, n % 2, :], q_stack[0:ROWS_A, b % 3, hh, tile_cols(t)],
                               k_stack[0:ROWS_A, b % 3, hh, :], start=True, stop=True).then_inc(scores_full, 1)
                    if kind == "turn_max":
                        pe.wait_ge(max_parts, k + 1)
                        tr(ps[0:3 * H * TB, 7, 0:P // 2].bitcast(BF16),
                           nmax_part[:, k % 2].rearrange("p j m -> p (j m)"), id_b[:]).then_inc(bank_full, 1)
                    if kind == "probs":
                        b, hh = k // H, k % H
                        if hh == 0:
                            pe.wait_ge(max_in[b], 48)
                        for m in range(2):
                            n = 2 * k + m
                            if n >= 2:
                                pe.wait_ge(expo_read, n - 1)
                            for t in range(2 * m, 2 * m + 2):
                                ins = mm(ps[:, 2 + t, :], k_stack[0:ROWS_B, b % 3, hh, tile_cols(t)],
                                         q_stack[0:ROWS_B, b % 3, hh, :], start=True, stop=True)
                            ins.then_inc(expo_full, 1)
                    if kind == "pv":
                        b, g = k // NG, k % NG
                        pe.wait_ge(expo_read, 2 * G * (k + 1))
                        if k:
                            pe.wait_ge(pv_read, k)
                        for t in range(TB):
                            for j in range(G):
                                ins = mm(ps[32 * j:32 * j + 32, 6, :], v_aug[:, b * TB + t, g * G + j, :],
                                         probs[:, k % 2, j, t, :], start=(t == 0), stop=(t == TB - 1))
                        ins.then_inc(pv_full, 1)
                    if kind == "turn_out":
                        pe.wait_ge(pv_read, k + 1)
                        for t in range(TB):
                            ins = tr(ps[:, 7, tile_cols(t)], oT[:, k % 2, tile_cols(t)], id_f[:])
                        ins.then_inc(bank_full, 1)
                    if kind == "turn_back":
                        for t in range(TB):
                            ins = tr(ps[:, 7, tile_cols(t)], o_nat[:, t].rearrange("p h e -> p (h e)"), id_f[:])
                        ins.then_inc(bank_full, 1)
                    if kind == "project":
                        for t in range(TB):
                            mm(ps[:, 7, tile_cols(t)], ones_f[0:1, :], ob_sb[:], start=True, stop=False)
                            ins = mm(ps[:, 7, tile_cols(t)], onT[:, tile_cols(t)], wo_sb[:], start=False, stop=True)
                        ins.then_inc(bank_full, 1)
                    if kind == "norm":
                        pe.wait_ge(ln_done, B + k + 1)
                        for t in range(TB):
                            ins = tr(ps[:, 7, tile_cols(t)], xn[:, k * TB + t, :], id_f[:])
                        ins.then_inc(bank_full, 1)

            pe.wait_ge(bank_read, len(BANK_USE))
            pe.wait_ge(ffn_in, 32)
            mm(ps[0:B, 0, 0:EXPERTS0], pooled[:], wg_sb[:], start=True, stop=True).then_inc(gate_full, 1)
            pe.wait_ge(gate_diag, 1)
            mm(ps[:, 0, 32:32 + 2 * B], ones_f[0:B, :], small[:, 0:2 * B], start=True, stop=True).then_inc(gate_rows, 1)
            for b in range(B):
                pe.wait_ge(sel_done, b + 1)
                for t in range(TB):
                    ins = mm(ps[:, b, tile_cols(t)], xT[:, b * N + t * P:b * N + (t + 1) * P], w_sel[:, 1, b, :],
                             start=True, stop=True)
                ins.then_inc(y0_full, 1)
            for b in range(B):
                pe.wait_ge(ln_done, 2 * B + b + 1)
                for t in range(TB):
                    ins = tr(ps[:, b, tile_cols(t)], xn[:, b * TB + t, :], id_f[:])
                ins.then_inc(turned3, 1)
            pe.wait_ge(mamba_in, 16 * 12)
            for b in range(B):
                pe.wait_ge(xT3_done, B if b else 1)
                if b >= 2:
                    pe.wait_ge(z_done, b - 1)
                for k in range(4):
                    ins = mm(ps[:, 4 * ((b + 1) % 2) + k, :], win_sb[:, tile_cols(k)], xT[:, b * N:(b + 1) * N],
                             start=True, stop=True)
                ins.then_inc(xz_full, 1)
            pe.wait_ge(z_done, B)
            for b in range(B):
                pe.wait_ge(xc_done, NH * (b + 1))
                for half in range(NH):
                    ins = mm(ps[:, b, :], wx_sb[:, half, :], xc[:, half, b * N:(b + 1) * N],
                             start=(half == 0), stop=(half == NH - 1))
                ins.then_inc(dbl_full, 1)
            for b in range(B):
                pe.wait_ge(dbl_done, b + 1)
                for half in range(NH):
                    k = NH * b + half
                    if k >= 4:
                        pe.wait_ge(dt_abs, k - 3)
                        pe.wait_ge(dt_relu, k - 3)
                    mm(ps[:, 4 + k % 4, :], wdt_sb[:, tile_cols(half)], dbl[0:DR, b * N:(b + 1) * N],
                       start=True, stop=True).then_inc(dt_full, 1)
            pe.wait_ge(c_done, B)
            pe.wait_ge(dt_abs, NH * B)
            pe.wait_ge(dt_relu, NH * B)
            pe.wait_ge(diag_done, 1)
            pe.sem_inc(y_added, 2)
            for q in range(NSPAN):
                if q:
                    pe.wait_ge(y_done, q)
                for half in range(NH):
                    for b in range(2):
                        mm(ps[:, 2 * half + b, :], d_diag[:, half, :],
                           xc[:, half, q * SPAN + b * N:q * SPAN + (b + 1) * N], start=True, stop=True)
                with pe.Fori(0, DS // 2) as i:
                    for j in range(2):
                        pe.wait_ge(c_used, i * 2 + (q * DS + j + 1))
                        for b in range(2):
                            ins = mm(ps[:, 4 + 2 * j + b, :],
                                     pick_sb[:, bass.ds(i * 2 + j, 1), :].rearrange("p o m -> p (o m)"),
                                     c_stack[:, q * SPAN + b * N:q * SPAN + (b + 1) * N], start=True, stop=True)
                        ins.then_inc(c_full, 1)
                        for half in range(NH):
                            pe.wait_ge(read_full, i * 4 + (q * 2 * DS + 2 * j + half + 1))
                            for b in range(2):
                                ins = mm(ps[:, 2 * half + b, :], id_f[:], read_out[:, half, b * N:(b + 1) * N],
                                         start=False, stop=True, skip_group_check=True)
                            ins.then_inc(y_added, 1)
                pe.wait_ge(y_added, (q + 1) * 2 * DS + 2)
                pe.sem_inc(y_full, 1)
            pe.wait_ge(y_done, NSPAN)
            for b in range(B):
                for t in range(TB):
                    cols = slice(b * N + t * P, b * N + (t + 1) * P)
                    for half in range(NH):
                        ins = mm(ps[:, 4 + b, tile_cols(t)], sz[:, half, cols], wout_sb[:, half, :],
                                 start=(half == 0), stop=(half == NH - 1))
                ins.then_inc(out1_full, 1)
            for b in range(B):
                pe.wait_ge(ln_done, 4 * B + b + 1)
                for t in range(TB):
                    ins = tr(ps[:, b, tile_cols(t)], xn[:, b * TB + t, :], id_f[:])
                ins.then_inc(turned4, 1)
            pe.wait_ge(moe_in, 16 * 10)
            pe.wait_ge(xT4_done, B)
            for t in range(NT):
                ins = mm(ps[:, 4, t * E1:(t + 1) * E1], xT[:, tile_cols(t)], gw_sb[:], start=True, stop=True)
            ins.then_inc(logits_full, 1)
            pe.wait_ge(probs_done, 1)
            for k in range(2):
                ins = tr(ps[:, 5, tile_cols(k)], prob[:, k * 8:(k + 1) * 8, :].rearrange("p i e -> p (i e)"), id_f[:])
            ins.then_inc(probs_turned, 1)
            with pe.Fori(0, BITS) as i:
                pe.wait_ge(counted, i + 1)
                mm(ps[:, 6, 0:1], same_sb[:], count[:], start=True, stop=True).then_inc(summed, 1)
            pe.wait_ge(thr_ready, 1)
            tr(ps[:, 6, P:2 * P], thr_b[:], id_f[:]).then_inc(thr_turned, 1)
            pe.wait_ge(runs_done, 1)
            mm(ps[:, 7, 0:256], before_sb[:], even[:].rearrange("p e i -> p (e i)"), start=True, stop=False)
            mm(ps[:, 7, 0:256], onesb_sb[:], run_b[:, 1].rearrange("p e i -> p (e i)"), start=False, stop=True)
            mm(ps[:, 7, 256:256 + E1], onesb_sb[:], run_b[:, 0, :, NT - 1], start=True,
               stop=True).then_inc(ranks_full, 1)
            pe.wait_ge(runs_done, 2)
            mm(ps[:, 6, 256:512], before_sb[:], picked_b[:].rearrange("p e i -> p (e i)"), start=True, stop=False)
            mm(ps[:, 6, 256:512], onesb_sb[:], run_b[:, 0].rearrange("p e i -> p (e i)"), start=False,
               stop=True).then_inc(ranks_full, 1)
            pe.wait_ge(hot_done, 1)
            for g in range(2):
                for t in range(NT):
                    ins = mm(ps[:, 5 + 2 * g, 0:P], hot_a[:, t, g * 8:(g + 1) * 8, :].rearrange("p e a -> p (e a)"),
                             val_b[:, g * 8:(g + 1) * 8, t].rearrange("p e k b -> p e (k b)"),
                             start=(t == 0), stop=(t == NT - 1))
                ins.then_inc(idx_full, 1)
            pe.wait_ge(idx_done, 2)
            pe.wait_ge(moe_w_in, 16 * 8)

            def shared_out(b):
                pe.wait_ge(shid_done, HC * (b + 1))
                for t in range(TB):
                    mm(ps[:, 4 + b, tile_cols(t)], ones_f[0:1, :], sb2_sb[:], start=True, stop=False)
                    for c in range(HC):
                        ins = mm(ps[:, 4 + b, tile_cols(t)], shid[:, b % 2, c, tile_cols(t)], sw2_sb[:, c, :],
                                 start=False, stop=(c == HC - 1))
                ins.then_inc(sy_full, 1)

            for b in range(B):
                for c in range(HC):
                    k = HC * b + c
                    if k >= 3:
                        pe.wait_ge(shid_done, k - 2)
                    mm(ps[:, 1 + k % 3, :], sw1_sb[:, tile_cols(c)], xT[:, b * N:(b + 1) * N], start=True,
                       stop=True).then_inc(shid_full, 1)
                if b:
                    shared_out(b - 1)
            shared_out(B - 1)

            def expert_in(e):
                pe.wait_ge(rows_in[e % AHEAD], 16 * (e // AHEAD + 1))
                if e >= 2:
                    pe.wait_ge(rowsT_done, e - 1)
                tr(ps[:, 4 * (e % 2), 0:P], rows[:, e, 0:D], id_f[:]).then_inc(rows_turned, 1)

            def expert_hidden(e):
                pe.wait_ge(rowsT_done, e + 1)
                if e >= 2:
                    pe.wait_ge(pre_done, e - 1)
                for c in range(HC):
                    ins = mm(ps[:, 1 + e % 2, tile_cols(c)], w1_sb[:, e, tile_cols(c)], rowsT[:, e % 2, :],
                             start=True, stop=True)
                ins.then_inc(eh_full, 1)

            def expert_out(e):
                pe.wait_ge(eh_done, e + 1)
                if e >= 2:
                    pe.wait_ge(routed_done, e - 1)
                o = ps[:, 3 + 2 * (e % 2), 0:P]
                mm(o, ones_f[0:1, :], b2_sb[:, e, :], start=True, stop=False)
                for c in range(HC):
                    ins = mm(o, hid[:, e % 2, c, :], w2_sb[:, e, c, :], start=False, stop=(c == HC - 1))
                ins.then_inc(ey_full, 1)

            pe.wait_ge(shid_done, HC * B)
            pe.wait_ge(base_done, B)
            expert_in(0)
            for e in range(E1 + 1):
                if e + 1 < E1:
                    expert_in(e + 1)
                if e < E1:
                    expert_hidden(e)
                if e:
                    expert_out(e - 1)


def _layout(x, L0_tok_W_emb, L0_tok_W_pos, L0_attn_edge_index, L0_attn_edge_attr, L0_attn_q_w, L0_attn_q_b,
            L0_attn_k_w, L0_attn_k_b, L0_attn_v_w, L0_attn_v_b, L0_attn_o_w, L0_attn_o_b, L0_attn_eb_w,
            L0_attn_eb_b, L0_ffn_Wg, L0_ffn_bg, L0_ffn_We, L0_ffn_be, L1_attn_W_in, L1_attn_conv_w, L1_attn_conv_b,
            L1_attn_W_xproj, L1_attn_W_dt, L1_attn_b_dt, L1_attn_A_log, L1_attn_D, L1_attn_W_out, L1_attn_gamma,
            L1_attn_beta, L1_ffn_gate_w, L1_ffn_w1, L1_ffn_b1, L1_ffn_w2, L1_ffn_b2, L1_ffn_sw1, L1_ffn_sb1,
            L1_ffn_sw2, L1_ffn_sb2):
    c = np.ascontiguousarray
    rows = lambda a: np.broadcast_to(a, (P,) + a.shape)
    wanted = np.full((P, 8), 2 * FAR, np.float32) + np.arange(8, dtype=np.float32)
    wanted[:, 0:TB] = np.arange(P)[:, None] + P * np.arange(TB)
    bf16 = mybir.dt.np(BF16)

    def halves(a):
        return c(a.reshape((NH, P) + a.shape[1:]).swapaxes(0, 1))

    wx = np.zeros((DI, P), np.float32)
    wx[:, 0:DR] = L1_attn_W_xproj[:, 0:DR]
    wx[:, 16:16 + DS] = L1_attn_W_xproj[:, DR:DR + DS]
    pick = np.zeros((P, DS, P), np.float32)
    for row in (32, 64, 96):
        wx[:, row:row + DS] = L1_attn_W_xproj[:, DR + DS:]
        pick[row + np.arange(DS), np.arange(DS)] = 1.0
    k = np.arange(P)
    return {
        "ids": c(x.reshape(NT, P).T.astype(np.int32)),
        "emb": c(L0_tok_W_emb.T),
        "pos": c(L0_tok_W_pos.reshape(TB, P, D).transpose(1, 0, 2)),
        "edges": c(L0_attn_edge_index[:, ::-1].reshape(2, P, EDGES // P).transpose(1, 0, 2).astype(np.int32)),
        "wanted": wanted,
        "attrs": c(L0_attn_edge_attr[::-1]),
        "ebw": c(rows(np.concatenate([L0_attn_eb_w.T, L0_attn_eb_b[None]]))),
        "ident": np.eye(P, dtype=np.float32),
        "identb": np.eye(P, dtype=np.float32).astype(bf16),
        "ones": np.ones((3, 3, H, N), bf16),
        "wq": c(L0_attn_q_w.T), "wk": c(L0_attn_k_w.T), "wv": c(L0_attn_v_w.T), "wo": c(L0_attn_o_w.T),
        "qb": c(L0_attn_q_b[:, None]), "kb": c(L0_attn_k_b[:, None]),
        "vb": c(rows(L0_attn_v_b)), "ob": c(L0_attn_o_b[None]),
        "lane": np.arange(P, dtype=np.float32)[:, None],
        "wg0": L0_ffn_Wg, "bg0": c(np.broadcast_to(L0_ffn_bg, (B, EXPERTS0))),
        "we0": c(L0_ffn_We.reshape(EXPERTS0 * D, D)), "be0": L0_ffn_be,
        "w_in": L1_attn_W_in, "conv_w": halves(L1_attn_conv_w), "conv_b": halves(L1_attn_conv_b),
        "w_x": halves(wx), "c_pick": pick.astype(bf16), "w_dt": L1_attn_W_dt, "b_dt": halves(L1_attn_b_dt),
        "a_log": halves(L1_attn_A_log), "d_skip": halves(L1_attn_D), "w_out": halves(L1_attn_W_out),
        "gamma": c(rows(L1_attn_gamma)), "beta": c(rows(L1_attn_beta)),
        "gate_w": L1_ffn_gate_w, "w1": c(L1_ffn_w1.transpose(1, 0, 2)),
        "b1": c(L1_ffn_b1.reshape(E1, HC, P).transpose(2, 0, 1)),
        "w2": c(L1_ffn_w2.reshape(E1, HC, P, D).transpose(2, 0, 1, 3)), "b2": c(L1_ffn_b2[None]),
        "sw1": L1_ffn_sw1, "sb1": c(L1_ffn_sb1.reshape(HC, P).T),
        "sw2": c(L1_ffn_sw2.reshape(HC, P, D).transpose(1, 0, 2)), "sb2": c(L1_ffn_sb2[None]),
        "same_expert": (k[:, None] % E1 == k[None] % E1).astype(np.float32),
        "bit_values": c(np.broadcast_to(1 << np.arange(BITS - 1, -1, -1), (P, BITS)).astype(np.int32)),
        "before": (k[:, None] < k[None]).astype(bf16), "onesb": np.ones((P, P), bf16),
        "run_start": c(rows((np.arange(E1 * NT) % NT != 0).astype(np.float32))),
        "a_iota": c(rows(np.arange(1, A1 + 1)).astype(bf16)), "b_iota": c(rows(np.arange(B1)).astype(bf16)),
        "tile_of": c(np.broadcast_to((np.arange(E1 * NT) % NT)[:, None], (P, E1 * NT, B1)).astype(bf16)),
        "own_expert": (k[:, None] // A1 == np.arange(B1)[None]).astype(np.float32),
    }


def kernel(**inputs):
    import concourse.bacc as bacc
    from concourse.bass_utils import run_bass_kernel_spmd

    arrays = _layout(**{k: np.asarray(v) for k, v in inputs.items()})
    nc = bacc.Bacc("TRN2", target_bir_lowering=False, num_devices=1)
    args = [nc.dram_tensor(name, a.shape, mybir.dt.from_np(a.dtype), kind="ExternalInput").ap()
            for name, a in arrays.items()]
    out = nc.dram_tensor("out", (T, D), F32, kind="ExternalOutput").ap()
    tower_kernel(nc, **dict(zip(arrays, args)), out=out)
    r = run_bass_kernel_spmd(nc, [arrays], core_ids=[0])
    return r.results[0]["out"].reshape(B, N, D)
```

```python
from contextlib import ExitStack

import numpy as np

import concourse.bass as bass
from concourse import mybir

F32 = mybir.dt.float32
BF16 = mybir.dt.bfloat16
F16 = mybir.dt.float16
I32 = mybir.dt.int32
U32 = mybir.dt.uint32
ACT = mybir.ActivationFunctionType
ALU = mybir.AluOpType
AX = mybir.AxisListType

P = 128
B, N, D = 4, 512, 128
T = B * N
NT = T // P
TB = N // P
H, HD = 8, 16
G = 4
NG = H // G
EDGES = 8192
EPS = 1e-5
EXPERTS0 = 16
DI, DS, DR, DC = 256, 16, 8, 4
NH = DI // P
E1, HID = 16, 512
CAP = T // E1
HC = HID // P
FAR = 1024.0
Q_PART = (0, 0, 0, 1, 1, 2)
K_PART = (0, 1, 2, 0, 1, 0)
NTERM = len(Q_PART)
Q_RUNS = ((0, 3, 0, 0), (3, 2, 1, 0), (5, 1, 2, 0))
K_RUNS = ((0, 3, 0, 1), (3, 2, 0, 1), (5, 1, 0, 0))
STACK_LOADS = len(Q_RUNS) + len(K_RUNS)
ROW_CB = NTERM * HD
ROW_MAX = ROW_CB + 3
ROWS_A, ROWS_B = ROW_MAX, ROW_MAX + 3
UNITS = B * H
QKV_BANK = (0, 3, 2, 5)
LAG = 7
SPAN = 1024
NSPAN = T // SPAN
ROUTE = D + E1
BITS = 30
STEPS = 16
AHEAD = 4
A1, B1 = 16, 8


def slots():
    out = []
    for u in range(UNITS + LAG + 10):
        now = []
        v = u - LAG

        def score(t, u=u, now=now):
            if u < UNITS:
                now.append(("score", u, t))

        def when(first, step, kind, count, v=v, now=now):
            if v >= first and (v - first) % step == 0 and (v - first) // step < count:
                now.append((kind, (v - first) // step, 0))

        score(0)
        if 0 <= v - G < UNITS:
            now.append(("pv", (v - G) // G, (v - G) % G))
        score(1)
        if u % G == 0 and 0 < u <= UNITS:
            now.append(("turn_max", u // G - 1, 0))
        if 0 <= v < UNITS:
            now.append(("prob", v, 0))
        score(2)
        if 0 <= v < UNITS:
            now.append(("prob", v, 1))
        score(3)
        if u < 2:
            now.append(("qkv", u + 2, 0))
        if 2 <= u < 4:
            now.append(("parts", u, 0))
        when(2 * G, G, "turn_out", UNITS // G)
        when(H + G + 2, H, "turn_back", B)
        when(H + G + 3, H, "project", B)
        when(H + G + 4, H, "normalise", B)
        when(H + G + 5, H, "norm", B)
        out.append(now)
    return out


SLOTS = slots()
BANK_USES = ("turn_max", "turn_out", "turn_back", "project", "norm")
BANK_USE = {piece: k for k, piece in enumerate(p for now in SLOTS for p in now if p[0] in BANK_USES)}


def tower_kernel(nc, ids, emb, pos, edges, wanted, absent, attrs, ebw, ident, identb, ones,
                 wq, wk, wv, wo, qb, kb, vb, ob,
                 lane, wg0, bg0, we0, be0,
                 w_in, conv_w, conv_b, w_x, c_pick, w_dt, b_dt, a_log, d_skip, w_out, gamma, beta,
                 gate_w, w1, b1, w2, b2, sw1, sb1, sw2, sb2,
                 same_expert, bit_values, before, onesb, run_start, a_iota, b_iota, tile_of, own_expert,
                 out):
    ctx = ExitStack()
    with ctx:
        def sb(name, shape, dt=F32, stack=ctx):
            return stack.enter_context(nc.sbuf_tensor(name, shape, dt))

        def sem(name):
            return ctx.enter_context(nc.semaphore(name))

        def dram(name, shape, dt=F32):
            return nc.dram_tensor(name, shape, dt, kind="Internal").ap()

        h = sb("h", [P, NT, D])
        xn = sb("xn", [P, NT, D])
        xT = sb("xT", [P, T])
        stats = sb("stats", [P, NT, 6])
        mv = sb("mv", [P, NT, 2])
        rstd = sb("rstd", [P, NT])
        vare = sb("vare", [P, NT])
        minus_half = sb("minus_half", [P, TB])
        id_f = sb("id_f", [P, P])
        id_b = sb("id_b", [P, P], BF16)

        ones_f = sb("ones_f", [P, P])
        lane_sb = sb("lane_sb", [P, 1])
        pooled = sb("pooled", [P, B])
        wg_sb = sb("wg_sb", [P, EXPERTS0])
        bg_sb = sb("bg_sb", [B, EXPERTS0])
        win_sb = sb("win_sb", [P, 2 * DI])
        cw_sb = sb("cw_sb", [P, NH, DC])
        cvb_sb = sb("cvb_sb", [P, NH])
        wx_sb = sb("wx_sb", [P, NH, P])
        pick_sb = sb("pick_sb", [P, DS, P], BF16)
        wdt_sb = sb("wdt_sb", [DR, DI])
        bdt_sb = sb("bdt_sb", [P, NH])
        a_sb = sb("a_sb", [P, NH, DS])
        ds_sb = sb("ds_sb", [P, NH])
        wout_sb = sb("wout_sb", [P, NH, D])
        gamma_sb = sb("gamma_sb", [P, D])
        beta_sb = sb("beta_sb", [P, D])

        ps = ctx.enter_context(nc.psum_tensor("ps", [P, 8, 512], F32))

        att = ExitStack()
        ids_sb = sb("ids_sb", [P, NT], I32, att)
        pos_sb = sb("pos_sb", [P, TB, D], F32, att)
        edge_sb = sb("edge_sb", [P, 2, EDGES // P], I32, att)
        edge_f = sb("edge_f", [P, 7, EDGES // P], F32, att)
        want_sb = sb("want_sb", [P, 8], F32, att)
        key_sb = sb("key_sb", [P, EDGES // P], F16, att)
        last = sb("last", [P, 8], U32, att)
        last_f = sb("last_f", [P, TB], F32, att)
        hit = sb("hit", [P, TB], F32, att)
        last_i = sb("last_i", [P, TB], I32, att)
        edge_a = sb("edge_a", [P, TB, 3], F32, att)
        ebw_sb = sb("ebw_sb", [P, 4, H], F32, att)
        cb = sb("cb", [P, 3, TB, H], F32, att)
        cb_prod = sb("cb_prod", [P, TB, H, 3], F32, att)
        cb_part = sb("cb_part", [P, 3, H, TB], BF16, att)
        cb_rest = sb("cb_rest", [P, H, TB], F32, att)
        cb_row = sb("cb_row", [3 * H * TB, P], BF16, att)
        wq_sb = sb("wq_sb", [P, P], F32, att)
        wk_sb = sb("wk_sb", [P, P], F32, att)
        wv_sb = sb("wv_sb", [P, P], F32, att)
        wo_sb = sb("wo_sb", [P, P], F32, att)
        qb_sb = sb("qb_sb", [P, 1], F32, att)
        qb4 = sb("qb4", [P, 1], F32, att)
        kb_sb = sb("kb_sb", [P, 1], F32, att)
        vb_sb = sb("vb_sb", [P, D], F32, att)
        ob_sb = sb("ob_sb", [1, D], F32, att)
        qk = sb("qk", [P, 2, 2, N], F32, att)
        qk_rest = sb("qk_rest", [P, 2, N], F32, att)
        qk_part = sb("qk_part", [P, 2, 2, 3, N], BF16, att)
        q_stack = sb("q_stack", [P, 3, H, N], BF16, att)
        k_stack = sb("k_stack", [P, 3, H, N], BF16, att)
        v_aug = sb("v_aug", [P, NT, H, 2 * HD], F32, att)
        nmax = sb("nmax", [P, 2, G * TB], F32, att)
        nmax_rest = sb("nmax_rest", [P, G * TB], F32, att)
        nmax_part = sb("nmax_part", [P, 2, 3, G * TB], BF16, att)
        nmax_row = sb("nmax_row", [3 * G * TB, 2, P], BF16, att)
        probs_mem = sb("probs_mem", [P, 2 * G * TB * N], F32, att)
        probs = probs_mem[:].rearrange("p (a g t n) -> p a g t n", a=2, g=G, t=TB)
        keys = probs_mem[:].bitcast(F16)[:, 0:EDGES + 8]
        oT = sb("oT", [P, 2, N], F32, att)
        r_den = sb("r_den", [P, TB, G], F32, att)
        o_nat = sb("o_nat", [P, TB, H, HD], F32, att)
        onT = sb("onT", [P, N], F32, att)
        att.close()

        mam = ExitStack()
        small = sb("small", [B, 96], F32, mam)
        top_i = sb("top_i", [B, 8], U32, mam)
        pick_b = sb("pick_b", [P, 2 * B], F32, mam)
        off_w = sb("off_w", [P, B], I32, mam)
        off_b = sb("off_b", [P, B], I32, mam)
        w_sel = sb("w_sel", [P, 2, B, D], F32, mam)
        b_sel = sb("b_sel", [P, 2, B, D], F32, mam)
        xi = sb("xi", [P, NH, B, N + DC - 1], F32, mam)
        sz = sb("sz", [P, NH, T], F32, mam)
        xc = sb("xc", [P, NH, T], F32, mam)
        dt = sb("dt", [P, NH, T], F32, mam)
        dtx = sb("dtx", [P, NH, T], F32, mam)
        dbl = sb("dbl", [32, T], F32, mam)
        c_stack = sb("c_stack", [P, T], BF16, mam)
        c_rest = sb("c_rest", [P, 2, N], F32, mam)
        c_mid = sb("c_mid", [P, 2, N], BF16, mam)
        a_neg = sb("a_neg", [P, NH, DS], F32, mam)
        d_diag = sb("d_diag", [P, NH, P], F32, mam)
        decay = sb("decay", [P, 4, SPAN], F32, mam)
        drive = sb("drive", [P, 4, SPAN], F32, mam)
        state = sb("state", [P, 2, SPAN], F32, mam)
        read_out = sb("read_out", [P, 2, SPAN], F32, mam)
        conv = read_out[:].rearrange("p k (j n) -> p (k j) n", n=N)
        b_row = sb("b_row", [P, 2, SPAN], F32, mam)
        mam.close()

        moe = ExitStack()
        gw_sb = sb("gw_sb", [P, E1], F32, moe)
        same_sb = sb("same_sb", [P, P], F32, moe)
        bits_sb = sb("bits_sb", [P, STEPS, 4], I32, moe)
        before_sb = sb("before_sb", [P, P], BF16, moe)
        onesb_sb = sb("onesb_sb", [P, P], BF16, moe)
        start_sb = sb("start_sb", [P, E1 * NT], F32, moe)
        ai_sb = sb("ai_sb", [P, A1], BF16, moe)
        bi_sb = sb("bi_sb", [P, B1], BF16, moe)
        tile_sb = sb("tile_sb", [P, E1 * NT, B1], BF16, moe)
        own_sb = sb("own_sb", [P, B1], F32, moe)
        sw1_sb = sb("sw1_sb", [P, HID], F32, moe)
        sw2_sb = sb("sw2_sb", [P, HC, D], F32, moe)
        sb1_sb = sb("sb1_sb", [P, HC], F32, moe)
        sb2_sb = sb("sb2_sb", [P, D], F32, moe)
        b1_sb = sb("b1_sb", [P, E1, HC], F32, moe)
        b2_sb = sb("b2_sb", [1, E1, D], F32, moe)
        zero_sb = sb("zero_sb", [P, D], F32, moe)
        logit = sb("logit", [P, NT, E1], F32, moe)
        prob = sb("prob", [P, NT, E1], F32, moe)
        rowmax = sb("rowmax", [P, 3, NT], F32, moe)
        prob_x = sb("prob_x", [P, 2 * P], F32, moe)
        hits_x = sb("hits_x", [P, 3, 2 * P], F32, moe)
        thr = sb("thr", [P, 1], I32, moe)
        cand = sb("cand", [P, 3], I32, moe)
        reach = sb("reach", [P, 3], F32, moe)
        reached = sb("reached", [P, 1], F32, moe)
        gained = sb("gained", [P, 1], I32, moe)
        count = sb("count", [P, 3], F32, moe)
        thr_b = sb("thr_b", [P, P], F32, moe)
        thr_n = sb("thr_n", [P, E1], F32, moe)
        need = sb("need", [P, E1], F32, moe)
        over = sb("over", [P, E1, NT], BF16, moe)
        even = sb("even", [P, E1, NT], BF16, moe)
        run = sb("run", [P, 2, E1, NT], F32, moe)
        run_b = sb("run_b", [P, 2, E1, NT], BF16, moe)
        picked = sb("picked", [P, 3, E1, NT], F32, moe)
        picked_b = sb("picked_b", [P, E1, NT], BF16, moe)
        slot_i = sb("slot_i", [P, 3, E1, NT], I32, moe)
        slot_b = sb("slot_b", [P, 2, E1, NT], BF16, moe)
        hot_a = sb("hot_a", [P, NT, E1, A1], BF16, moe)
        hot_b = sb("hot_b", [P, E1 * NT, B1], BF16, moe)
        val_b = sb("val_b", [P, E1, NT, 2, B1], BF16, moe)
        diag = sb("diag", [P, B1, 2 * B1], F32, moe)
        idx_v = sb("idx_v", [P, 2, 2 * B1], F32, moe)
        idx_i = sb("idx_i", [P, 2, B1], I32, moe)
        idx_t = sb("idx_t", [P, E1], I32, moe)
        w1_sb = sb("w1_sb", [P, E1, HID], F32, moe)
        w2_sb = sb("w2_sb", [P, E1, HC, D], F32, moe)
        rows = sb("rows", [P, E1, ROUTE], F32, moe)
        rowsT = sb("rowsT", [P, 2, P], F32, moe)
        hid = sb("hid", [P, 2, HC, P], F32, moe)
        pre = sb("pre", [P, 2, HC, P], F32, moe)
        shid = sb("shid", [P, HC, N], F32, moe)
        shared = sb("shared", [P, T], F32, moe)
        routed = sb("routed", [P, E1, D], F32, moe)
        moe.close()

        key_d = dram("key_d", [EDGES], F16)
        part_d = dram("part_d", [B, 2, 3, P, N], BF16)

        b_d = dram("b_d", [DS, T])
        route_d = dram("route_d", [T, ROUTE])
        odd_d = dram("odd_d", [T, D])
        idx_d = dram("idx_d", [E1 * CAP], I32)

        ids_in, pos_in, edges_in, proj_in, const_in, ebw_in = (
            sem(n) for n in ("ids_in", "pos_in", "edges_in", "proj_in", "const_in", "ebw_in"))
        emb_in = [sem(f"emb_in{b}") for b in range(B)]
        keys_out, keys_in, attr_in = sem("keys_out"), sem("keys_in"), sem("attr_in")
        key_done, last_done = sem("key_done"), sem("last_done")
        minus_half_set = sem("minus_half_set")
        dve_step, act_step, pool_step = sem("dve_step"), sem("act_step"), sem("pool_step")
        ln_mv, ln_rstd, ln_done = sem("ln_mv"), sem("ln_rstd"), sem("ln_done")
        turned, xT_done = sem("turned"), sem("xT_done")
        qkv_full, v_read = sem("qkv_full"), sem("v_read")
        part_cast, part_rest, parts_done = sem("part_cast"), sem("part_rest"), sem("parts_done")
        parts_out = [sem(f"parts_out{b}") for b in range(B)]
        stack_in = [sem(f"stack_in{b}") for b in range(B)]
        ones_in, row_in = sem("ones_in"), sem("row_in")
        cb_parts, cb_turned, cb_rows, cb_in = sem("cb_parts"), sem("cb_turned"), sem("cb_rows"), sem("cb_in")
        scores_full, scores_read = sem("scores_full"), sem("scores_read")
        max_parts = sem("max_parts")
        max_in = [sem(f"max_in{j}") for j in range(2)]
        expo_full, expo_read = sem("expo_full"), sem("expo_read")
        pv_full, pv_read = sem("pv_full"), sem("pv_read")
        bank_full, bank_read = sem("bank_full"), sem("bank_read")
        out_done = sem("out_done")
        lane_in, ffn_in, mamba_in, moe_in, moe_w_in = (
            sem(n) for n in ("lane_in", "ffn_in", "mamba_in", "moe_in", "moe_w_in"))
        gate_full, gate_exp, gate_diag, gate_rows, gate_off, sel_in, sel_done, y0_full = (
            sem(n) for n in ("gate_full", "gate_exp", "gate_diag", "gate_rows", "gate_off", "sel_in",
                             "sel_done", "y0_full"))
        gate_arg = sem("gate_arg")
        turned3, xT3_done = sem("turned3"), sem("xT3_done")
        pads_set, xz_full, xi_done, z_done = sem("pads_set"), sem("xz_full"), sem("xi_done"), sem("z_done")
        conv_done, xc_done = sem("conv_done"), sem("xc_done")
        dbl_full, dbl_done, c_cast, c_read0, c_done = (
            sem(n) for n in ("dbl_full", "dbl_done", "c_cast", "c_read0", "c_done"))
        b_out = sem("b_out")
        dt_full, dt_abs, dt_relu, dt_log, dt_done, dtx_done = (
            sem(n) for n in ("dt_full", "dt_abs", "dt_relu", "dt_log", "dt_done", "dtx_done"))
        a_done, diag_done, edge_zero = sem("a_done"), sem("diag_done"), sem("edge_zero")
        row_b_in = [sem(f"row_b_in{j}") for j in range(2)]
        c_full, c_used, b_used = sem("c_full"), sem("c_used"), sem("b_used")
        decay_full, drive_full, scanned, read_full, y_added = (
            sem(n) for n in ("decay_full", "drive_full", "scanned", "read_full", "y_added"))
        y_full, y_done = sem("y_full"), sem("y_done")
        out1_full, post_h2, h3_done = sem("out1_full"), sem("post_h2"), sem("h3_done")
        turned4, xT4_done = sem("turned4"), sem("xT4_done")
        logits_full, shifted, exped, probs_done, probs_turned, prob_x_done = (
            sem(n) for n in ("logits_full", "shifted", "exped", "probs_done", "probs_turned", "prob_x_done"))
        route_out = sem("route_out")
        counted, summed, bit_step = sem("counted"), sem("summed"), sem("bit_step")
        thr_ready, thr_turned = sem("thr_ready"), sem("thr_turned")
        runs_done, ranks_full = sem("runs_done"), sem("ranks_full")
        hot_done, idx_full, idx_done, idx_out, idx_in = (
            sem(n) for n in ("hot_done", "idx_full", "idx_done", "idx_out", "idx_in"))
        shid_full, shid_done, sy_full, base_done, base_out = (
            sem(n) for n in ("shid_full", "shid_done", "sy_full", "base_done", "base_out"))
        rows_in = [sem(f"rows_in{e}") for e in range(AHEAD)]
        rows_turned, rowsT_done, eh_full, pre_done, eh_done, ey_full, routed_done = (
            sem(n) for n in ("rows_turned", "rowsT_done", "eh_full", "pre_done", "eh_done", "ey_full",
                             "routed_done"))
        added = [sem("added_even"), sem("added_odd")]
        zeroed, shared_done, merged = sem("zeroed"), sem("shared_done"), sem("merged")

        block = ctx.enter_context(nc.Block())

        def tile_cols(i):
            return slice(i * P, (i + 1) * P)

        def load_stacks(queue, b):
            queue.wait_ge(parts_done, b + 1)
            queue.dma_start(part_d[b].rearrange("s j p n -> p s j n"), qk_part[:, b % 2]).then_inc(parts_out[b], 16)
            queue.wait_ge(parts_out[b], 16)
            if b >= 3:
                queue.wait_ge(expo_full, (b - 2) * H * 2)
            for dst, side, runs in ((q_stack, 0, Q_RUNS), (k_stack, 1, K_RUNS)):
                for first, count, part, step in runs:
                    src = part_d[b, side, part:part + 1 + step * (count - 1)].rearrange(
                        "c (e h) n -> c e (h n)", e=HD)
                    if not step:
                        src = src.to_broadcast([count, HD, H * N])
                    queue.dma_start(dst[first * HD:(first + count) * HD, b % 3], src).then_inc(stack_in[b], 16)

        @block.sync
        def _(sp):
            sp.dma_start(edge_sb[:], edges).then_inc(edges_in, 16)
            sp.dma_start(ids_sb[:], ids).then_inc(ids_in, 16)
            sp.dma_start(pos_sb[:], pos).then_inc(pos_in, 16)
            sp.dma_start(id_f[:], ident).then_inc(const_in, 16)
            sp.dma_start(id_b[:], identb).then_inc(const_in, 16)
            sp.dma_start(want_sb[:], wanted).then_inc(ebw_in, 16)
            sp.dma_start(keys[:, EDGES:], absent).then_inc(ebw_in, 16)
            sp.wait_ge(key_done, 1)
            sp.dma_start(key_d.rearrange("(p c) -> p c", p=P), key_sb[:]).then_inc(keys_out, 16)
            sp.dma_start(ebw_sb[:], ebw).then_inc(ebw_in, 16)
            sp.dma_start(wq_sb[:], wq).then_inc(proj_in, 16)
            sp.dma_start(wk_sb[:], wk).then_inc(proj_in, 16)
            sp.wait_ge(keys_out, 16)
            for k in range(4):
                part = slice(k * EDGES // 4, (k + 1) * EDGES // 4)
                sp.dma_start(keys[:, part], key_d[part].partition_broadcast(P)).then_inc(keys_in, 16)
            for dst, src in ((wv_sb, wv), (wo_sb, wo), (qb_sb, qb), (kb_sb, kb),
                             (vb_sb, vb), (ob_sb, ob)):
                sp.dma_start(dst[:], src).then_inc(proj_in, 16)
            sp.dma_start(q_stack[ROW_CB:ROW_MAX], ones).then_inc(row_in, 16)
            sp.dma_start(k_stack[ROW_MAX:ROWS_B], ones).then_inc(row_in, 16)
            sp.dma_start(lane_sb[:], lane).then_inc(lane_in, 16)
            sp.dma_start(wg_sb[:], wg0).then_inc(ffn_in, 16)
            sp.dma_start(bg_sb[:], bg0).then_inc(ffn_in, 16)
            load_stacks(sp, 0)
            sp.wait_ge(cb_rows, 1)
            for k in range(3):
                sp.dma_start(k_stack[ROW_CB:ROW_CB + 3, k].rearrange("j h (t n) -> j (h t) n", n=P),
                             cb_row[:]).then_inc(cb_in, 16)
            load_stacks(sp, 1)
            load_stacks(sp, 2)

            for g in range(UNITS // G):
                sp.wait_ge(bank_read, BANK_USE["turn_max", g, 0] + 1)
                b, g0 = g // NG, g % NG * G
                sp.dma_start(q_stack[ROW_MAX:ROWS_B, b % 3, g0:g0 + G].rearrange("j h (t n) -> j (h t) n", n=P),
                             nmax_row[:, g % 2, :]).then_inc(max_in[g % 2], 16)
                if g == 1:
                    for dst, src in ((win_sb, w_in), (cw_sb, conv_w), (cvb_sb, conv_b), (wx_sb, w_x),
                                     (pick_sb, c_pick), (wdt_sb, w_dt), (bdt_sb, b_dt), (a_sb, a_log),
                                     (ds_sb, d_skip), (wout_sb, w_out), (gamma_sb, gamma), (beta_sb, beta)):
                        sp.dma_start(dst[:], src).then_inc(mamba_in, 16)
            for b in range(B):
                sp.wait_ge(dbl_done, b + 1)
                sp.dma_start(b_d[:, b * N:(b + 1) * N], dbl[16:32, b * N:(b + 1) * N]).then_inc(b_out, 16)
            sp.wait_ge(b_out, 16 * B)
            for q in range(NSPAN):
                with sp.Fori(0, DS // 2) as i:
                    for j in range(2):
                        sp.wait_ge(b_used, i * 2 + (q * DS + j + 1))
                        sp.dma_start(b_row[:, j, :],
                                     b_d[bass.ds(i * 2 + j, 1), q * SPAN:(q + 1) * SPAN].partition_broadcast(P)
                                     ).then_inc(row_b_in[j], 16)
            sp.wait_ge(y_done, NSPAN)
            for k in range(4):
                part = slice(k * E1 // 4, (k + 1) * E1 // 4)
                sp.dma_start(w1_sb[:, part], w1[:, part]).then_inc(moe_w_in, 16)
                sp.dma_start(w2_sb[:, part], w2[:, part]).then_inc(moe_w_in, 16)
            sp.wait_ge(zeroed, 1)
            sp.dma_start(odd_d.rearrange("(i p) d -> p i d", p=P),
                         zero_sb[:].rearrange("p (o d) -> p o d", o=1).to_broadcast([P, NT, D])
                         ).then_inc(zeroed, 16)
            sp.wait_ge(ln_done, 5 * B)
            route_v = route_d.rearrange("(i p) c -> p i c", p=P)
            sp.dma_start(route_v[:, :, 0:D], xn[:]).then_inc(route_out, 16)
            sp.wait_ge(probs_done, 1)
            sp.dma_start(route_v[:, :, D:], prob[:]).then_inc(route_out, 16)
            sp.wait_ge(idx_done, 2)
            sp.dma_start(idx_d.rearrange("(g q b) -> q g b", g=2, b=B1), idx_i[:]).then_inc(idx_out, 16)
            sp.wait_ge(idx_out, 16)
            with nc.allow_non_contiguous_dma(reason="2048 token numbers"):
                sp.dma_start(idx_t[:], idx_d.rearrange("(e s) -> s e", e=E1)).then_inc(idx_in, 16)
            sp.wait_ge(base_done, 2)
            sp.dma_start(out.rearrange("(i p) d -> p i d", p=P), h[:]).then_inc(base_out, 16)
            sp.wait_ge(added[0], 8 * E1)
            sp.wait_ge(merged, 16)

        @block.gpsimd
        def _(pool):
            pool.memset(minus_half[:], -0.5).then_inc(minus_half_set, 1)
            pool.memset(ones_f[:], 1.0).then_inc(minus_half_set, 1)
            pool.wait_ge(ids_in, 16)
            roots = [0]

            def gather_tokens(b):
                for i in range(b * TB, (b + 1) * TB):
                    pool.indirect_dma_start(h[:, i, :], None, emb,
                                            bass.IndirectOffsetOnAxis(ids_sb[:, i:i + 1], 0)).then_inc(emb_in[b], 16)

            def root():
                k = roots[0]
                b = k % B
                pool.wait_ge(ln_mv, k + 1)
                nc.gpsimd.tensor_scalar(vare[:, b * TB:(b + 1) * TB], mv[:, b * TB:(b + 1) * TB, 1], EPS, None,
                                        ALU.add).then_inc(pool_step, 1)
                pool.wait_ge(pool_step, k + 1)
                if k == 0:
                    pool.wait_ge(minus_half_set, 2)
                nc.gpsimd.tensor_tensor(rstd[:, b * TB:(b + 1) * TB], vare[:, b * TB:(b + 1) * TB],
                                        minus_half[:], ALU.pow).then_inc(ln_rstd, 1)
                roots[0] += 1

            gather_tokens(0)
            gather_tokens(1)
            root()
            gather_tokens(2)
            root()
            gather_tokens(3)
            pool.memset(v_aug[:], 1.0).then_inc(ones_in, 1)
            pool.wait_ge(last_done, 1)
            for t in range(TB):
                pool.indirect_dma_start(edge_a[:, t, :], None, attrs,
                                        bass.IndirectOffsetOnAxis(last_i[:, t:t + 1], 0)).then_inc(attr_in, 16)
            root()
            root()
            load_stacks(pool, 3)
            for b in range(B):
                root()
            pool.wait_ge(gate_off, 1)
            for b in range(B):
                pool.indirect_dma_start(w_sel[:, 0, b, :], None, we0,
                                        bass.IndirectOffsetOnAxis(off_w[:, b:b + 1], 0)).then_inc(sel_in, 16)
                pool.indirect_dma_start(b_sel[:, 0, b, :], None, be0,
                                        bass.IndirectOffsetOnAxis(off_b[:, b:b + 1], 0)).then_inc(sel_in, 16)
            for b in range(B):
                root()
                if b == 0:
                    pool.memset(xi[:, :, :, 0:DC - 1], 0.0).then_inc(pads_set, 1)
                    pool.memset(decay[:].rearrange("p j (b n) -> p j b n", n=N)[:, :, :, 0:1], 0.0
                                ).then_inc(edge_zero, 1)
            pool.sem_inc(b_used, 2)
            pool.wait_ge(dtx_done, NH)
            for q in range(NSPAN):
                with pool.Fori(0, DS // 2) as i:
                    for j in range(2):
                        pool.wait_ge(row_b_in[j], i * 16 + (q * DS // 2 + 1) * 16)
                        for half in range(NH):
                            n = 2 * j + half
                            pool.wait_ge(scanned, i * 4 + (q * 2 * DS + n + 1))
                            ins = nc.gpsimd.tensor_tensor(drive[:, n, :], dtx[:, half, q * SPAN:(q + 1) * SPAN],
                                                          b_row[:, j, :], ALU.mult).then_inc(drive_full, 1)
                        pool.wait_ge(drive_full, i * 4 + (q * 2 * DS + 2 * j + 2))
                        pool.sem_inc(b_used, 1)
            for b in range(2 * B):
                root()
            pool.memset(zero_sb[:], 0.0).then_inc(zeroed, 1)
            pool.wait_ge(ln_done, 5 * B)
            pool.wait_ge(moe_in, 16 * 16)
            pool.wait_ge(h3_done, B)
            nc.gpsimd.tensor_tensor(h[:], h[:], sb2_sb[:].rearrange("p (o d) -> p o d", o=1)
                                    .to_broadcast([P, NT, D]), ALU.add).then_inc(base_done, 1)
            pool.wait_ge(base_done, 1)
            pool.wait_ge(shared_done, B + 1)
            nc.gpsimd.tensor_tensor(h[:], h[:], shared[:].rearrange("p (i d) -> p i d", d=D),
                                    ALU.add).then_inc(base_done, 1)
            pool.wait_ge(idx_in, 16)
            pool.wait_ge(route_out, 32)

            def gather_rows(e):
                if e >= AHEAD:
                    pool.wait_ge(rows_turned, e - AHEAD + 1)
                pool.indirect_dma_start(rows[:, e, :], None, route_d,
                                        bass.IndirectOffsetOnAxis(idx_t[:, e:e + 1], 0)).then_inc(rows_in[e % AHEAD], 16)

            def add_rows(e):
                k = e // 2
                pool.wait_ge(routed_done, e + 1)
                if k:
                    pool.wait_ge(added[e % 2], 16 * k)
                elif e:
                    pool.wait_ge(zeroed, 17)
                else:
                    pool.wait_ge(base_out, 16)
                pool.indirect_dma_start((out, odd_d)[e % 2], bass.IndirectOffsetOnAxis(idx_t[:, e:e + 1], 0),
                                        routed[:, e, :], None, compute_op=ALU.add).then_inc(added[e % 2], 16)

            for e in range(E1 + AHEAD):
                if e < E1:
                    gather_rows(e)
                if e >= AHEAD:
                    add_rows(e - AHEAD)
            pool.wait_ge(added[0], 8 * E1)
            pool.wait_ge(added[1], 8 * E1)
            pool.dma_start(out, odd_d, accum_op=ALU.add, max_dma_last_dim=8192).then_inc(merged, 16)

        @block.scalar
        def _(act):
            steps = [0]

            def link(ins):
                steps[0] += 1
                ins.then_inc(act_step, 1)
                act.wait_ge(act_step, steps[0])

            act.wait_ge(proj_in, 128)
            link(nc.scalar.mul(qb4[:], qb_sb[:], 1.0 / HD ** 0.5))

            def xT_copy(b):
                act.wait_ge(turned, b + 1)
                nc.scalar.copy(xT[:, b * N:(b + 1) * N], ps[:, 6 + b % 2, :]).then_inc(xT_done, 1)

            def qk_parts(b):
                act.wait_ge(qkv_full, b + 1)
                if b >= 2:
                    act.wait_ge(parts_done, b - 1)
                nc.scalar.activation(qk[:, b % 2, 0, :], ps[:, QKV_BANK[b], :], ACT.Identity, bias=qb4[:],
                                     scale=1.0 / HD ** 0.5)
                link(nc.scalar.activation(qk[:, b % 2, 1, :], ps[:, QKV_BANK[b] + 1, :], ACT.Identity,
                                          bias=kb_sb[:]))
                if b >= 2:
                    act.wait_ge(parts_out[b - 2], 16)
                nc.scalar.copy(qk_part[:, b % 2, :, 0, :], qk[:, b % 2]).then_inc(part_cast, 1)
                act.wait_ge(part_rest, b + 1)
                nc.scalar.copy(qk_part[:, b % 2, :, 1, :], qk_rest[:]).then_inc(part_cast, 1)

            xT_copy(0)
            xT_copy(1)
            qk_parts(0)
            qk_parts(1)
            xT_copy(2)
            xT_copy(3)
            act.wait_ge(cb_turned, 1)
            nc.scalar.copy(cb_row[:], ps[0:3 * H * TB, 7, 0:P // 2].bitcast(BF16)).then_inc(cb_rows, 1)
            for now in SLOTS:
                for piece in now:
                    kind, k, j = piece
                    if kind in ("turn_max", "turn_back", "norm"):
                        act.wait_ge(bank_full, BANK_USE[piece] + 1)
                    if kind == "qkv":
                        qk_parts(k)
                    if kind == "turn_max":
                        if k >= 2:
                            act.wait_ge(max_in[k % 2], 16 * (k // 2))
                        nc.scalar.copy(nmax_row[:, k % 2, :],
                                       ps[0:3 * G * TB, 7, 0:P // 2].bitcast(BF16)).then_inc(bank_read, 1)
                    if kind == "prob":
                        g, hh = k // G, k % G
                        if hh == 0 and j == 0 and g >= 2:
                            act.wait_ge(pv_full, g - 1)
                        act.wait_ge(expo_full, 2 * k + j + 1)
                        nc.scalar.activation(probs[:, g % 2, hh, 2 * j:2 * j + 2, :],
                                             ps[:, 2 + 2 * j:4 + 2 * j, :], ACT.Exp).then_inc(expo_read, 1)
                    if kind == "pv" and j == G - 1:
                        act.wait_ge(pv_full, k + 1)
                        nc.scalar.copy(oT[:, k % 2, :], ps[:, 6, :]).then_inc(pv_read, 1)
                    if kind == "turn_back":
                        nc.scalar.copy(onT[:], ps[:, 7, :]).then_inc(bank_read, 1)
                    if kind == "norm":
                        nc.scalar.activation(xT[:, k * N:(k + 1) * N], ps[:, 7, :], ACT.Copy,
                                             accum_out=pooled[:, k:k + 1]).then_inc(bank_read, 1)
            act.wait_ge(gate_full, 2)
            nc.scalar.activation(small[:, 32:48], small[:, 16:32], ACT.Exp, bias=small[:, 80:81],
                                 accum_out=small[:, 81:82]).then_inc(gate_exp, 1)
            for b in range(B):
                act.wait_ge(turned3, b + 1)
                nc.scalar.copy(xT[:, b * N:(b + 1) * N], ps[:, b, :]).then_inc(xT3_done, 1)
            for b in range(B):
                act.wait_ge(xz_full, b + 1)
                k0 = 4 * ((b + 1) % 2)
                for half in range(NH):
                    ins = nc.scalar.copy(xi[:, half, b, DC - 1:], ps[:, k0 + half, :])
                ins.then_inc(xi_done, 1)
                for half in range(NH):
                    ins = nc.scalar.activation(sz[:, half, b * N:(b + 1) * N], ps[:, k0 + NH + half, :], ACT.Silu)
                ins.then_inc(z_done, 1)
            for b in range(B):
                for half in range(NH):
                    act.wait_ge(conv_done, NH * b + half + 1)
                    nc.scalar.activation(xc[:, half, b * N:(b + 1) * N], conv[:, (half * 2 + 1), :], ACT.Silu,
                                         bias=cvb_sb[:, half:half + 1]).then_inc(xc_done, 1)
                act.wait_ge(dbl_full, b + 1)
                nc.scalar.copy(dbl[:, b * N:(b + 1) * N], ps[0:32, b, :]).then_inc(dbl_done, 1)
                nc.scalar.copy(c_stack[:, b * N:(b + 1) * N], ps[:, b, :]).then_inc(c_cast, 1)
            for b in range(B):
                for half in range(NH):
                    k = NH * b + half
                    act.wait_ge(dt_full, k + 1)
                    nc.scalar.activation(dt[:, half, b * N:(b + 1) * N], ps[:, 4 + k % 4, :], ACT.Abs,
                                         bias=bdt_sb[:, half:half + 1]).then_inc(dt_abs, 1)
            act.wait_ge(dt_abs, NH * B)
            for half in range(NH):
                link(nc.scalar.activation(dt[:, half, :], dt[:, half, :], ACT.Exp, scale=-1.0))
            act.wait_ge(mamba_in, 16 * 12)
            link(nc.scalar.activation(a_neg[:], a_sb[:], ACT.Exp))
            link(nc.scalar.mul(a_neg[:], a_neg[:], -1.0))
            for half in range(NH):
                nc.scalar.activation(dt[:, half, :], dt[:, half, :], ACT.Ln, bias=1.0).then_inc(dt_log, 1)
            act.wait_ge(dt_done, NH)
            act.wait_ge(edge_zero, 1)
            for q in range(NSPAN):
                if q == 1:
                    for dst, src in ((gw_sb, gate_w), (same_sb, same_expert), (bits_sb, bit_values),
                                     (before_sb, before), (onesb_sb, onesb), (start_sb, run_start), (ai_sb, a_iota),
                                     (bi_sb, b_iota), (tile_sb, tile_of), (own_sb, own_expert), (sw1_sb, sw1),
                                     (sw2_sb, sw2), (sb1_sb, sb1), (sb2_sb, sb2), (b1_sb, b1), (b2_sb, b2)):
                        act.dma_start(dst[:], src).then_inc(moe_in, 16)
                with act.Fori(0, DS // 2) as i:
                    for n in range(4):
                        j, half = n // 2, n % 2
                        act.wait_ge(scanned, i * 4 + (q * 2 * DS + n + 1))
                        nc.scalar.activation(
                            decay[:, n, :].rearrange("p (b n) -> p b n", n=N)[:, :, 1:],
                            dt[:, half, q * SPAN:(q + 1) * SPAN].rearrange("p (b n) -> p b n", n=N)[:, :, 1:],
                            ACT.Exp, scale=a_neg[:, half, bass.ds(i * 2 + j, 1)]).then_inc(decay_full, 1)
            for b in range(B):
                act.wait_ge(turned4, b + 1)
                nc.scalar.copy(xT[:, b * N:(b + 1) * N], ps[:, b, :]).then_inc(xT4_done, 1)
            act.wait_ge(shifted, 1)
            nc.scalar.activation(prob[:], logit[:], ACT.Exp).then_inc(exped, 1)
            act.sem_inc(shid_done, HC)
            act.wait_ge(moe_in, 16 * 16)
            act.sem_inc(shared_done, 1)
            with act.Fori(0, B) as i:
                for c in range(HC):
                    act.wait_ge(shid_full, i * HC + (c + 1))
                    act.wait_ge(sy_full, i + 1)
                    nc.scalar.activation(shid[:, c, :], ps[:, c, :], ACT.Gelu_apprx_tanh,
                                         bias=sb1_sb[:, c:c + 1]).then_inc(shid_done, 1)
                act.wait_ge(sy_full, i + 2)
                nc.scalar.activation(shared[:, bass.ds(i * N, N)], ps[:, 7, :], ACT.Copy).then_inc(shared_done, 1)

            def rows_turn(e):
                act.wait_ge(rows_turned, e + 1)
                if e >= 2:
                    act.wait_ge(eh_full, e - 1)
                nc.scalar.copy(rowsT[:, e % 2, :], ps[:, 4 * (e % 2), 0:P]).then_inc(rowsT_done, 1)

            rows_turn(0)
            rows_turn(1)
            for e in range(E1):
                if e + 2 < E1:
                    rows_turn(e + 2)
                act.wait_ge(pre_done, e + 1)
                if e >= 2:
                    act.wait_ge(ey_full, e - 1)
                nc.scalar.activation(hid[:, e % 2], pre[:, e % 2], ACT.Gelu_apprx_tanh).then_inc(eh_done, 1)

        @block.vector
        def _(dve):
            steps = [0]
            norms = [0]

            def link(ins):
                steps[0] += 1
                ins.then_inc(dve_step, 1)
                dve.wait_ge(dve_step, steps[0])

            def norm_stats(b, src):
                for i in range(b * TB, (b + 1) * TB):
                    ins = nc.vector.bn_stats(stats[:, i, :], src[:, i, :])
                link(ins)
                for i in range(b * TB, (b + 1) * TB):
                    ins = nc.vector.bn_aggr(mv[:, i, :], stats[:, i, :])
                ins.then_inc(ln_mv, 1)

            def normalise(b, src):
                norms[0] += 1
                dve.wait_ge(ln_rstd, norms[0])
                for i in range(b * TB, (b + 1) * TB):
                    ins = nc.vector.tensor_scalar(xn[:, i, :], src[:, i, :], mv[:, i, 0:1], rstd[:, i:i + 1],
                                                  ALU.subtract, ALU.mult)
                ins.then_inc(ln_done, 1)

            dve.wait_ge(edges_in, 16)
            src, tgt = edge_f[:, 0, :], edge_f[:, 1, :]
            link(nc.vector.tensor_copy(edge_f[:, 0:2, :], edge_sb[:]))
            link(nc.vector.tensor_scalar(edge_f[:, 2, :], src, 0.0, None, ALU.is_ge))
            link(nc.vector.scalar_tensor_tensor(edge_f[:, 3, :], src, float(N), edge_f[:, 2, :], ALU.is_lt, ALU.mult))
            link(nc.vector.scalar_tensor_tensor(edge_f[:, 4, :], tgt, 0.0, edge_f[:, 3, :], ALU.is_ge, ALU.mult))
            link(nc.vector.scalar_tensor_tensor(edge_f[:, 5, :], tgt, float(N), edge_f[:, 4, :], ALU.is_lt, ALU.mult))
            link(nc.vector.scalar_tensor_tensor(edge_f[:, 6, :], tgt, -FAR, edge_f[:, 5, :], ALU.add, ALU.mult))
            nc.vector.tensor_scalar(key_sb[:], edge_f[:, 6, :], FAR, None, ALU.add).then_inc(key_done, 1)

            def embed(b):
                dve.wait_ge(emb_in[b], 16 * TB)
                link(nc.vector.tensor_tensor(h[:, b * TB:(b + 1) * TB, :], h[:, b * TB:(b + 1) * TB, :],
                                             pos_sb[:], ALU.add))
                norm_stats(b, h)

            def qkv_parts(b):
                dve.wait_ge(part_cast, 2 * b + 1)
                nc.vector.tensor_tensor(qk_rest[:], qk[:, b % 2], qk_part[:, b % 2, :, 0, :],
                                        ALU.subtract).then_inc(part_rest, 1)
                dve.wait_ge(qkv_full, b + 1)
                vp = ps[:, QKV_BANK[b] + 2, :].rearrange("p (t h e) -> p t h e", t=TB, h=H)
                nc.vector.tensor_tensor(v_aug[:, b * TB:(b + 1) * TB, :, 0:HD], vp,
                                        vb_sb[:].rearrange("p (o h e) -> p o h e", o=1, h=H)
                                        .to_broadcast([P, TB, H, HD]), ALU.add).then_inc(v_read, 1)
                dve.wait_ge(part_cast, 2 * b + 2)
                nc.vector.tensor_tensor(qk_part[:, b % 2, :, 2, :], qk_rest[:], qk_part[:, b % 2, :, 1, :],
                                        ALU.subtract).then_inc(parts_done, 1)
                dve.wait_ge(parts_done, b + 1)

            dve.wait_ge(pos_in, 16)
            embed(0)
            embed(1)
            normalise(0, h)
            normalise(1, h)
            dve.wait_ge(keys_in, 64)
            dve.wait_ge(ebw_in, 48)
            link(nc.vector.max_index(last[:], want_sb[:], keys))
            link(nc.vector.tensor_copy(last_f[:], last[:, 0:TB]))
            nc.vector.tensor_scalar(hit[:], last_f[:], float(EDGES), None, ALU.is_lt)
            nc.vector.tensor_scalar(last_i[:], last_f[:], float(EDGES - 1), None, ALU.min).then_inc(last_done, 1)
            dve.wait_ge(proj_in, 128)
            dve.wait_ge(ones_in, 1)
            qkv_parts(0)
            embed(2)
            embed(3)
            normalise(2, h)
            normalise(3, h)
            dve.wait_ge(attr_in, 16 * TB)
            link(nc.vector.tensor_tensor(
                cb_prod[:], ebw_sb[:, 0:3, :].rearrange("p f (o h) -> p o h f", o=1).to_broadcast([P, TB, H, 3]),
                edge_a[:].rearrange("p t (o f) -> p t o f", o=1).to_broadcast([P, TB, H, 3]), ALU.mult))
            link(nc.vector.tensor_reduce(cb[:, 0], cb_prod[:], AX.X, ALU.add))
            link(nc.vector.tensor_tensor(cb[:, 1], cb[:, 0], ebw_sb[:, 3:4, :].to_broadcast([P, TB, H]), ALU.add))
            link(nc.vector.tensor_tensor(cb[:, 2], cb[:, 1], hit[:].rearrange("p (t o) -> p t o", o=1)
                                         .to_broadcast([P, TB, H]), ALU.mult))
            cbv = cb[:, 2].rearrange("p t h -> p h t")
            link(nc.vector.tensor_copy(cb_part[:, 0], cbv))
            link(nc.vector.tensor_tensor(cb_rest[:], cbv, cb_part[:, 0], ALU.subtract))
            link(nc.vector.tensor_copy(cb_part[:, 1], cb_rest[:]))
            nc.vector.tensor_tensor(cb_part[:, 2], cb_rest[:], cb_part[:, 1], ALU.subtract).then_inc(cb_parts, 1)
            qkv_parts(1)

            for now in SLOTS:
                for piece in now:
                    kind, k, j = piece
                    if kind == "parts":
                        qkv_parts(k)
                    if kind == "score":
                        g, hh, n = k // G, k % G, TB * k + j
                        dve.wait_ge(scores_full, n + 1)
                        nc.vector.tensor_reduce(nmax[:, g % 2, hh * TB + j:hh * TB + j + 1], ps[:, n % 2, :],
                                                AX.X, ALU.max, negate=True).then_inc(scores_read, 1)
                        if hh == G - 1 and j == TB - 1:
                            dve.wait_ge(scores_read, TB * (k + 1))
                            m = nmax[:, g % 2]
                            link(nc.vector.tensor_copy(nmax_part[:, g % 2, 0], m))
                            link(nc.vector.tensor_tensor(nmax_rest[:], m, nmax_part[:, g % 2, 0], ALU.subtract))
                            link(nc.vector.tensor_copy(nmax_part[:, g % 2, 1], nmax_rest[:]))
                            nc.vector.tensor_tensor(nmax_part[:, g % 2, 2], nmax_rest[:], nmax_part[:, g % 2, 1],
                                                    ALU.subtract).then_inc(max_parts, 1)
                            dve.wait_ge(max_parts, g + 1)
                    if kind in ("turn_out", "project"):
                        dve.wait_ge(bank_full, BANK_USE[piece] + 1)
                    if kind == "turn_out":
                        g = k % NG
                        o = ps[:, 7, :].rearrange("p (t g e) -> p t g e", t=TB, g=G)
                        link(nc.vector.reciprocal(r_den[:], o[:, :, :, HD]))
                        nc.vector.tensor_tensor(
                            o_nat[:, :, g * G:(g + 1) * G, :], o[:, :, :, 0:HD],
                            r_den[:].rearrange("p t (g o) -> p t g o", o=1).to_broadcast([P, TB, G, HD]),
                            ALU.mult).then_inc(bank_read, 1)
                    if kind == "project":
                        hb = h[:, k * TB:(k + 1) * TB, :]
                        nc.vector.tensor_tensor(hb, hb, ps[:, 7, :].rearrange("p (t d) -> p t d", t=TB),
                                                ALU.add).then_inc(bank_read, 1)
                        dve.wait_ge(bank_read, BANK_USE[piece] + 1)
                        norm_stats(k, h)
                    if kind == "normalise":
                        normalise(k, h)

            lg, ex, pr, top = small[:, 16:32], small[:, 32:48], small[:, 48:64], small[:, 64:72]
            dve.wait_ge(gate_full, 1)
            link(nc.vector.scalar_tensor_tensor(lg, ps[0:B, 0, 0:EXPERTS0], 1.0 / N, bg_sb[:], ALU.mult, ALU.add))
            nc.vector.tensor_reduce(small[:, 80:81], lg, AX.X, ALU.max, negate=True).then_inc(gate_full, 1)
            dve.wait_ge(gate_exp, 1)
            link(nc.vector.reciprocal(small[:, 82:83], small[:, 81:82]))
            link(nc.vector.tensor_scalar(pr, ex, small[:, 82:83], None, ALU.mult))
            link(nc.vector.max(top, pr))
            link(nc.vector.max_index(top_i[:], top, pr))
            link(nc.vector.tensor_copy(small[:, 83:84], top_i[:, 0:1]))
            nc.vector.tensor_scalar(small[:, 0:B], id_f[0:B, 0:B], small[:, 83:84], None, ALU.mult)
            nc.vector.tensor_scalar(small[:, B:2 * B], id_f[0:B, 0:B], top[:, 0:1], None,
                                    ALU.mult).then_inc(gate_diag, 1)
            dve.wait_ge(gate_rows, 1)
            dve.wait_ge(lane_in, 16)
            link(nc.vector.tensor_copy(pick_b[:], ps[:, 0, 32:32 + 2 * B]))
            nc.vector.tensor_scalar(off_w[:], pick_b[:, 0:B], float(D), lane_sb[:], ALU.mult, ALU.add)
            nc.vector.tensor_copy(off_b[:], pick_b[:, 0:B]).then_inc(gate_off, 1)
            dve.wait_ge(sel_in, 16 * 2 * B)
            for b in range(B):
                nc.vector.tensor_scalar(w_sel[:, 1, b, :], w_sel[:, 0, b, :], pick_b[:, B + b:B + b + 1], None,
                                        ALU.mult).then_inc(sel_done, 1)
            for b in range(B):
                ins = nc.vector.tensor_scalar(b_sel[:, 1, b, :], b_sel[:, 0, b, :], pick_b[:, B + b:B + b + 1], None,
                                              ALU.mult)
            link(ins)
            for b in range(B + 1):
                if b < B:
                    hb = h[:, b * TB:(b + 1) * TB, :]
                    link(nc.vector.tensor_tensor(hb, hb, b_sel[:, 1, b:b + 1, :].to_broadcast([P, TB, D]), ALU.add))
                    dve.wait_ge(y0_full, b + 1)
                    link(nc.vector.tensor_tensor(hb, hb, ps[:, b, :].rearrange("p (t d) -> p t d", t=TB), ALU.add))
                    norm_stats(b, h)
                if b:
                    normalise(b - 1, h)

            dve.wait_ge(mamba_in, 16 * 12)
            dve.wait_ge(pads_set, 1)
            for half in range(NH):
                ins = nc.vector.tensor_scalar(d_diag[:, half, :], id_f[:], ds_sb[:, half:half + 1], None, ALU.mult)
            ins.then_inc(diag_done, 1)
            for b in range(B):
                dve.wait_ge(xi_done, b + 1)
                for half in range(NH):
                    if b:
                        dve.wait_ge(xc_done, NH * (b - 1) + half + 1)
                    c0, c1 = conv[:, half * 2, :], conv[:, half * 2 + 1, :]
                    link(nc.vector.tensor_scalar(c0, xi[:, half, b, 0:N], cw_sb[:, half, 0:1], None, ALU.mult))
                    link(nc.vector.scalar_tensor_tensor(c1, xi[:, half, b, 1:1 + N], cw_sb[:, half, 1:2], c0,
                                                        ALU.mult, ALU.add))
                    link(nc.vector.scalar_tensor_tensor(c0, xi[:, half, b, 2:2 + N], cw_sb[:, half, 2:3], c1,
                                                        ALU.mult, ALU.add))
                    nc.vector.scalar_tensor_tensor(c1, xi[:, half, b, 3:3 + N], cw_sb[:, half, 3:4], c0,
                                                   ALU.mult, ALU.add).then_inc(conv_done, 1)
            for b in range(B):
                cols = slice(b * N, (b + 1) * N)
                dve.wait_ge(c_cast, b + 1)
                rest, mid = c_rest[:, b % 2, :], c_mid[:, b % 2, :]
                link(nc.vector.tensor_tensor(rest, ps[:, b, :], c_stack[:, cols], ALU.subtract))
                link(nc.vector.tensor_copy(mid, rest))
                nc.vector.tensor_copy(c_stack[64:96, cols], mid[64:96])
                nc.vector.tensor_tensor(c_stack[96:128, cols], rest[96:128], mid[96:128],
                                        ALU.subtract).then_inc(c_done, 1)
            for b in range(B):
                for half in range(NH):
                    k = NH * b + half
                    dve.wait_ge(dt_abs, k + 1)
                    nc.vector.tensor_scalar(dtx[:, half, b * N:(b + 1) * N], ps[:, 4 + k % 4, :],
                                            bdt_sb[:, half:half + 1], 0.0, ALU.add, ALU.max).then_inc(dt_relu, 1)
            dve.wait_ge(dt_relu, NH * B)
            for half in range(NH):
                dve.wait_ge(dt_log, half + 1)
                nc.vector.tensor_tensor(dt[:, half, :], dt[:, half, :], dtx[:, half, :], ALU.add).then_inc(dt_done, 1)
            dve.wait_ge(xc_done, NH * B)
            for half in range(NH):
                dve.wait_ge(dt_done, half + 1)
                nc.vector.tensor_tensor(dtx[:, half, :], dt[:, half, :], xc[:, half, :], ALU.mult).then_inc(dtx_done, 1)
            dve.sem_inc(scanned, 4)
            dve.sem_inc(c_used, 2)
            for q in range(NSPAN):
                with dve.Fori(0, DS // 2) as i:
                    for n in range(4):
                        j, half = n // 2, n % 2
                        unit = q * 2 * DS + n
                        dve.wait_ge(decay_full, i * 4 + (unit + 1))
                        dve.wait_ge(drive_full, i * 4 + (unit + 1))
                        nc.vector.tensor_tensor_scan(state[:, half, :], decay[:, n, :], drive[:, n, :], 0.0,
                                                     ALU.mult, ALU.add).then_inc(scanned, 1)
                        dve.wait_ge(scanned, i * 4 + (unit + 5))
                        if half == 0:
                            dve.wait_ge(c_full, i * 2 + (q * DS + j + 1))
                        dve.wait_ge(y_added, i * 4 + (unit + 1))
                        ins = nc.vector.tensor_tensor(read_out[:, half, :].rearrange("p (b n) -> p b n", n=N),
                                                      state[:, half, :].rearrange("p (b n) -> p b n", n=N),
                                                      ps[:, 4 + 2 * j:6 + 2 * j, :], ALU.mult)
                        ins.then_inc(read_full, 1)
                        if half == 1:
                            dve.wait_ge(read_full, i * 4 + (unit + 1))
                            dve.sem_inc(c_used, 1)
                dve.wait_ge(y_full, q + 1)
                for half in range(NH):
                    s_ = sz[:, half, q * SPAN:(q + 1) * SPAN].rearrange("p (b n) -> p b n", n=N)
                    ins = nc.vector.tensor_tensor(s_, ps[:, 2 * half:2 * half + 2, :], s_, ALU.mult)
                ins.then_inc(y_done, 1)
            for b in range(B + 1):
                if b < B:
                    xb = xn[:, b * TB:(b + 1) * TB, :]
                    dve.wait_ge(out1_full, b + 1)
                    link(nc.vector.tensor_tensor(xb, xb, ps[:, 4 + b, :].rearrange("p (t d) -> p t d", t=TB), ALU.add))
                    norm_stats(b, xn)
                if b:
                    k = b - 1
                    normalise(k, xn)
                    dve.wait_ge(ln_done, 3 * B + b)
                    xb, hb = xn[:, k * TB:b * TB, :], h[:, k * TB:b * TB, :]
                    link(nc.vector.tensor_tensor(
                        xb, xb, gamma_sb[:].rearrange("p (o d) -> p o d", o=1).to_broadcast([P, TB, D]), ALU.mult))
                    link(nc.vector.tensor_tensor(
                        hb, hb, beta_sb[:].rearrange("p (o d) -> p o d", o=1).to_broadcast([P, TB, D]), ALU.add))
                    nc.vector.tensor_tensor(hb, hb, xb, ALU.add).then_inc(h3_done, 1)
            for b in range(B + 1):
                if b < B:
                    dve.wait_ge(h3_done, b + 1)
                    norm_stats(b, h)
                if b:
                    normalise(b - 1, h)
            dve.wait_ge(logits_full, 1)
            lgp = ps[:, 4, 0:NT * E1].rearrange("p (i e) -> p i e", e=E1)

            def over_e(a):
                return a.rearrange("p (i o) -> p i o", o=1).to_broadcast([P, NT, E1])

            link(nc.vector.tensor_reduce(rowmax[:, 0, :], lgp, AX.X, ALU.max))
            nc.vector.tensor_tensor(logit[:], lgp, over_e(rowmax[:, 0, :]), ALU.subtract).then_inc(shifted, 1)
            dve.wait_ge(exped, 1)
            link(nc.vector.tensor_reduce(rowmax[:, 1, :], prob[:], AX.X, ALU.add))
            link(nc.vector.reciprocal(rowmax[:, 2, :], rowmax[:, 1, :]))
            nc.vector.tensor_tensor(prob[:], prob[:], over_e(rowmax[:, 2, :]), ALU.mult).then_inc(probs_done, 1)
            dve.wait_ge(probs_turned, 1)
            nc.vector.tensor_copy(prob_x[:], ps[:, 5, 0:2 * P]).then_inc(prob_x_done, 1)
            dve.wait_ge(prob_x_done, 1)
            dve.wait_ge(moe_in, 16 * 16)
            nc.vector.memset(thr[:], 0).then_inc(bit_step, 1)
            with dve.Fori(0, STEPS) as i:
                dve.wait_ge(bit_step, i * 4 + 1)
                nc.vector.tensor_tensor(cand[:], thr[:].to_broadcast([P, 3]),
                                        bits_sb[:, bass.ds(i, 1), 0:3].rearrange("p o k -> p (o k)"),
                                        ALU.bitwise_or).then_inc(bit_step, 1)
                dve.wait_ge(bit_step, i * 4 + 2)
                for k in range(3):
                    ins = nc.vector.tensor_scalar(hits_x[:, k], prob_x[:], cand[:, k:k + 1].bitcast(F32), None, ALU.is_ge,
                                                  ALU.add, accum_out=count[:, k:k + 1])
                ins.then_inc(counted, 1)
                dve.wait_ge(summed, i + 1)
                nc.vector.tensor_scalar(reach[:], ps[:, 6, 0:3], float(CAP) - 0.5, None, ALU.is_gt, ALU.add,
                                        accum_out=reached[:]).then_inc(bit_step, 1)
                dve.wait_ge(bit_step, i * 4 + 3)
                nc.vector.tensor_tensor(gained[:], reached[:], bits_sb[:, bass.ds(i, 1), 0:1].rearrange("p o k -> p (o k)"),
                                        ALU.mult).then_inc(bit_step, 1)
                dve.wait_ge(bit_step, i * 4 + 4)
                nc.vector.tensor_tensor(thr[:], thr[:], gained[:], ALU.bitwise_or).then_inc(bit_step, 1)
            dve.wait_ge(bit_step, 4 * STEPS + 1)
            nc.vector.tensor_scalar(thr_b[:], ones_f[:], thr[:].bitcast(F32), None, ALU.mult).then_inc(thr_ready, 1)
            dve.wait_ge(thr_turned, 1)
            link(nc.vector.tensor_copy(thr_n[:], ps[:, 6, P:P + E1]))
            pe_t = prob[:].rearrange("p i e -> p e i")

            def over_i(a):
                return a.rearrange("p (e o) -> p e o", o=1).to_broadcast([P, E1, NT])

            def flat(a):
                return a.rearrange("p e i -> p (e i)")

            link(nc.vector.tensor_tensor(over[:], pe_t, over_i(thr_n[:]), ALU.is_gt))
            link(nc.vector.tensor_tensor(even[:], pe_t, over_i(thr_n[:]), ALU.is_equal))

            def runs(mask, k):
                link(nc.vector.tensor_tensor_scan(flat(run[:, k]), start_sb[:], flat(mask), 0.0, ALU.mult, ALU.add))

            link(nc.vector.tensor_copy(picked[:, 2], over[:]))
            runs(over[:], 0)
            runs(even[:], 1)
            link(nc.vector.tensor_copy(run_b[:, 0], run[:, 0]))
            nc.vector.tensor_tensor(run_b[:, 1], run[:, 1], even[:], ALU.subtract).then_inc(runs_done, 1)
            dve.wait_ge(ranks_full, 1)
            link(nc.vector.tensor_scalar(need[:], ps[:, 7, 256:256 + E1], -1.0, float(CAP), ALU.mult, ALU.add))
            link(nc.vector.tensor_tensor(picked[:, 0], ps[:, 7, 0:256].rearrange("p (e i) -> p e i", e=E1),
                                         over_i(need[:]), ALU.is_lt))
            link(nc.vector.tensor_tensor(picked[:, 1], picked[:, 0], even[:], ALU.mult))
            link(nc.vector.tensor_tensor(picked[:, 0], picked[:, 1], picked[:, 2], ALU.add))
            link(nc.vector.tensor_copy(picked_b[:], picked[:, 0]))
            runs(picked_b[:], 0)
            nc.vector.tensor_tensor(run_b[:, 0], run[:, 0], picked_b[:], ALU.subtract).then_inc(runs_done, 1)
            dve.wait_ge(ranks_full, 2)
            link(nc.vector.tensor_copy(slot_i[:, 0], ps[:, 6, 256:512].rearrange("p (e i) -> p e i", e=E1)))
            nc.vector.tensor_single_scalar(slot_i[:, 1], slot_i[:, 0], 3, ALU.arith_shift_right)
            link(nc.vector.tensor_single_scalar(slot_i[:, 2], slot_i[:, 0], B1 - 1, ALU.bitwise_and))
            nc.vector.scalar_tensor_tensor(slot_b[:, 0], slot_i[:, 1], 1.0, picked[:, 0], ALU.add, ALU.mult)
            link(nc.vector.tensor_copy(slot_b[:, 1], slot_i[:, 2]))
            link(nc.vector.tensor_tensor(
                hot_b[:], bi_sb[:].rearrange("p (o b) -> p o b", o=1).to_broadcast([P, E1 * NT, B1]),
                slot_b[:, 1].rearrange("p e (i o) -> p (e i) o", o=1).to_broadcast([P, E1 * NT, B1]), ALU.is_equal))
            vb_ = val_b[:].rearrange("p e i k b -> p (e i) k b")
            nc.vector.tensor_scalar(vb_[:, :, 0, :], hot_b[:], lane_sb[:], None, ALU.mult)
            nc.vector.tensor_tensor(vb_[:, :, 1, :], hot_b[:], tile_sb[:], ALU.mult)
            nc.vector.tensor_tensor(
                hot_a[:].rearrange("p i e a -> p e i a"),
                ai_sb[:].rearrange("p (o u a) -> p o u a", o=1, u=1).to_broadcast([P, E1, NT, A1]),
                slot_b[:, 0].rearrange("p e (i o) -> p e i o", o=1).to_broadcast([P, E1, NT, A1]),
                ALU.is_equal).then_inc(hot_done, 1)
            for g in range(2):
                dve.wait_ge(idx_full, g + 1)
                link(nc.vector.tensor_tensor(
                    diag[:], ps[:, 5 + 2 * g, 0:P].rearrange("p (e k) -> p e k", e=B1),
                    own_sb[:].rearrange("p (e o) -> p e o", o=1).to_broadcast([P, B1, 2 * B1]), ALU.mult))
                link(nc.vector.tensor_reduce(idx_v[:, g, :], diag[:].rearrange("p e k -> p k e"), AX.X, ALU.add))
                nc.vector.scalar_tensor_tensor(idx_i[:, g, :], idx_v[:, g, B1:], float(P), idx_v[:, g, 0:B1],
                                               ALU.mult, ALU.add).then_inc(idx_done, 1)
            def expert_bias(e):
                dve.wait_ge(eh_full, e + 1)
                if e >= 2:
                    dve.wait_ge(eh_done, e - 1)
                nc.vector.tensor_tensor(pre[:, e % 2], ps[:, 1 + e % 2, :].rearrange("p (c n) -> p c n", c=HC),
                                        b1_sb[:, e, :].rearrange("p (c o) -> p c o", o=1).to_broadcast([P, HC, P]),
                                        ALU.add).then_inc(pre_done, 1)

            expert_bias(0)
            for e in range(E1):
                if e + 1 < E1:
                    expert_bias(e + 1)
                dve.wait_ge(ey_full, e + 1)
                nc.vector.tensor_scalar(routed[:, e, :], ps[:, 3 + 2 * (e % 2), 0:P],
                                        rows[:, e, D + e:D + e + 1], None, ALU.mult).then_inc(routed_done, 1)

        @block.tensor
        def _(pe):
            mm, tr = nc.tensor.matmul, nc.tensor.transpose
            pe.wait_ge(const_in, 32)
            def turn(b):
                pe.wait_ge(ln_done, b + 1)
                if b >= 2:
                    pe.wait_ge(xT_done, b - 1)
                for i in range(TB):
                    ins = tr(ps[:, 6 + b % 2, tile_cols(i)], xn[:, b * TB + i, :], id_f[:])
                ins.then_inc(turned, 1)

            def project(b):
                if b == 0:
                    pe.wait_ge(proj_in, 128)
                if b >= 2:
                    pe.wait_ge(part_cast, 3)
                    pe.wait_ge(v_read, b - 1)
                    pe.wait_ge(cb_rows, 1)
                pe.wait_ge(xT_done, b + 1)
                cols = slice(b * N, (b + 1) * N)
                mm(ps[:, QKV_BANK[b], :], wq_sb[:], xT[:, cols], start=True, stop=True)
                mm(ps[:, QKV_BANK[b] + 1, :], wk_sb[:], xT[:, cols], start=True, stop=True)
                for i in range(TB):
                    ins = mm(ps[:, QKV_BANK[b] + 2, tile_cols(i)], xT[:, b * N + i * P:b * N + (i + 1) * P], wv_sb[:],
                             start=True, stop=True)
                ins.then_inc(qkv_full, 1)

            turn(0)
            turn(1)
            project(0)
            project(1)
            turn(2)
            turn(3)
            pe.wait_ge(cb_parts, 1)
            pe.wait_ge(xT_done, B)
            tr(ps[0:3 * H * TB, 7, 0:P // 2].bitcast(BF16), cb_part[:].rearrange("p j h t -> p (j h t)"),
               id_b[:]).then_inc(cb_turned, 1)
            pe.wait_ge(cb_in, 16 * 3)
            pe.wait_ge(row_in, 32)
            pe.wait_ge(minus_half_set, 2)
            pe.wait_ge(cb_rows, 1)
            pe.wait_ge(part_cast, 1)
            for now in SLOTS:
                for piece in now:
                    kind, k, j = piece
                    if kind in BANK_USES:
                        use = BANK_USE[piece]
                        if use:
                            pe.wait_ge(bank_read, use)
                    if kind == "score":
                        b, hh, n = k // H, k % H, TB * k + j
                        if hh == 0 and j == 0:
                            pe.wait_ge(stack_in[b], 16 * STACK_LOADS)
                        if n >= 2:
                            pe.wait_ge(scores_read, n - 1)
                        mm(ps[:, n % 2, :], q_stack[0:ROWS_A, b % 3, hh, tile_cols(j)],
                           k_stack[0:ROWS_A, b % 3, hh, :], start=True, stop=True).then_inc(scores_full, 1)
                    if kind == "qkv":
                        project(k)
                    if kind == "turn_max":
                        pe.wait_ge(max_parts, k + 1)
                        pe.wait_ge(v_read, B)
                        tr(ps[0:3 * G * TB, 7, 0:P // 2].bitcast(BF16),
                           nmax_part[:, k % 2].rearrange("p j m -> p (j m)"), id_b[:]).then_inc(bank_full, 1)
                    if kind == "prob":
                        b, hh, g, n = k // H, k % H, k // G, 2 * k + j
                        if n < 2:
                            pe.wait_ge(part_cast, 2 * B)
                        if k % G == 0 and j == 0:
                            pe.wait_ge(max_in[g % 2], 16 * (g // 2 + 1))
                        if n >= 2:
                            pe.wait_ge(expo_read, n - 1)
                        for t in range(2 * j, 2 * j + 2):
                            ins = mm(ps[:, 2 + t, :], k_stack[0:ROWS_B, b % 3, hh, tile_cols(t)],
                                     q_stack[0:ROWS_B, b % 3, hh, :], start=True, stop=True)
                        ins.then_inc(expo_full, 1)
                    if kind == "pv":
                        b, g = k // NG, k % NG
                        pe.wait_ge(expo_read, 2 * G * (k + 1) - (1 if j < 2 else 0))
                        if k and j == 0:
                            pe.wait_ge(pv_read, k)
                        for i in range(G):
                            ins = mm(ps[32 * i:32 * i + 32, 6, :], v_aug[:, b * TB + j, g * G + i, :],
                                     probs[:, k % 2, i, j, :], start=(j == 0), stop=(j == TB - 1))
                        if j == TB - 1:
                            ins.then_inc(pv_full, 1)
                    if kind == "turn_out":
                        pe.wait_ge(pv_read, k + 1)
                        for t in range(TB):
                            ins = tr(ps[:, 7, tile_cols(t)], oT[:, k % 2, tile_cols(t)], id_f[:])
                        ins.then_inc(bank_full, 1)
                    if kind == "turn_back":
                        for t in range(TB):
                            ins = tr(ps[:, 7, tile_cols(t)], o_nat[:, t].rearrange("p h e -> p (h e)"), id_f[:])
                        ins.then_inc(bank_full, 1)
                    if kind == "project":
                        for t in range(TB):
                            mm(ps[:, 7, tile_cols(t)], ones_f[0:1, :], ob_sb[:], start=True, stop=False)
                            ins = mm(ps[:, 7, tile_cols(t)], onT[:, tile_cols(t)], wo_sb[:], start=False, stop=True)
                        ins.then_inc(bank_full, 1)
                    if kind == "norm":
                        pe.wait_ge(ln_done, B + k + 1)
                        for t in range(TB):
                            ins = tr(ps[:, 7, tile_cols(t)], xn[:, k * TB + t, :], id_f[:])
                        ins.then_inc(bank_full, 1)

            pe.wait_ge(bank_read, len(BANK_USE))
            pe.wait_ge(ffn_in, 32)
            mm(ps[0:B, 0, 0:EXPERTS0], pooled[:], wg_sb[:], start=True, stop=True).then_inc(gate_full, 1)
            pe.wait_ge(gate_diag, 1)
            mm(ps[:, 0, 32:32 + 2 * B], ones_f[0:B, :], small[:, 0:2 * B], start=True, stop=True).then_inc(gate_rows, 1)
            for b in range(B):
                pe.wait_ge(sel_done, b + 1)
                for t in range(TB):
                    ins = mm(ps[:, b, tile_cols(t)], xT[:, b * N + t * P:b * N + (t + 1) * P], w_sel[:, 1, b, :],
                             start=True, stop=True)
                ins.then_inc(y0_full, 1)
            for b in range(B):
                pe.wait_ge(ln_done, 2 * B + b + 1)
                for t in range(TB):
                    ins = tr(ps[:, b, tile_cols(t)], xn[:, b * TB + t, :], id_f[:])
                ins.then_inc(turned3, 1)
            pe.wait_ge(mamba_in, 16 * 12)
            for b in range(B):
                pe.wait_ge(xT3_done, B if b else 1)
                if b >= 2:
                    pe.wait_ge(z_done, b - 1)
                for k in range(4):
                    ins = mm(ps[:, 4 * ((b + 1) % 2) + k, :], win_sb[:, tile_cols(k)], xT[:, b * N:(b + 1) * N],
                             start=True, stop=True)
                ins.then_inc(xz_full, 1)
            pe.wait_ge(z_done, B)
            for b in range(B):
                pe.wait_ge(xc_done, NH * (b + 1))
                for half in range(NH):
                    ins = mm(ps[:, b, :], wx_sb[:, half, :], xc[:, half, b * N:(b + 1) * N],
                             start=(half == 0), stop=(half == NH - 1))
                ins.then_inc(dbl_full, 1)
            for b in range(B):
                pe.wait_ge(dbl_done, b + 1)
                for half in range(NH):
                    k = NH * b + half
                    if k >= 4:
                        pe.wait_ge(dt_abs, k - 3)
                        pe.wait_ge(dt_relu, k - 3)
                    mm(ps[:, 4 + k % 4, :], wdt_sb[:, tile_cols(half)], dbl[0:DR, b * N:(b + 1) * N],
                       start=True, stop=True).then_inc(dt_full, 1)
            pe.wait_ge(c_done, B)
            pe.wait_ge(dt_abs, NH * B)
            pe.wait_ge(dt_relu, NH * B)
            pe.wait_ge(diag_done, 1)
            pe.sem_inc(y_added, 2)
            for q in range(NSPAN):
                if q:
                    pe.wait_ge(y_done, q)
                for half in range(NH):
                    for b in range(2):
                        mm(ps[:, 2 * half + b, :], d_diag[:, half, :],
                           xc[:, half, q * SPAN + b * N:q * SPAN + (b + 1) * N], start=True, stop=True)
                with pe.Fori(0, DS // 2) as i:
                    for j in range(2):
                        pe.wait_ge(c_used, i * 2 + (q * DS + j + 1))
                        for b in range(2):
                            ins = mm(ps[:, 4 + 2 * j + b, :],
                                     pick_sb[:, bass.ds(i * 2 + j, 1), :].rearrange("p o m -> p (o m)"),
                                     c_stack[:, q * SPAN + b * N:q * SPAN + (b + 1) * N], start=True, stop=True)
                        ins.then_inc(c_full, 1)
                        for half in range(NH):
                            pe.wait_ge(read_full, i * 4 + (q * 2 * DS + 2 * j + half + 1))
                            for b in range(2):
                                ins = mm(ps[:, 2 * half + b, :], id_f[:], read_out[:, half, b * N:(b + 1) * N],
                                         start=False, stop=True, skip_group_check=True)
                            ins.then_inc(y_added, 1)
                pe.wait_ge(y_added, (q + 1) * 2 * DS + 2)
                pe.sem_inc(y_full, 1)
            pe.wait_ge(y_done, NSPAN)
            for b in range(B):
                for t in range(TB):
                    cols = slice(b * N + t * P, b * N + (t + 1) * P)
                    for half in range(NH):
                        ins = mm(ps[:, 4 + b, tile_cols(t)], sz[:, half, cols], wout_sb[:, half, :],
                                 start=(half == 0), stop=(half == NH - 1))
                ins.then_inc(out1_full, 1)
            for b in range(B):
                pe.wait_ge(ln_done, 4 * B + b + 1)
                for t in range(TB):
                    ins = tr(ps[:, b, tile_cols(t)], xn[:, b * TB + t, :], id_f[:])
                ins.then_inc(turned4, 1)
            pe.wait_ge(moe_in, 16 * 16)
            pe.wait_ge(xT4_done, B)
            for t in range(NT):
                ins = mm(ps[:, 4, t * E1:(t + 1) * E1], xT[:, tile_cols(t)], gw_sb[:], start=True, stop=True)
            ins.then_inc(logits_full, 1)
            pe.wait_ge(probs_done, 1)
            for k in range(2):
                ins = tr(ps[:, 5, tile_cols(k)], prob[:, k * 8:(k + 1) * 8, :].rearrange("p i e -> p (i e)"), id_f[:])
            ins.then_inc(probs_turned, 1)
            pe.wait_ge(shifted, 1)
            pe.wait_ge(prob_x_done, 1)
            pe.sem_inc(sy_full, 1)
            with pe.Fori(0, B) as i:
                for step in range(4):
                    pe.wait_ge(counted, i * 4 + (step + 1))
                    mm(ps[:, 6, 0:3], same_sb[:], count[:], start=True, stop=True).then_inc(summed, 1)
                    for k in range(2 * (step % 2), 2 * (step % 2) + 2):
                        if step < 2:
                            pe.wait_ge(shid_done, i * HC + (k + 1))
                            mm(ps[:, k, :], sw1_sb[:, tile_cols(k)], xT[:, bass.ds(i * N, N)], start=True,
                               stop=True).then_inc(shid_full, 1)
                        else:
                            if k == 0:
                                pe.wait_ge(shid_done, i * HC + 2 * HC)
                                pe.wait_ge(shared_done, i + 1)
                            for c in range(HC):
                                ins = mm(ps[:, 7, tile_cols(k)], shid[:, c, tile_cols(k)], sw2_sb[:, c, :],
                                         start=(c == 0), stop=(c == HC - 1))
                            if k == TB - 1:
                                ins.then_inc(sy_full, 1)
            pe.wait_ge(thr_ready, 1)
            tr(ps[:, 6, P:2 * P], thr_b[:], id_f[:]).then_inc(thr_turned, 1)
            pe.wait_ge(runs_done, 1)
            pe.wait_ge(shared_done, B + 1)
            mm(ps[:, 7, 0:256], before_sb[:], even[:].rearrange("p e i -> p (e i)"), start=True, stop=False)
            mm(ps[:, 7, 0:256], onesb_sb[:], run_b[:, 1].rearrange("p e i -> p (e i)"), start=False, stop=True)
            mm(ps[:, 7, 256:256 + E1], onesb_sb[:], run_b[:, 0, :, NT - 1], start=True,
               stop=True).then_inc(ranks_full, 1)
            pe.wait_ge(runs_done, 2)
            mm(ps[:, 6, 256:512], before_sb[:], picked_b[:].rearrange("p e i -> p (e i)"), start=True, stop=False)
            mm(ps[:, 6, 256:512], onesb_sb[:], run_b[:, 0].rearrange("p e i -> p (e i)"), start=False,
               stop=True).then_inc(ranks_full, 1)
            pe.wait_ge(hot_done, 1)
            for g in range(2):
                for t in range(NT):
                    ins = mm(ps[:, 5 + 2 * g, 0:P], hot_a[:, t, g * 8:(g + 1) * 8, :].rearrange("p e a -> p (e a)"),
                             val_b[:, g * 8:(g + 1) * 8, t].rearrange("p e k b -> p e (k b)"),
                             start=(t == 0), stop=(t == NT - 1))
                ins.then_inc(idx_full, 1)
            pe.wait_ge(idx_done, 2)
            pe.wait_ge(moe_w_in, 16 * 8)

            def expert_in(e):
                pe.wait_ge(rows_in[e % AHEAD], 16 * (e // AHEAD + 1))
                if e >= 2:
                    pe.wait_ge(rowsT_done, e - 1)
                tr(ps[:, 4 * (e % 2), 0:P], rows[:, e, 0:D], id_f[:]).then_inc(rows_turned, 1)

            def expert_hidden(e):
                pe.wait_ge(rowsT_done, e + 1)
                if e >= 2:
                    pe.wait_ge(pre_done, e - 1)
                for c in range(HC):
                    ins = mm(ps[:, 1 + e % 2, tile_cols(c)], w1_sb[:, e, tile_cols(c)], rowsT[:, e % 2, :],
                             start=True, stop=True)
                ins.then_inc(eh_full, 1)

            def expert_out(e):
                pe.wait_ge(eh_done, e + 1)
                if e >= 2:
                    pe.wait_ge(routed_done, e - 1)
                o = ps[:, 3 + 2 * (e % 2), 0:P]
                mm(o, ones_f[0:1, :], b2_sb[:, e, :], start=True, stop=False)
                for c in range(HC):
                    ins = mm(o, hid[:, e % 2, c, :], w2_sb[:, e, c, :], start=False, stop=(c == HC - 1))
                ins.then_inc(ey_full, 1)

            expert_in(0)
            expert_in(1)
            expert_hidden(0)
            for e in range(E1):
                if e + 2 < E1:
                    expert_in(e + 2)
                if e + 1 < E1:
                    expert_hidden(e + 1)
                expert_out(e)


def _layout(x, L0_tok_W_emb, L0_tok_W_pos, L0_attn_edge_index, L0_attn_edge_attr, L0_attn_q_w, L0_attn_q_b,
            L0_attn_k_w, L0_attn_k_b, L0_attn_v_w, L0_attn_v_b, L0_attn_o_w, L0_attn_o_b, L0_attn_eb_w,
            L0_attn_eb_b, L0_ffn_Wg, L0_ffn_bg, L0_ffn_We, L0_ffn_be, L1_attn_W_in, L1_attn_conv_w, L1_attn_conv_b,
            L1_attn_W_xproj, L1_attn_W_dt, L1_attn_b_dt, L1_attn_A_log, L1_attn_D, L1_attn_W_out, L1_attn_gamma,
            L1_attn_beta, L1_ffn_gate_w, L1_ffn_w1, L1_ffn_b1, L1_ffn_w2, L1_ffn_b2, L1_ffn_sw1, L1_ffn_sb1,
            L1_ffn_sw2, L1_ffn_sb2):
    c = np.ascontiguousarray
    rows = lambda a: np.broadcast_to(a, (P,) + a.shape)
    wanted = np.full((P, 8), 2 * FAR, np.float32) + np.arange(8, dtype=np.float32)
    wanted[:, 0:TB] = np.arange(P)[:, None] + P * np.arange(TB)
    bf16 = mybir.dt.np(BF16)

    def halves(a):
        return c(a.reshape((NH, P) + a.shape[1:]).swapaxes(0, 1))

    by_dim = np.arange(P).reshape(H, HD).T.reshape(P)
    wx = np.zeros((DI, P), np.float32)
    wx[:, 0:DR] = L1_attn_W_xproj[:, 0:DR]
    wx[:, 16:16 + DS] = L1_attn_W_xproj[:, DR:DR + DS]
    pick = np.zeros((P, DS, P), np.float32)
    for row in (32, 64, 96):
        wx[:, row:row + DS] = L1_attn_W_xproj[:, DR + DS:]
        pick[row + np.arange(DS), np.arange(DS)] = 1.0
    k = np.arange(P)
    steps = np.zeros((STEPS, 4), np.int32)
    steps[0:BITS // 2] = np.arange(1, 5) << np.arange(BITS - 2, -1, -2)[:, None]
    return {
        "ids": c(x.reshape(NT, P).T.astype(np.int32)),
        "emb": c(L0_tok_W_emb.T),
        "pos": c(L0_tok_W_pos.reshape(TB, P, D).transpose(1, 0, 2)),
        "edges": c(L0_attn_edge_index[:, ::-1].reshape(2, P, EDGES // P).transpose(1, 0, 2).astype(np.int32)),
        "wanted": wanted, "absent": wanted.astype(np.float16),
        "attrs": c(L0_attn_edge_attr[::-1]),
        "ebw": c(rows(np.concatenate([L0_attn_eb_w.T, L0_attn_eb_b[None]]))),
        "ident": np.eye(P, dtype=np.float32),
        "identb": np.eye(P, dtype=np.float32).astype(bf16),
        "ones": np.ones((3, 3, H, N), bf16),
        "wq": c(L0_attn_q_w.T[:, by_dim]), "wk": c(L0_attn_k_w.T[:, by_dim]), "wv": c(L0_attn_v_w.T), "wo": c(L0_attn_o_w.T),
        "qb": c(L0_attn_q_b[by_dim, None]), "kb": c(L0_attn_k_b[by_dim, None]),
        "vb": c(rows(L0_attn_v_b)), "ob": c(L0_attn_o_b[None]),
        "lane": np.arange(P, dtype=np.float32)[:, None],
        "wg0": L0_ffn_Wg, "bg0": c(np.broadcast_to(L0_ffn_bg, (B, EXPERTS0))),
        "we0": c(L0_ffn_We.reshape(EXPERTS0 * D, D)), "be0": L0_ffn_be,
        "w_in": L1_attn_W_in, "conv_w": halves(L1_attn_conv_w), "conv_b": halves(L1_attn_conv_b),
        "w_x": halves(wx), "c_pick": pick.astype(bf16), "w_dt": L1_attn_W_dt, "b_dt": halves(L1_attn_b_dt),
        "a_log": halves(L1_attn_A_log), "d_skip": halves(L1_attn_D), "w_out": halves(L1_attn_W_out),
        "gamma": c(rows(L1_attn_gamma)), "beta": c(rows(L1_attn_beta)),
        "gate_w": L1_ffn_gate_w, "w1": c(L1_ffn_w1.transpose(1, 0, 2)),
        "b1": c(L1_ffn_b1.reshape(E1, HC, P).transpose(2, 0, 1)),
        "w2": c(L1_ffn_w2.reshape(E1, HC, P, D).transpose(2, 0, 1, 3)), "b2": c(L1_ffn_b2[None]),
        "sw1": L1_ffn_sw1, "sb1": c(L1_ffn_sb1.reshape(HC, P).T),
        "sw2": c(L1_ffn_sw2.reshape(HC, P, D).transpose(1, 0, 2)), "sb2": c(rows(L1_ffn_sb2)),
        "same_expert": (k[:, None] % E1 == k[None] % E1).astype(np.float32),
        "bit_values": c(np.broadcast_to(steps, (P, STEPS, 4)).astype(np.int32)),
        "before": (k[:, None] < k[None]).astype(bf16), "onesb": np.ones((P, P), bf16),
        "run_start": c(rows((np.arange(E1 * NT) % NT != 0).astype(np.float32))),
        "a_iota": c(rows(np.arange(1, A1 + 1)).astype(bf16)), "b_iota": c(rows(np.arange(B1)).astype(bf16)),
        "tile_of": c(np.broadcast_to((np.arange(E1 * NT) % NT)[:, None], (P, E1 * NT, B1)).astype(bf16)),
        "own_expert": (k[:, None] // A1 == np.arange(B1)[None]).astype(np.float32),
    }


def kernel(**inputs):
    import concourse.bacc as bacc
    from concourse.bass_utils import run_bass_kernel_spmd

    arrays = _layout(**{k: np.asarray(v) for k, v in inputs.items()})
    nc = bacc.Bacc("TRN2", target_bir_lowering=False, num_devices=1)
    args = [nc.dram_tensor(name, a.shape, mybir.dt.from_np(a.dtype), kind="ExternalInput").ap()
            for name, a in arrays.items()]
    out = nc.dram_tensor("out", (T, D), F32, kind="ExternalOutput").ap()
    tower_kernel(nc, **dict(zip(arrays, args)), out=out)
    r = run_bass_kernel_spmd(nc, [arrays], core_ids=[0])
    return r.results[0]["out"].reshape(B, N, D)
```

```python
from contextlib import ExitStack

import numpy as np

import concourse.bass as bass
from concourse import mybir

F32 = mybir.dt.float32
BF16 = mybir.dt.bfloat16
F16 = mybir.dt.float16
I32 = mybir.dt.int32
U32 = mybir.dt.uint32
ACT = mybir.ActivationFunctionType
ALU = mybir.AluOpType
AX = mybir.AxisListType

P = 128
B, N, D = 4, 512, 128
T = B * N
NT = T // P
TB = N // P
H, HD = 8, 16
G = 4
NG = H // G
EDGES = 8192
EPS = 1e-5
EXPERTS0 = 16
DI, DS, DR, DC = 256, 16, 8, 4
NH = DI // P
E1, HID = 16, 512
CAP = T // E1
HC = HID // P
FAR = 1024.0
Q_PART = (0, 0, 0, 1, 1, 2)
K_PART = (0, 1, 2, 0, 1, 0)
NTERM = len(Q_PART)
Q_RUNS = ((0, 3, 0, 0), (3, 2, 1, 0), (5, 1, 2, 0))
K_RUNS = ((0, 3, 0, 1), (3, 2, 0, 1), (5, 1, 0, 0))
STACK_LOADS = len(Q_RUNS) + len(K_RUNS)
ROW_CB = NTERM * HD
ROW_MAX = ROW_CB + 3
ROWS_A, ROWS_B = ROW_MAX, ROW_MAX + 3
UNITS = B * H
QKV_BANK = (0, 3, 2, 5)
LAG = 7
SPAN = 1024
NSPAN = T // SPAN
SU = 4
ROUTE = D + E1
BITS = 30
STEPS = BITS // 2
LAST_NORMS = [("own", 0), ("own", 1), ("own", 2), ("next", 0), ("own", 3), ("next", 1), ("next", 2), ("next", 3)]
AHEAD = 5
A1, B1 = 16, 8


def slots():
    out = []
    for u in range(UNITS + LAG + 11):
        now = []
        v = u - LAG

        def score(t, u=u, now=now):
            if u < UNITS:
                now.append(("score", u, t))

        def when(first, step, kind, count, v=v, now=now):
            if v >= first and (v - first) % step == 0 and (v - first) // step < count:
                now.append((kind, (v - first) // step, 0))

        score(0)
        if 0 <= v - G < UNITS:
            now.append(("pv", (v - G) // G, (v - G) % G))
        score(1)
        if u % G == 0 and 0 < u <= UNITS:
            now.append(("turn_max", u // G - 1, 0))
        if 0 <= v < UNITS:
            now.append(("prob", v, 0))
        score(2)
        if 0 <= v < UNITS:
            now.append(("prob", v, 1))
        score(3)
        if u < 2:
            now.append(("qkv", u + 2, 0))
        if 2 <= u < 4:
            now.append(("parts", u, 0))
        when(2 * G, G, "turn_out", UNITS // G)
        when(H + G + 2, H, "turn_back", B)
        when(H + G + 3, H, "project", B)
        when(H + G + 4, H, "normalise", B)
        when(H + G + 6, H, "norm", B)
        out.append(now)
    last = [["gate 0"], [], [], [], ["pick 0"], [], [],
            ["select 0", "select 1", "update 0", "update 1"],
            ["renorm 0", "expand 0", "renorm 1"], [], [],
            ["conv 0 0", "gate 1", "expand 1", "conv 0 1", "smooth 0", "pick 1", "conv 1 0", "select 2", "select 3",
             "update 2", "update 3", "renorm 2", "renorm 3", "expand 2", "conv 1 1", "smooth 1", "expand 3", "conv 2 0",
             "conv 2 1", "conv 3 0", "conv 3 1"]]
    for now, more in zip(out[UNITS + LAG - 1:], last):
        for piece in more:
            kind, k, *half = piece.split()
            now.append((kind, int(k), int(half[0]) if half else 0))
    return out


SLOTS = slots()
NORMED = {piece: k for k, piece in enumerate((p for now in SLOTS for p in now if p[0] in ("normalise", "renorm")),
                                             B + 1)}
BANK_USES = ("turn_max", "turn_out", "turn_back", "project", "norm")
BANK_USE = {piece: k for k, piece in enumerate(p for now in SLOTS for p in now if p[0] in BANK_USES)}


def tower_kernel(nc, ids, emb, pos, edges, wanted, absent, attrs, ebw, ident, identb, ones,
                 wq, wk, wv, wo, qb, kb, vb, ob,
                 lane, wg0, bg0, we0, be0,
                 w_in, conv_w, conv_b, w_x, c_pick, w_dt, b_dt, a_log, d_skip, w_out, gamma, beta,
                 gate_w, w1, b1, w2, b2, sw1, sb1, sw2, sb2,
                 same_expert, bit_values, before, onesb, run_start, a_iota, b_iota, tile_of, own_expert, own_a,
                 out):
    ctx = ExitStack()
    with ctx:
        def sb(name, shape, dt=F32, stack=ctx):
            return stack.enter_context(nc.sbuf_tensor(name, shape, dt))

        def sem(name):
            return ctx.enter_context(nc.semaphore(name))

        def dram(name, shape, dt=F32):
            return nc.dram_tensor(name, shape, dt, kind="Internal").ap()

        h = sb("h", [P, NT, D])
        xn = sb("xn", [P, NT, D])
        xT = sb("xT", [P, T])
        stats = sb("stats", [P, NT, 6])
        mv = sb("mv", [P, NT, 2])
        rstd = sb("rstd", [P, NT])
        shift = sb("shift", [P, NT])
        vare = sb("vare", [P, NT])
        minus_half = sb("minus_half", [P, TB])
        id_f = sb("id_f", [P, P])
        id_b = sb("id_b", [P, P], BF16)

        ones_f = sb("ones_f", [P, P])
        lane_sb = sb("lane_sb", [P, 1])
        pooled = sb("pooled", [P, B])
        wg_sb = sb("wg_sb", [P, EXPERTS0])
        bg_sb = sb("bg_sb", [B, EXPERTS0])
        win_sb = sb("win_sb", [P, 2 * DI])
        cw_sb = sb("cw_sb", [P, NH, DC])
        cvb_sb = sb("cvb_sb", [P, NH])
        wx_sb = sb("wx_sb", [P, NH, P])
        pick_sb = sb("pick_sb", [P, DS + 1, P], BF16)
        wdt_sb = sb("wdt_sb", [DR, DI])
        bdt_sb = sb("bdt_sb", [P, NH])
        a_sb = sb("a_sb", [P, NH, DS])
        ds_sb = sb("ds_sb", [P, NH])
        wout_sb = sb("wout_sb", [P, NH, D])
        gamma_sb = sb("gamma_sb", [P, D])
        beta_sb = sb("beta_sb", [P, D])

        ps = ctx.enter_context(nc.psum_tensor("ps", [P, 8, 512], F32))

        att = ExitStack()
        qk = sb("qk", [P, 2, 2, N], F32, att)
        qk_rest = sb("qk_rest", [P, 2, N], F32, att)
        qk_part = sb("qk_part", [P, 2, 2, 3, N], BF16, att)
        q_stack = sb("q_stack", [P, 3, H, N], BF16, att)
        k_stack = sb("k_stack", [P, 3, H, N], BF16, att)
        ids_sb = sb("ids_sb", [P, NT], I32, att)
        pos_sb = sb("pos_sb", [P, TB, D], F32, att)
        edge_sb = sb("edge_sb", [P, 2, EDGES // P], I32, att)
        edge_f = sb("edge_f", [P, 7, EDGES // P], F32, att)
        want_sb = sb("want_sb", [P, 8], F32, att)
        key_sb = sb("key_sb", [P, EDGES // P], F16, att)
        last = sb("last", [P, 8], U32, att)
        last_f = sb("last_f", [P, TB], F32, att)
        hit = sb("hit", [P, TB], F32, att)
        last_i = sb("last_i", [P, TB], I32, att)
        edge_a = sb("edge_a", [P, TB, 3], F32, att)
        ebw_sb = sb("ebw_sb", [P, 4, H], F32, att)
        cb = sb("cb", [P, 3, TB, H], F32, att)
        cb_prod = sb("cb_prod", [P, TB, H, 3], F32, att)
        cb_part = sb("cb_part", [P, 3, H, TB], BF16, att)
        cb_rest = sb("cb_rest", [P, H, TB], F32, att)
        cb_row = sb("cb_row", [3 * H * TB, P], BF16, att)
        wq_sb = sb("wq_sb", [P, P], F32, att)
        wk_sb = sb("wk_sb", [P, P], F32, att)
        wv_sb = sb("wv_sb", [P, P], F32, att)
        wo_sb = sb("wo_sb", [P, P], F32, att)
        qb_sb = sb("qb_sb", [P, 1], F32, att)
        qb4 = sb("qb4", [P, 1], F32, att)
        kb_sb = sb("kb_sb", [P, 1], F32, att)
        vb_sb = sb("vb_sb", [P, D], F32, att)
        ob_sb = sb("ob_sb", [1, D], F32, att)
        v_aug = sb("v_aug", [P, NT, H, 2 * HD], F32, att)
        nmax = sb("nmax", [P, 2, G * TB], F32, att)
        nmax_rest = sb("nmax_rest", [P, G * TB], F32, att)
        nmax_part = sb("nmax_part", [P, 2, 3, G * TB], BF16, att)
        nmax_row = sb("nmax_row", [3 * G * TB, 2, P], BF16, att)
        probs_mem = sb("probs_mem", [P, 2 * G * TB * N], F32, att)
        probs = probs_mem[:].rearrange("p (a g t n) -> p a g t n", a=2, g=G, t=TB)
        keys = probs_mem[:].bitcast(F16)[:, 0:EDGES + 8]
        oT = sb("oT", [P, 2, N], F32, att)
        r_den = sb("r_den", [P, TB, G], F32, att)
        o_nat = sb("o_nat", [P, TB, H, HD], F32, att)
        onT = sb("onT", [P, N], F32, att)
        att.close()

        mam = ExitStack()
        small = sb("small", [2, 96], F32, mam)
        top_i = sb("top_i", [2, 8], U32, mam)
        pick_b = sb("pick_b", [P, 2, 4], F32, mam)
        off_w = sb("off_w", [P, B], I32, mam)
        off_b = sb("off_b", [P, B], I32, mam)
        sel_mem = sb("sel_mem", [P, 4, B * D], F32, mam)
        w_sel, b_sel = (sel_mem[:, k:k + 2].rearrange("p k (b d) -> p k b d", d=D) for k in (0, 2))
        c_rest = sel_mem[:].rearrange("p k e -> p (k e)").rearrange("p (b n) -> p b n", n=N)
        xi = sb("xi", [P, NH, B, N + DC - 1], F32, mam)
        sz = sb("sz", [P, NH, T], F32, mam)
        xc = sb("xc", [P, NH, T], F32, mam)
        dt = sb("dt", [P, NH, T], F32, mam)
        dtx = sb("dtx", [P, NH, T], F32, mam)
        dbl_mem = sb("dbl_mem", [P, 2, SPAN], F32, mam)
        dbl = dbl_mem[0:32].rearrange("p k n -> p (k n)")
        c_stack = sb("c_stack", [P, T], BF16, mam)
        c_mid = sb("c_mid", [P, B, N], BF16, mam)
        a_neg = sb("a_neg", [P, NH, DS], F32, mam)
        d_diag = sb("d_diag", [P, NH, P], F32, mam)
        decay = sb("decay", [P, 4, SPAN], F32, mam)
        drive = sb("drive", [P, 4, SPAN], F32, mam)
        state = sb("state", [P, 2, SPAN], F32, mam)
        read_out = sb("read_out", [P, 4, SPAN], F32, mam)
        conv = [a.rearrange("p k (j n) -> p k j n", n=N) for a in (read_out[:, 0:2], state[:])]
        b_mem = sb("b_mem", [P, 2, SPAN], F32, mam)
        b_row = (b_mem[:, 0, :], b_mem[:, 1, :], dbl_mem[:, 0, :], dbl_mem[:, 1, :])
        mam.close()

        moe = ExitStack()
        gw_sb = sb("gw_sb", [P, E1], F32, moe)
        same_sb = sb("same_sb", [P, P], F32, moe)
        bits_sb = sb("bits_sb", [P, STEPS + 1, 4], I32, moe)
        before_sb = sb("before_sb", [P, P], BF16, moe)
        onesb_sb = sb("onesb_sb", [P, P], BF16, moe)
        start_sb = sb("start_sb", [P, E1 * NT], F32, moe)
        ai_sb = sb("ai_sb", [P, A1], BF16, moe)
        bi_sb = sb("bi_sb", [P, B1], BF16, moe)
        tile_sb = sb("tile_sb", [P, E1 * NT, B1], BF16, moe)
        own_sb = sb("own_sb", [P, B1], F32, moe)
        own_a_sb = sb("own_a_sb", [P, A1], F32, moe)
        sw1_sb = sb("sw1_sb", [P, HID], F32, moe)
        sw2_sb = sb("sw2_sb", [P, HC, D], F32, moe)
        sb1_sb = sb("sb1_sb", [P, HC], F32, moe)
        sb2_sb = sb("sb2_sb", [P, D], F32, moe)
        b1_sb = sb("b1_sb", [P, E1, HC], F32, moe)
        b2_sb = sb("b2_sb", [1, E1, D], F32, moe)
        zero_sb = sb("zero_sb", [P, D], F32, moe)
        logit = sb("logit", [P, NT, E1], F32, moe)
        prob = sb("prob", [P, NT, E1], F32, moe)
        rowmax = sb("rowmax", [P, 3, NT], F32, moe)
        prob_x = sb("prob_x", [P, 2 * P], F32, moe)
        hits_x = sb("hits_x", [P, 3, 2 * P], F32, moe)
        cand = sb("cand", [P, 4], I32, moe)
        base = sb("base", [P, 4], I32, moe)
        reach = sb("reach", [P, 3], F32, moe)
        reached = sb("reached", [P, 1], F32, moe)
        gained = sb("gained", [P, 1], I32, moe)
        count = sb("count", [P, 3], F32, moe)
        thr_b = sb("thr_b", [P, P], F32, moe)
        thr_n = sb("thr_n", [P, E1], F32, moe)
        need = sb("need", [P, E1], F32, moe)
        over = sb("over", [P, E1, NT], BF16, moe)
        even = sb("even", [P, E1, NT], BF16, moe)
        run = sb("run", [P, 2, E1, NT], F32, moe)
        run_b = sb("run_b", [P, 2, E1, NT], BF16, moe)
        picked = sb("picked", [P, 3, E1, NT], F32, moe)
        picked_b = sb("picked_b", [P, E1, NT], BF16, moe)
        slot_i = sb("slot_i", [P, 3, E1, NT], I32, moe)
        slot_b = sb("slot_b", [P, 2, E1, NT], BF16, moe)
        hot_a = sb("hot_a", [P, NT, E1, A1], BF16, moe)
        hot_b = sb("hot_b", [P, E1 * NT, B1], BF16, moe)
        val_b = sb("val_b", [P, E1, NT, 2, B1], BF16, moe)
        diag = sb("diag", [P, B1, 2 * B1], F32, moe)
        idx_v = sb("idx_v", [P, 2, 2 * B1], F32, moe)
        idx_f = sb("idx_f", [P, 2, B1], F32, moe)
        idx_x = sb("idx_x", [P, 2, A1, B1], F32, moe)
        idx_t = sb("idx_t", [P, E1], I32, moe)
        w1_sb = sb("w1_sb", [P, E1, HID], F32, moe)
        w2_sb = sb("w2_sb", [P, E1, HC, D], F32, moe)
        rows = sb("rows", [P, E1, ROUTE], F32, moe)
        rowsT = sb("rowsT", [P, 2, P], F32, moe)
        hid = sb("hid", [P, 2, HC, P], F32, moe)
        pre = sb("pre", [P, 2, HC, P], F32, moe)
        shid = sb("shid", [P, HC, N], F32, moe)
        shared = sb("shared", [P, T], F32, moe)
        routed = sb("routed", [P, E1, D], F32, moe)
        moe.close()

        key_d = dram("key_d", [EDGES], F16)
        part_d = dram("part_d", [B, 2, 3, P, N], BF16)

        b_d = dram("b_d", [DS, T])
        route_d = dram("route_d", [T, ROUTE])
        odd_d = dram("odd_d", [T, D])

        ids_in, pos_in, edges_in, proj_in, const_in, ebw_in = (
            sem(n) for n in ("ids_in", "pos_in", "edges_in", "proj_in", "const_in", "ebw_in"))
        emb_in = [sem(f"emb_in{b}") for b in range(B)]
        keys_out, keys_in, attr_in = sem("keys_out"), sem("keys_in"), sem("attr_in")
        key_done, last_done = sem("key_done"), sem("last_done")
        minus_half_set = sem("minus_half_set")
        dve_step, act_step, pool_step = sem("dve_step"), sem("act_step"), sem("pool_step")
        ln_mv, ln_rstd, ln_shift, ln_done = sem("ln_mv"), sem("ln_rstd"), sem("ln_shift"), sem("ln_done")
        turned, xT_done = sem("turned"), sem("xT_done")
        qkv_full, v_read = sem("qkv_full"), sem("v_read")
        part_cast, part_rest, parts_done = sem("part_cast"), sem("part_rest"), sem("parts_done")
        parts_out = [sem(f"parts_out{b}") for b in range(B)]
        stack_in = [sem(f"stack_in{b}") for b in range(B)]
        ones_in, row_in = sem("ones_in"), sem("row_in")
        cb_parts, cb_turned, cb_rows, cb_in = sem("cb_parts"), sem("cb_turned"), sem("cb_rows"), sem("cb_in")
        scores_full, scores_read = sem("scores_full"), sem("scores_read")
        max_parts = sem("max_parts")
        max_in = [sem(f"max_in{j}") for j in range(2)]
        expo_full, expo_read = sem("expo_full"), sem("expo_read")
        pv_full, pv_read = sem("pv_full"), sem("pv_read")
        bank_full, bank_read = sem("bank_full"), sem("bank_read")
        lane_in, ffn_in, mamba_in, moe_in, moe_w_in = (
            sem(n) for n in ("lane_in", "ffn_in", "mamba_in", "moe_in", "moe_w_in"))
        gate_full, gate_exp, gate_diag, gate_rows, gate_off, sel_done, y0_full = (
            sem(n) for n in ("gate_full", "gate_exp", "gate_diag", "gate_rows", "gate_off", "sel_done", "y0_full"))
        bias_in = [sem(f"bias_in{b}") for b in range(B)]
        turned3, xT3_done = sem("turned3"), sem("xT3_done")
        pads_set, xz_full, xi_done, z_done = sem("pads_set"), sem("xz_full"), sem("xi_done"), sem("z_done")
        conv_done, xc_done = sem("conv_done"), sem("xc_done")
        beta_added = sem("beta_added")
        c_rest_done, c_mid_done = sem("c_rest_done"), sem("c_mid_done")
        late_mid_done, late_c_done = sem("late_mid_done"), sem("late_c_done")
        dbl_full, dbl_done, c_cast, c_done = (
            sem(n) for n in ("dbl_full", "dbl_done", "c_cast", "c_done"))
        b_out = sem("b_out")
        dt_full, dt_abs, dt_relu, dt_log, dt_done, dtx_done = (
            sem(n) for n in ("dt_full", "dt_abs", "dt_relu", "dt_log", "dt_done", "dtx_done"))
        diag_done, edge_zero = sem("diag_done"), sem("edge_zero")
        row_b_in = [sem(f"row_b_in{j}") for j in range(SU)]
        c_full = sem("c_full")
        decay_full, drive_full, scanned, read_full, y_added = (
            sem(n) for n in ("decay_full", "drive_full", "scanned", "read_full", "y_added"))
        y_full, y_done = sem("y_full"), sem("y_done")
        out1_full, out1_read = sem("out1_full"), sem("out1_read")
        turned4, xT4_done = sem("turned4"), sem("xT4_done")
        logits_full, shifted, exped, probs_done, probs_turned, prob_x_done = (
            sem(n) for n in ("logits_full", "shifted", "exped", "probs_done", "probs_turned", "prob_x_done"))
        route_out = sem("route_out")
        counted, summed, bit_step = sem("counted"), sem("summed"), sem("bit_step")
        thr_ready, thr_turned = sem("thr_ready"), sem("thr_turned")
        runs_done, ranks_full = sem("runs_done"), sem("ranks_full")
        hot_done, val_done, idx_full, idx_spread, idx_turned, idx_done = (
            sem(n) for n in ("hot_done", "val_done", "idx_full", "idx_spread", "idx_turned", "idx_done"))
        shid_full, shid_done, sy_full, base_done, base_out = (
            sem(n) for n in ("shid_full", "shid_done", "sy_full", "base_done", "base_out"))
        rows_in = [sem(f"rows_in{e}") for e in range(AHEAD)]
        rows_turned, rowsT_done, eh_full, pre_done, eh_done, ey_full, routed_done = (
            sem(n) for n in ("rows_turned", "rowsT_done", "eh_full", "pre_done", "eh_done", "ey_full",
                             "routed_done"))
        added = [sem("added_even"), sem("added_odd")]
        zeroed, shared_done, merged = sem("zeroed"), sem("shared_done"), sem("merged")

        block = ctx.enter_context(nc.Block())

        def tile_cols(i):
            return slice(i * P, (i + 1) * P)

        def load_stacks(queue, b):
            queue.wait_ge(parts_done, b + 1)
            queue.dma_start(part_d[b].rearrange("s j p n -> p s j n"), qk_part[:, b % 2]).then_inc(parts_out[b], 16)
            queue.wait_ge(parts_out[b], 16)
            if b >= 3:
                queue.wait_ge(expo_full, (b - 2) * H * 2)
            for dst, side, runs in ((q_stack, 0, Q_RUNS), (k_stack, 1, K_RUNS)):
                for first, count, part, step in runs:
                    src = part_d[b, side, part:part + 1 + step * (count - 1)].rearrange(
                        "c (e h) n -> c e (h n)", e=HD)
                    if not step:
                        src = src.to_broadcast([count, HD, H * N])
                    queue.dma_start(dst[first * HD:(first + count) * HD, b % 3], src).then_inc(stack_in[b], 16)

        @block.sync
        def _(sp):
            sp.dma_start(edge_sb[:], edges).then_inc(edges_in, 16)
            sp.dma_start(ids_sb[:], ids).then_inc(ids_in, 16)
            sp.dma_start(pos_sb[:], pos).then_inc(pos_in, 16)
            sp.dma_start(id_f[:], ident).then_inc(const_in, 16)
            sp.dma_start(id_b[:], identb).then_inc(const_in, 16)
            sp.dma_start(want_sb[:], wanted).then_inc(ebw_in, 16)
            sp.dma_start(keys[:, EDGES:], absent).then_inc(ebw_in, 16)
            sp.wait_ge(key_done, 1)
            sp.dma_start(key_d.rearrange("(p c) -> p c", p=P), key_sb[:]).then_inc(keys_out, 16)
            sp.dma_start(ebw_sb[:], ebw).then_inc(ebw_in, 16)
            sp.dma_start(wq_sb[:], wq).then_inc(proj_in, 16)
            sp.dma_start(wk_sb[:], wk).then_inc(proj_in, 16)
            sp.wait_ge(keys_out, 16)
            for k in range(4):
                part = slice(k * EDGES // 4, (k + 1) * EDGES // 4)
                sp.dma_start(keys[:, part], key_d[part].partition_broadcast(P)).then_inc(keys_in, 16)
            for dst, src in ((wv_sb, wv), (wo_sb, wo), (qb_sb, qb), (kb_sb, kb),
                             (vb_sb, vb), (ob_sb, ob)):
                sp.dma_start(dst[:], src).then_inc(proj_in, 16)
            sp.dma_start(q_stack[ROW_CB:ROW_MAX], ones).then_inc(row_in, 16)
            sp.dma_start(k_stack[ROW_MAX:ROWS_B], ones).then_inc(row_in, 16)
            sp.dma_start(lane_sb[:], lane).then_inc(lane_in, 16)
            sp.dma_start(wg_sb[:], wg0).then_inc(ffn_in, 16)
            sp.dma_start(bg_sb[:], bg0).then_inc(ffn_in, 16)
            load_stacks(sp, 0)
            sp.wait_ge(cb_rows, 1)
            for k in range(3):
                sp.dma_start(k_stack[ROW_CB:ROW_CB + 3, k].rearrange("j h (t n) -> j (h t) n", n=P),
                             cb_row[:]).then_inc(cb_in, 16)
            load_stacks(sp, 1)
            load_stacks(sp, 2)

            for g in range(UNITS // G):
                sp.wait_ge(bank_read, BANK_USE["turn_max", g, 0] + 1)
                b, g0 = g // NG, g % NG * G
                sp.dma_start(q_stack[ROW_MAX:ROWS_B, b % 3, g0:g0 + G].rearrange("j h (t n) -> j (h t) n", n=P),
                             nmax_row[:, g % 2, :]).then_inc(max_in[g % 2], 16)
                if g == 1:
                    for dst, src in ((win_sb, w_in), (cw_sb, conv_w), (cvb_sb, conv_b), (wx_sb, w_x),
                                     (pick_sb, c_pick), (wdt_sb, w_dt), (bdt_sb, b_dt), (a_sb, a_log),
                                     (ds_sb, d_skip), (wout_sb, w_out), (gamma_sb, gamma), (beta_sb, beta)):
                        sp.dma_start(dst[:], src).then_inc(mamba_in, 16)
            def row_of(q, i, j):
                sp.wait_ge(drive_full, i * (NH * SU) + (q * NH * DS + NH * (j + 1)))
                sp.dma_start(b_row[j],
                             b_d[bass.ds(i * SU + j, 1), q * SPAN:(q + 1) * SPAN].partition_broadcast(P)
                             ).then_inc(row_b_in[j], 16)

            for b in range(B):
                sp.wait_ge(dbl_done, b + 1)
                sp.dma_start(b_d[:, b * N:(b + 1) * N], dbl[16:32, b * N:(b + 1) * N]).then_inc(b_out, 16)
                if b == 1:
                    sp.wait_ge(b_out, 16 * 2)
                    row_of(0, 0, 0)
                    row_of(0, 0, 1)
            sp.wait_ge(b_out, 16 * B)
            sp.wait_ge(dt_full, NH * B)
            row_of(0, 0, 2)
            row_of(0, 0, 3)
            for q in range(NSPAN):
                with sp.Fori(1 - q, DS // SU) as i:
                    for j in range(SU):
                        row_of(q, i, j)
            sp.wait_ge(y_done, NH * NSPAN)
            for k in range(4):
                part = slice(k * E1 // 4, (k + 1) * E1 // 4)
                sp.dma_start(w1_sb[:, part], w1[:, part]).then_inc(moe_w_in, 16)
                sp.dma_start(w2_sb[:, part], w2[:, part]).then_inc(moe_w_in, 16)
            sp.wait_ge(zeroed, 1)
            sp.dma_start(odd_d.rearrange("(i p) d -> p i d", p=P),
                         zero_sb[:].rearrange("p (o d) -> p o d", o=1).to_broadcast([P, NT, D])
                         ).then_inc(zeroed, 16)
            sp.wait_ge(ln_done, 5 * B)
            route_v = route_d.rearrange("(i p) c -> p i c", p=P)
            sp.dma_start(route_v[:, :, 0:D], xn[:]).then_inc(route_out, 16)
            sp.wait_ge(probs_done, 1)
            sp.dma_start(route_v[:, :, D:], prob[:]).then_inc(route_out, 16)
            sp.wait_ge(base_done, 2)
            sp.dma_start(out.rearrange("(i p) d -> p i d", p=P), h[:]).then_inc(base_out, 16)
            sp.wait_ge(added[0], 8 * E1)
            sp.wait_ge(merged, 16)

        @block.gpsimd
        def _(pool):
            pool.memset(minus_half[:], -0.5).then_inc(minus_half_set, 1)
            pool.memset(ones_f[:], 1.0).then_inc(minus_half_set, 1)
            pool.wait_ge(ids_in, 16)
            roots = [0]

            def gather_tokens(b):
                for i in range(b * TB, (b + 1) * TB):
                    pool.indirect_dma_start(h[:, i, :], None, emb,
                                            bass.IndirectOffsetOnAxis(ids_sb[:, i:i + 1], 0)).then_inc(emb_in[b], 16)

            def root(b, shifted=False):
                tiles = slice(b * TB, (b + 1) * TB)
                pool.wait_ge(ln_mv, roots[0] + 1)
                if shifted:
                    nc.gpsimd.tensor_scalar(shift[:, tiles], mv[:, tiles, 0], -1.0, None, ALU.mult)
                nc.gpsimd.tensor_scalar(vare[:, tiles], mv[:, tiles, 1], EPS, None, ALU.add).then_inc(pool_step, 1)
                pool.wait_ge(pool_step, roots[0] + 1)
                if not roots[0]:
                    pool.wait_ge(minus_half_set, 2)
                nc.gpsimd.tensor_tensor(rstd[:, tiles], vare[:, tiles], minus_half[:], ALU.pow).then_inc(ln_rstd, 1)
                roots[0] += 1
                if shifted:
                    pool.wait_ge(ln_rstd, roots[0])
                    nc.gpsimd.tensor_tensor(shift[:, tiles], shift[:, tiles], rstd[:, tiles],
                                            ALU.mult).then_inc(ln_shift, 1)

            gather_tokens(0)
            gather_tokens(1)
            root(0)
            gather_tokens(2)
            root(1)
            gather_tokens(3)
            pool.memset(v_aug[:], 1.0).then_inc(ones_in, 1)
            pool.wait_ge(last_done, 1)
            for t in range(TB):
                pool.indirect_dma_start(edge_a[:, t, :], None, attrs,
                                        bass.IndirectOffsetOnAxis(last_i[:, t:t + 1], 0)).then_inc(attr_in, 16)
            root(2)
            root(3)
            load_stacks(pool, 3)
            for now in SLOTS:
                for kind, k, _ in now:
                    if kind in ("project", "update"):
                        root(k)
                    if kind == "update" and k == 0:
                        pool.memset(xi[:, :, :, 0:DC - 1], 0.0).then_inc(pads_set, 1)
                    if kind == "pick":
                        pool.wait_ge(gate_off, k + 1)
                        for b in (2 * k, 2 * k + 1):
                            pool.indirect_dma_start(w_sel[:, 0, b, :], None, we0,
                                                    bass.IndirectOffsetOnAxis(off_w[:, b:b + 1], 0)
                                                    ).then_inc(emb_in[b], 16)
                        for b in (2 * k, 2 * k + 1):
                            pool.indirect_dma_start(b_sel[:, 0, b, :], None, be0,
                                                    bass.IndirectOffsetOnAxis(off_b[:, b:b + 1], 0)
                                                    ).then_inc(bias_in[b], 16)
            pool.memset(decay[:].rearrange("p j (b n) -> p j b n", n=N)[:, :, :, 0:1], 0.0).then_inc(edge_zero, 1)
            pool.sem_inc(drive_full, NH * SU)
            pool.wait_ge(mamba_in, 16 * 12)
            pool.wait_ge(ln_done, 3 * B)
            nc.gpsimd.tensor_tensor(h[:], h[:], beta_sb[:].rearrange("p (o d) -> p o d", o=1)
                                    .to_broadcast([P, NT, D]), ALU.add).then_inc(beta_added, 1)
            for b in range(2):
                cols, rest, mid = slice(b * N, (b + 1) * N), c_rest[:, b, :], c_mid[:, b, :]
                pool.wait_ge(c_rest_done, b + 1)
                if not b:
                    pool.wait_ge(beta_added, 1)
                if b:
                    pool.wait_ge(c_done, 2 * b)
                nc.gpsimd.tensor_copy(mid[64:128], rest[64:128]).then_inc(c_mid_done, 1)
                pool.wait_ge(c_mid_done, b + 1)
                nc.gpsimd.tensor_copy(c_stack[64:96, cols], mid[64:96]).then_inc(c_done, 1)
                nc.gpsimd.tensor_tensor(c_stack[96:128, cols], rest[96:128], mid[96:128],
                                        ALU.subtract).then_inc(c_done, 1)
            pool.wait_ge(c_done, 4)
            for q in range(NSPAN):
                if q == 1:
                    pool.wait_ge(drive_full, NH * SU + NH * DS)
                    for b in range(2, B):
                        pool.wait_ge(late_mid_done, 2 * (b - 1))
                        nc.gpsimd.tensor_tensor(c_stack[96:128, b * N:(b + 1) * N], c_rest[96:128, b, :],
                                                c_mid[96:128, b, :], ALU.subtract).then_inc(late_c_done, 1)
                    pool.wait_ge(late_c_done, B - 2)
                with pool.Fori(0, DS // SU) as i:
                    for j in range(SU):
                        pool.wait_ge(row_b_in[j], i * 16 + (q * DS // SU + 1) * 16)
                        for half in range(NH):
                            n = NH * j + half
                            pool.wait_ge(dtx_done, NH * q + half + 1)
                            pool.wait_ge(scanned, i * (NH * SU) + (q * NH * DS + n + 1))
                            nc.gpsimd.tensor_tensor(drive[:, n % 4, :], dtx[:, half, q * SPAN:(q + 1) * SPAN],
                                                    b_row[j], ALU.mult).then_inc(drive_full, 1)
            for norm, b in LAST_NORMS:
                root(b, shifted=True)
            pool.memset(zero_sb[:], 0.0).then_inc(zeroed, 1)
            pool.wait_ge(ln_done, 5 * B)
            pool.wait_ge(moe_in, 16 * 17)
            nc.gpsimd.tensor_tensor(h[:], h[:], sb2_sb[:].rearrange("p (o d) -> p o d", o=1)
                                    .to_broadcast([P, NT, D]), ALU.add).then_inc(base_done, 1)
            pool.wait_ge(base_done, 1)
            pool.wait_ge(shared_done, B + 1)
            nc.gpsimd.tensor_tensor(h[:], h[:], shared[:].rearrange("p (i d) -> p i d", d=D),
                                    ALU.add).then_inc(base_done, 1)
            pool.wait_ge(route_out, 32)

            def gather_rows(e):
                if e % B1 == 0:
                    pool.wait_ge(idx_done, e // B1 + 1)
                if e >= AHEAD:
                    pool.wait_ge(rows_turned, e - AHEAD + 1)
                pool.indirect_dma_start(rows[:, e, :], None, route_d,
                                        bass.IndirectOffsetOnAxis(idx_t[:, e:e + 1], 0)
                                        ).then_inc(rows_in[e % AHEAD], 16)

            def add_rows(e):
                k = e // 2
                pool.wait_ge(routed_done, e + 1)
                if k:
                    pool.wait_ge(added[e % 2], 16 * k)
                elif e:
                    pool.wait_ge(zeroed, 17)
                else:
                    pool.wait_ge(base_out, 16)
                pool.indirect_dma_start((out, odd_d)[e % 2], bass.IndirectOffsetOnAxis(idx_t[:, e:e + 1], 0),
                                        routed[:, e, :], None, compute_op=ALU.add).then_inc(added[e % 2], 16)

            for e in range(E1 + AHEAD):
                if e < E1:
                    gather_rows(e)
                if e >= AHEAD:
                    add_rows(e - AHEAD)
            pool.wait_ge(added[0], 8 * E1)
            pool.wait_ge(added[1], 8 * E1)
            pool.dma_start(out, odd_d, accum_op=ALU.add, max_dma_last_dim=8192).then_inc(merged, 16)

        @block.scalar
        def _(act):
            steps = [0]

            def link(ins):
                steps[0] += 1
                ins.then_inc(act_step, 1)
                act.wait_ge(act_step, steps[0])

            act.wait_ge(proj_in, 128)
            link(nc.scalar.mul(qb4[:], qb_sb[:], 1.0 / HD ** 0.5))

            def xT_copy(b):
                act.wait_ge(turned, b + 1)
                nc.scalar.copy(xT[:, b * N:(b + 1) * N], ps[:, 6 + b % 2, :]).then_inc(xT_done, 1)

            def qk_parts(b):
                act.wait_ge(qkv_full, b + 1)
                if b >= 2:
                    act.wait_ge(parts_done, b - 1)
                nc.scalar.activation(qk[:, b % 2, 0, :], ps[:, QKV_BANK[b], :], ACT.Identity, bias=qb4[:],
                                     scale=1.0 / HD ** 0.5)
                link(nc.scalar.activation(qk[:, b % 2, 1, :], ps[:, QKV_BANK[b] + 1, :], ACT.Identity,
                                          bias=kb_sb[:]))
                if b >= 2:
                    act.wait_ge(parts_out[b - 2], 16)
                nc.scalar.copy(qk_part[:, b % 2, :, 0, :], qk[:, b % 2]).then_inc(part_cast, 1)
                act.wait_ge(part_rest, b + 1)
                nc.scalar.copy(qk_part[:, b % 2, :, 1, :], qk_rest[:]).then_inc(part_cast, 1)

            xT_copy(0)
            xT_copy(1)
            qk_parts(0)
            qk_parts(1)
            xT_copy(2)
            xT_copy(3)
            act.wait_ge(cb_turned, 1)
            nc.scalar.copy(cb_row[:], ps[0:3 * H * TB, 7, 0:P // 2].bitcast(BF16)).then_inc(cb_rows, 1)
            def silus(b):
                act.wait_ge(xz_full, 2 * b + 1)
                for half in range(NH):
                    ins = nc.scalar.copy(xi[:, half, b, DC - 1:], ps[:, 2 + half, :])
                ins.then_inc(xi_done, 1)
                act.wait_ge(xz_full, 2 * b + 2)
                for half in range(NH):
                    ins = nc.scalar.activation(sz[:, half, b * N:(b + 1) * N], ps[:, 2 + NH + half, :], ACT.Silu)
                ins.then_inc(z_done, 1)

            def conv_silu(b):
                for half in range(NH):
                    act.wait_ge(conv_done, NH * b + half + 1)
                    nc.scalar.activation(xc[:, half, b * N:(b + 1) * N], conv[b % 2][:, half, 1, :], ACT.Silu,
                                         bias=cvb_sb[:, half:half + 1]).then_inc(xc_done, 1)

            for now in SLOTS:
                for piece in now:
                    kind, k, j = piece
                    if kind in ("turn_max", "turn_back", "norm"):
                        act.wait_ge(bank_full, BANK_USE[piece] + 1)
                    if kind == "qkv":
                        qk_parts(k)
                    if kind == "turn_max":
                        if k >= 2:
                            act.wait_ge(max_in[k % 2], 16 * (k // 2))
                        nc.scalar.copy(nmax_row[:, k % 2, :],
                                       ps[0:3 * G * TB, 7, 0:P // 2].bitcast(BF16)).then_inc(bank_read, 1)
                    if kind == "prob":
                        g, hh = k // G, k % G
                        if hh == 0 and j == 0 and g >= 2:
                            act.wait_ge(pv_full, g - 1)
                        act.wait_ge(expo_full, 2 * k + j + 1)
                        nc.scalar.activation(probs[:, g % 2, hh, 2 * j:2 * j + 2, :],
                                             ps[:, 2 + 2 * j:4 + 2 * j, :], ACT.Exp).then_inc(expo_read, 1)
                    if kind == "pv" and j == G - 1:
                        act.wait_ge(pv_full, k + 1)
                        nc.scalar.copy(oT[:, k % 2, :], ps[:, 6, :]).then_inc(pv_read, 1)
                    if kind == "turn_back":
                        nc.scalar.copy(onT[:], ps[:, 7, :]).then_inc(bank_read, 1)
                    if kind == "norm":
                        nc.scalar.activation(xT[:, k * N:(k + 1) * N], ps[:, 7, :], ACT.Copy,
                                             accum_out=pooled[:, k:k + 1]).then_inc(bank_read, 1)
                    if kind == "gate":
                        act.wait_ge(gate_full, 2 * k + 2)
                        nc.scalar.activation(small[:, 32:48], small[:, 16:32], ACT.Exp, bias=small[:, 80:81],
                                             accum_out=small[:, 81:82]).then_inc(gate_exp, 1)
                    if kind == "renorm":
                        act.wait_ge(turned3, k + 1)
                        nc.scalar.copy(xT[:, k * N:(k + 1) * N], ps[:, k % 2, :]).then_inc(xT3_done, 1)
                    if kind == "expand":
                        silus(k)
                    if kind == "smooth":
                        conv_silu(k)
            def projected(b):
                act.wait_ge(dbl_full, b + 1)
                nc.scalar.copy(dbl[:, b * N:(b + 1) * N], ps[0:32, b, :]).then_inc(dbl_done, 1)
                nc.scalar.copy(c_stack[:, b * N:(b + 1) * N], ps[:, b, :]).then_inc(c_cast, 1)

            def dt_abs_of(b):
                for half in range(NH):
                    k = NH * b + half
                    act.wait_ge(dt_full, k + 1)
                    nc.scalar.activation(dt[:, half, b * N:(b + 1) * N], ps[:, 4 + k % 4, :], ACT.Abs,
                                         bias=bdt_sb[:, half:half + 1]).then_inc(dt_abs, 1)

            projected(0)
            projected(1)
            dt_abs_of(0)
            conv_silu(2)
            dt_abs_of(1)
            conv_silu(3)

            def log_of(q):
                act.wait_ge(dt_abs, NH * 2 * (q + 1))
                for half in range(NH):
                    d_ = dt[:, half, q * SPAN:(q + 1) * SPAN]
                    ins = nc.scalar.activation(d_, d_, ACT.Exp, scale=-1.0)
                if q == 0:
                    link(nc.scalar.activation(a_neg[:], a_sb[:], ACT.Exp))
                    link(nc.scalar.mul(a_neg[:], a_neg[:], -1.0))
                    projected(2)
                    projected(3)
                else:
                    link(ins)
                for half in range(NH):
                    d_ = dt[:, half, q * SPAN:(q + 1) * SPAN]
                    nc.scalar.activation(d_, d_, ACT.Ln, bias=1.0).then_inc(dt_log, 1)

            def decay_of(q, i, n):
                j, half = n // NH, n % NH
                act.wait_ge(dt_done, NH * q + half + 1)
                act.wait_ge(scanned, i * (NH * SU) + (q * NH * DS + n + 1))
                nc.scalar.activation(
                    decay[:, n % 4, :].rearrange("p (b n) -> p b n", n=N)[:, :, 1:],
                    dt[:, half, q * SPAN:(q + 1) * SPAN].rearrange("p (b n) -> p b n", n=N)[:, :, 1:],
                    ACT.Exp, scale=a_neg[:, half, bass.ds(i * SU + j, 1)]).then_inc(decay_full, 1)

            log_of(0)
            act.wait_ge(edge_zero, 1)
            dt_abs_of(2)
            dt_abs_of(3)
            for n in range(NH * SU):
                decay_of(0, 0, n)
            log_of(1)
            for b in range(2, B):
                act.wait_ge(c_rest_done, b + 1)
                nc.scalar.copy(c_stack[64:96, b * N:(b + 1) * N], c_rest[64:96, b, :]).then_inc(late_mid_done, 1)
                nc.scalar.copy(c_mid[96:128, b, :], c_rest[96:128, b, :]).then_inc(late_mid_done, 1)
            with act.Fori(1, DS // SU) as i:
                for n in range(NH * SU):
                    decay_of(0, i, n)
            act.wait_ge(late_c_done, B - 2)
            for dst, src in ((gw_sb, gate_w), (same_sb, same_expert), (bits_sb, bit_values),
                             (before_sb, before), (onesb_sb, onesb), (start_sb, run_start), (ai_sb, a_iota),
                             (bi_sb, b_iota), (tile_sb, tile_of), (own_sb, own_expert), (own_a_sb, own_a),
                             (sw1_sb, sw1),
                             (sw2_sb, sw2), (sb1_sb, sb1), (sb2_sb, sb2), (b1_sb, b1), (b2_sb, b2)):
                act.dma_start(dst[:], src).then_inc(moe_in, 16)
            with act.Fori(0, DS // SU) as i:
                for n in range(NH * SU):
                    decay_of(1, i, n)
            def xT_of(b):
                act.wait_ge(turned4, b + 1)
                nc.scalar.copy(xT[:, b * N:(b + 1) * N], ps[:, b, :]).then_inc(xT4_done, 1)

            for k, (norm, b) in enumerate(LAST_NORMS):
                if norm == "next" and b:
                    xT_of(b - 1)
                act.wait_ge(ln_shift, k + 1)
                for i in range(b * TB, (b + 1) * TB):
                    ins = nc.scalar.activation(xn[:, i, :], (xn if norm == "own" else h)[:, i, :], ACT.Identity,
                                               bias=shift[:, i:i + 1], scale=rstd[:, i:i + 1])
                ins.then_inc(ln_done, 1)
            xT_of(B - 1)
            act.wait_ge(shifted, 1)
            nc.scalar.activation(prob[:], logit[:], ACT.Exp).then_inc(exped, 1)
            act.sem_inc(shid_done, HC)
            act.wait_ge(moe_in, 16 * 17)
            act.sem_inc(shared_done, 1)
            with act.Fori(0, B) as i:
                for c in range(HC):
                    act.wait_ge(shid_full, i * HC + (c + 1))
                    act.wait_ge(sy_full, i + 1)
                    nc.scalar.activation(shid[:, c, :], ps[:, c, :], ACT.Gelu_apprx_tanh,
                                         bias=sb1_sb[:, c:c + 1]).then_inc(shid_done, 1)
                act.wait_ge(sy_full, i + 2)
                nc.scalar.activation(shared[:, bass.ds(i * N, N)], ps[:, 7, :], ACT.Copy).then_inc(shared_done, 1)

            act.wait_ge(hot_done, 1)
            nc.scalar.activation(val_b[:].rearrange("p e i k b -> p (e i) k b")[:, :, 0, :], hot_b[:], ACT.Copy,
                                 scale=lane_sb[:]).then_inc(val_done, 1)

            def rows_turn(e):
                act.wait_ge(rows_turned, e + 1)
                if e >= 2:
                    act.wait_ge(eh_full, e - 1)
                nc.scalar.copy(rowsT[:, e % 2, :], ps[:, 4 * (e % 2), 0:P]).then_inc(rowsT_done, 1)

            rows_turn(0)
            rows_turn(1)
            for e in range(E1):
                act.wait_ge(pre_done, e + 1)
                if e >= 2:
                    act.wait_ge(ey_full, e - 1)
                nc.scalar.activation(hid[:, e % 2], pre[:, e % 2], ACT.Gelu_apprx_tanh).then_inc(eh_done, 1)
                if e + 2 < E1:
                    rows_turn(e + 2)

        @block.vector
        def _(dve):
            steps = [0]
            norms = [0]

            def link(ins):
                steps[0] += 1
                ins.then_inc(dve_step, 1)
                dve.wait_ge(dve_step, steps[0])

            def norm_stats(b, src):
                for i in range(b * TB, (b + 1) * TB):
                    ins = nc.vector.bn_stats(stats[:, i, :], src[:, i, :])
                link(ins)
                for i in range(b * TB, (b + 1) * TB):
                    ins = nc.vector.bn_aggr(mv[:, i, :], stats[:, i, :])
                ins.then_inc(ln_mv, 1)

            def normalise(b, src):
                norms[0] += 1
                dve.wait_ge(ln_rstd, norms[0])
                for i in range(b * TB, (b + 1) * TB):
                    ins = nc.vector.tensor_scalar(xn[:, i, :], src[:, i, :], mv[:, i, 0:1], rstd[:, i:i + 1],
                                                  ALU.subtract, ALU.mult)
                ins.then_inc(ln_done, 1)

            dve.wait_ge(edges_in, 16)
            src, tgt = edge_f[:, 0, :], edge_f[:, 1, :]
            link(nc.vector.tensor_copy(edge_f[:, 0:2, :], edge_sb[:]))
            link(nc.vector.tensor_scalar(edge_f[:, 2, :], src, 0.0, None, ALU.is_ge))
            link(nc.vector.scalar_tensor_tensor(edge_f[:, 3, :], src, float(N), edge_f[:, 2, :], ALU.is_lt, ALU.mult))
            link(nc.vector.scalar_tensor_tensor(edge_f[:, 4, :], tgt, 0.0, edge_f[:, 3, :], ALU.is_ge, ALU.mult))
            link(nc.vector.scalar_tensor_tensor(edge_f[:, 5, :], tgt, float(N), edge_f[:, 4, :], ALU.is_lt, ALU.mult))
            link(nc.vector.scalar_tensor_tensor(edge_f[:, 6, :], tgt, -FAR, edge_f[:, 5, :], ALU.add, ALU.mult))
            nc.vector.tensor_scalar(key_sb[:], edge_f[:, 6, :], FAR, None, ALU.add).then_inc(key_done, 1)

            def embed(b):
                dve.wait_ge(emb_in[b], 16 * TB)
                link(nc.vector.tensor_tensor(h[:, b * TB:(b + 1) * TB, :], h[:, b * TB:(b + 1) * TB, :],
                                             pos_sb[:], ALU.add))
                norm_stats(b, h)

            def qkv_parts(b):
                dve.wait_ge(part_cast, 2 * b + 1)
                nc.vector.tensor_tensor(qk_rest[:], qk[:, b % 2], qk_part[:, b % 2, :, 0, :],
                                        ALU.subtract).then_inc(part_rest, 1)
                dve.wait_ge(qkv_full, b + 1)
                vp = ps[:, QKV_BANK[b] + 2, :].rearrange("p (t h e) -> p t h e", t=TB, h=H)
                nc.vector.tensor_tensor(v_aug[:, b * TB:(b + 1) * TB, :, 0:HD], vp,
                                        vb_sb[:].rearrange("p (o h e) -> p o h e", o=1, h=H)
                                        .to_broadcast([P, TB, H, HD]), ALU.add).then_inc(v_read, 1)
                dve.wait_ge(part_cast, 2 * b + 2)
                nc.vector.tensor_tensor(qk_part[:, b % 2, :, 2, :], qk_rest[:], qk_part[:, b % 2, :, 1, :],
                                        ALU.subtract).then_inc(parts_done, 1)
                dve.wait_ge(parts_done, b + 1)

            dve.wait_ge(pos_in, 16)
            embed(0)
            embed(1)
            normalise(0, h)
            normalise(1, h)
            dve.wait_ge(keys_in, 64)
            dve.wait_ge(ebw_in, 48)
            link(nc.vector.max_index(last[:], want_sb[:], keys))
            link(nc.vector.tensor_copy(last_f[:], last[:, 0:TB]))
            nc.vector.tensor_scalar(hit[:], last_f[:], float(EDGES), None, ALU.is_lt)
            nc.vector.tensor_scalar(last_i[:], last_f[:], float(EDGES - 1), None, ALU.min).then_inc(last_done, 1)
            dve.wait_ge(proj_in, 128)
            dve.wait_ge(ones_in, 1)
            qkv_parts(0)
            embed(2)
            embed(3)
            normalise(2, h)
            normalise(3, h)
            dve.wait_ge(attr_in, 16 * TB)
            link(nc.vector.tensor_tensor(
                cb_prod[:], ebw_sb[:, 0:3, :].rearrange("p f (o h) -> p o h f", o=1).to_broadcast([P, TB, H, 3]),
                edge_a[:].rearrange("p t (o f) -> p t o f", o=1).to_broadcast([P, TB, H, 3]), ALU.mult))
            link(nc.vector.tensor_reduce(cb[:, 0], cb_prod[:], AX.X, ALU.add))
            link(nc.vector.tensor_tensor(cb[:, 1], cb[:, 0], ebw_sb[:, 3:4, :].to_broadcast([P, TB, H]), ALU.add))
            link(nc.vector.tensor_tensor(cb[:, 2], cb[:, 1], hit[:].rearrange("p (t o) -> p t o", o=1)
                                         .to_broadcast([P, TB, H]), ALU.mult))
            cbv = cb[:, 2].rearrange("p t h -> p h t")
            link(nc.vector.tensor_copy(cb_part[:, 0], cbv))
            link(nc.vector.tensor_tensor(cb_rest[:], cbv, cb_part[:, 0], ALU.subtract))
            link(nc.vector.tensor_copy(cb_part[:, 1], cb_rest[:]))
            nc.vector.tensor_tensor(cb_part[:, 2], cb_rest[:], cb_part[:, 1], ALU.subtract).then_inc(cb_parts, 1)
            qkv_parts(1)

            lg, ex, pr, top = small[:, 16:32], small[:, 32:48], small[:, 48:64], small[:, 64:72]

            def gate(g):
                dve.wait_ge(ffn_in, 32)
                dve.wait_ge(gate_full, 2 * g + 1)
                link(nc.vector.scalar_tensor_tensor(lg, ps[0:2, 6 * g, 0:EXPERTS0], 1.0 / N, bg_sb[0:2], ALU.mult,
                                                    ALU.add))
                nc.vector.tensor_reduce(small[:, 80:81], lg, AX.X, ALU.max, negate=True).then_inc(gate_full, 1)
                dve.wait_ge(gate_exp, g + 1)
                link(nc.vector.reciprocal(small[:, 82:83], small[:, 81:82]))
                link(nc.vector.tensor_scalar(pr, ex, small[:, 82:83], None, ALU.mult))
                link(nc.vector.max(top, pr))
                link(nc.vector.max_index(top_i[:], top, pr))
                link(nc.vector.tensor_copy(small[:, 83:84], top_i[:, 0:1]))
                nc.vector.tensor_scalar(small[:, 0:2], id_f[0:2, 0:2], small[:, 83:84], None, ALU.mult)
                nc.vector.tensor_scalar(small[:, 2:4], id_f[0:2, 0:2], top[:, 0:1], None,
                                        ALU.mult).then_inc(gate_diag, 1)

            def pick(g):
                dve.wait_ge(gate_rows, g + 1)
                dve.wait_ge(lane_in, 16)
                link(nc.vector.tensor_copy(pick_b[:, g, :], ps[:, 6 * g, 32:36]))
                nc.vector.tensor_scalar(off_w[:, 2 * g:2 * g + 2], pick_b[:, g, 0:2], float(D), lane_sb[:], ALU.mult,
                                        ALU.add)
                nc.vector.tensor_copy(off_b[:, 2 * g:2 * g + 2], pick_b[:, g, 0:2]).then_inc(gate_off, 1)

            def gate_of(b):
                return pick_b[:, b // 2, 2 + b % 2:3 + b % 2]

            def update(b):
                hb = h[:, b * TB:(b + 1) * TB, :]
                dve.wait_ge(bias_in[b], 16)
                link(nc.vector.tensor_scalar(b_sel[:, 1, b, :], b_sel[:, 0, b, :], gate_of(b), None, ALU.mult))
                link(nc.vector.tensor_tensor(hb, hb, b_sel[:, 1, b:b + 1, :].to_broadcast([P, TB, D]), ALU.add))
                dve.wait_ge(y0_full, b + 1)
                link(nc.vector.tensor_tensor(hb, hb, ps[:, b % 2, :].rearrange("p (t d) -> p t d", t=TB), ALU.add))
                norm_stats(b, h)

            def convolve(b, halves):
                dve.wait_ge(xi_done, b + 1)
                for half in halves:
                    if b >= 2:
                        dve.wait_ge(xc_done, NH * (b - 2) + half + 1)
                    c0, c1 = conv[b % 2][:, half, 0, :], conv[b % 2][:, half, 1, :]
                    link(nc.vector.tensor_scalar(c0, xi[:, half, b, 0:N], cw_sb[:, half, 0:1], None, ALU.mult))
                    link(nc.vector.scalar_tensor_tensor(c1, xi[:, half, b, 1:1 + N], cw_sb[:, half, 1:2], c0,
                                                        ALU.mult, ALU.add))
                    link(nc.vector.scalar_tensor_tensor(c0, xi[:, half, b, 2:2 + N], cw_sb[:, half, 2:3], c1,
                                                        ALU.mult, ALU.add))
                    nc.vector.scalar_tensor_tensor(c1, xi[:, half, b, 3:3 + N], cw_sb[:, half, 3:4], c0,
                                                   ALU.mult, ALU.add).then_inc(conv_done, 1)

            for now in SLOTS:
                for piece in now:
                    kind, k, j = piece
                    if kind == "parts":
                        qkv_parts(k)
                    if kind == "score":
                        g, hh, n = k // G, k % G, TB * k + j
                        dve.wait_ge(scores_full, n + 1)
                        nc.vector.tensor_reduce(nmax[:, g % 2, hh * TB + j:hh * TB + j + 1], ps[:, n % 2, :],
                                                AX.X, ALU.max, negate=True).then_inc(scores_read, 1)
                        if hh == G - 1 and j == TB - 1:
                            dve.wait_ge(scores_read, TB * (k + 1))
                            m = nmax[:, g % 2]
                            link(nc.vector.tensor_copy(nmax_part[:, g % 2, 0], m))
                            link(nc.vector.tensor_tensor(nmax_rest[:], m, nmax_part[:, g % 2, 0], ALU.subtract))
                            link(nc.vector.tensor_copy(nmax_part[:, g % 2, 1], nmax_rest[:]))
                            nc.vector.tensor_tensor(nmax_part[:, g % 2, 2], nmax_rest[:], nmax_part[:, g % 2, 1],
                                                    ALU.subtract).then_inc(max_parts, 1)
                            dve.wait_ge(max_parts, g + 1)
                    if kind in ("turn_out", "project"):
                        dve.wait_ge(bank_full, BANK_USE[piece] + 1)
                    if kind == "turn_out":
                        g = k % NG
                        o = ps[:, 7, :].rearrange("p (t g e) -> p t g e", t=TB, g=G)
                        link(nc.vector.reciprocal(r_den[:], o[:, :, :, HD]))
                        nc.vector.tensor_tensor(
                            o_nat[:, :, g * G:(g + 1) * G, :], o[:, :, :, 0:HD],
                            r_den[:].rearrange("p t (g o) -> p t g o", o=1).to_broadcast([P, TB, G, HD]),
                            ALU.mult).then_inc(bank_read, 1)
                    if kind == "project":
                        hb = h[:, k * TB:(k + 1) * TB, :]
                        nc.vector.tensor_tensor(hb, hb, ps[:, 7, :].rearrange("p (t d) -> p t d", t=TB),
                                                ALU.add).then_inc(bank_read, 1)
                        dve.wait_ge(bank_read, BANK_USE[piece] + 1)
                        norm_stats(k, h)
                    if kind in ("normalise", "renorm"):
                        normalise(k, h)
                    if kind == "gate":
                        gate(k)
                    if kind == "pick":
                        pick(k)
                    if kind == "select":
                        dve.wait_ge(emb_in[k], 16 * (TB + 1))
                        nc.vector.tensor_scalar(w_sel[:, 1, k, :], w_sel[:, 0, k, :], gate_of(k), None,
                                                ALU.mult).then_inc(sel_done, 1)
                    if kind == "update":
                        update(k)
                    if kind == "conv":
                        if k == j == 0:
                            dve.wait_ge(mamba_in, 16 * 12)
                            dve.wait_ge(pads_set, 1)
                            for half in range(NH):
                                ins = nc.vector.tensor_scalar(d_diag[:, half, :], id_f[:], ds_sb[:, half:half + 1],
                                                              None, ALU.mult)
                            ins.then_inc(diag_done, 1)
                        convolve(k, (j,))

            def c_left_over(b):
                cols = slice(b * N, (b + 1) * N)
                dve.wait_ge(c_cast, b + 1)
                nc.vector.tensor_tensor(c_rest[:, b, :], ps[:, b, :], c_stack[:, cols],
                                        ALU.subtract).then_inc(c_rest_done, 1)

            def dt_relu_of(b):
                for half in range(NH):
                    k = NH * b + half
                    dve.wait_ge(dt_abs, k + 1)
                    nc.vector.tensor_scalar(dtx[:, half, b * N:(b + 1) * N], ps[:, 4 + k % 4, :],
                                            bdt_sb[:, half:half + 1], 0.0, ALU.add, ALU.max).then_inc(dt_relu, 1)

            def dt_of(q, half):
                dve.wait_ge(dt_relu, NH * 2 * q + NH + half + 1)
                dve.wait_ge(xc_done, NH * 2 * q + NH + half + 1)
                dve.wait_ge(dt_log, NH * q + half + 1)
                d_, x_ = dt[:, half, q * SPAN:(q + 1) * SPAN], dtx[:, half, q * SPAN:(q + 1) * SPAN]
                nc.vector.tensor_tensor(d_, d_, x_, ALU.add).then_inc(dt_done, 1)
                dve.wait_ge(dt_done, NH * q + half + 1)
                nc.vector.tensor_tensor(x_, d_, xc[:, half, q * SPAN:(q + 1) * SPAN], ALU.mult).then_inc(dtx_done, 1)

            c_left_over(0)
            dt_relu_of(0)
            dve.sem_inc(scanned, 4)
            dve.sem_inc(read_full, NH)
            c_left_over(1)
            dt_relu_of(1)
            c_left_over(2)
            c_left_over(3)
            dt_of(0, 0)
            dt_of(0, 1)
            dt_relu_of(2)
            dt_relu_of(3)
            for q in range(NSPAN):
                with dve.Fori(0, DS // SU) as i:
                    for j in range(SU):
                        for half in range(NH):
                            n = NH * j + half
                            unit = q * NH * DS + n
                            dve.wait_ge(decay_full, i * (NH * SU) + (unit + 1))
                            dve.wait_ge(drive_full, i * (NH * SU) + (unit + 1 + NH * SU))
                            dve.wait_ge(read_full, i * (NH * SU) + (unit + 1))
                            nc.vector.tensor_tensor_scan(state[:, half, :], decay[:, n % 4, :], drive[:, n % 4, :],
                                                         0.0, ALU.mult, ALU.add).then_inc(scanned, 1)
                        dve.wait_ge(c_full, i * SU + (q * (DS + 1) + j + 1))
                        for half in range(NH):
                            unit = q * NH * DS + NH * j + half
                            dve.wait_ge(scanned, i * (NH * SU) + (unit + 5))
                            dve.wait_ge(y_added, i * (NH * SU) + (unit + 1))
                            product = read_out[:, (NH * j + half) % 4, :]
                            nc.vector.tensor_tensor(product.rearrange("p (b n) -> p b n", n=N),
                                                    state[:, half, :].rearrange("p (b n) -> p b n", n=N),
                                                    ps[:, 4 + 2 * (j % 2):6 + 2 * (j % 2), :], ALU.mult
                                                    ).then_inc(read_full, 1)
                if q == 0:
                    dt_of(1, 0)
                dve.wait_ge(y_full, q + 1)
                for half in range(NH):
                    s_ = sz[:, half, q * SPAN:(q + 1) * SPAN].rearrange("p (b n) -> p b n", n=N)
                    nc.vector.tensor_tensor(s_, ps[:, 2 * half:2 * half + 2, :], s_, ALU.mult).then_inc(y_done, 1)
                if q == 0:
                    dt_of(1, 1)
            for norm, b in LAST_NORMS:
                xb, hb = xn[:, b * TB:(b + 1) * TB, :], h[:, b * TB:(b + 1) * TB, :]
                if norm == "own":
                    dve.wait_ge(out1_full, b + 1)
                    nc.vector.tensor_tensor(xb, xb, ps[:, 4 + b, :].rearrange("p (t d) -> p t d", t=TB),
                                            ALU.add).then_inc(out1_read, 1)
                    dve.wait_ge(out1_read, b + 1)
                    norm_stats(b, xn)
                else:
                    dve.wait_ge(ln_done, 3 * B + LAST_NORMS.index(("own", b)) + 1)
                    link(nc.vector.tensor_tensor(xb, xb, gamma_sb[:].rearrange("p (o d) -> p o d", o=1)
                                                 .to_broadcast([P, TB, D]), ALU.mult))
                    if b == 0:
                        dve.wait_ge(beta_added, 1)
                    link(nc.vector.tensor_tensor(hb, hb, xb, ALU.add))
                    norm_stats(b, h)
            dve.wait_ge(logits_full, 1)
            lgp = ps[:, 4, 0:NT * E1].rearrange("p (i e) -> p i e", e=E1)

            def over_e(a):
                return a.rearrange("p (i o) -> p i o", o=1).to_broadcast([P, NT, E1])

            link(nc.vector.tensor_reduce(rowmax[:, 0, :], lgp, AX.X, ALU.max))
            nc.vector.tensor_tensor(logit[:], lgp, over_e(rowmax[:, 0, :]), ALU.subtract).then_inc(shifted, 1)
            dve.wait_ge(exped, 1)
            link(nc.vector.tensor_reduce(rowmax[:, 1, :], prob[:], AX.X, ALU.add))
            link(nc.vector.reciprocal(rowmax[:, 2, :], rowmax[:, 1, :]))
            nc.vector.tensor_tensor(prob[:], prob[:], over_e(rowmax[:, 2, :]), ALU.mult).then_inc(probs_done, 1)
            dve.wait_ge(probs_turned, 1)
            nc.vector.tensor_copy(prob_x[:], ps[:, 5, 0:2 * P]).then_inc(prob_x_done, 1)
            dve.wait_ge(prob_x_done, 1)
            dve.wait_ge(moe_in, 16 * 17)
            nc.vector.tensor_copy(cand[:], bits_sb[:, 0, :]).then_inc(bit_step, 1)

            def search(i, step):
                def bits(step, k0, k1):
                    return bits_sb[:, bass.ds(i * 4 + step, 1), k0:k1].rearrange("p o k -> p (o k)")

                dve.wait_ge(bit_step, i * 16 + (4 * step + 1))
                for k in range(3):
                    ins = nc.vector.tensor_scalar(hits_x[:, k], prob_x[:], cand[:, k + 1:k + 2].bitcast(F32), None,
                                                  ALU.is_ge, ALU.add, accum_out=count[:, k:k + 1])
                ins.then_inc(counted, 1)
                nc.vector.tensor_tensor(base[:], cand[:, 0:1].to_broadcast([P, 4]), bits(step + 1, 0, 4),
                                        ALU.bitwise_or).then_inc(bit_step, 1)
                dve.wait_ge(summed, i * 4 + (step + 1))
                nc.vector.tensor_scalar(reach[:], ps[:, 6, 0:3], float(CAP) - 0.5, None, ALU.is_gt, ALU.add,
                                        accum_out=reached[:]).then_inc(bit_step, 1)
                dve.wait_ge(bit_step, i * 16 + (4 * step + 3))
                nc.vector.tensor_tensor(gained[:], reached[:], bits(step, 1, 2), ALU.mult).then_inc(bit_step, 1)
                dve.wait_ge(bit_step, i * 16 + (4 * step + 4))
                nc.vector.tensor_tensor(cand[:], base[:], gained[:].to_broadcast([P, 4]),
                                        ALU.bitwise_or).then_inc(bit_step, 1)

            with dve.Fori(0, STEPS // 4) as i:
                for step in range(4):
                    search(i, step)
            for step in range(STEPS % 4):
                search(STEPS // 4, step)
            dve.wait_ge(bit_step, 4 * STEPS + 1)
            nc.vector.tensor_scalar(thr_b[:], ones_f[:], cand[:, 0:1].bitcast(F32), None,
                                    ALU.mult).then_inc(thr_ready, 1)
            dve.wait_ge(thr_turned, 1)
            link(nc.vector.tensor_copy(thr_n[:], ps[:, 6, P:P + E1]))
            pe_t = prob[:].rearrange("p i e -> p e i")

            def over_i(a):
                return a.rearrange("p (e o) -> p e o", o=1).to_broadcast([P, E1, NT])

            def flat(a):
                return a.rearrange("p e i -> p (e i)")

            link(nc.vector.tensor_tensor(over[:], pe_t, over_i(thr_n[:]), ALU.is_gt))
            link(nc.vector.tensor_tensor(even[:], pe_t, over_i(thr_n[:]), ALU.is_equal))

            def runs(mask, k):
                link(nc.vector.tensor_tensor_scan(flat(run[:, k]), start_sb[:], flat(mask), 0.0, ALU.mult, ALU.add))

            link(nc.vector.tensor_copy(picked[:, 2], over[:]))
            runs(over[:], 0)
            runs(even[:], 1)
            link(nc.vector.tensor_copy(run_b[:, 0], run[:, 0]))
            nc.vector.tensor_tensor(run_b[:, 1], run[:, 1], even[:], ALU.subtract).then_inc(runs_done, 1)
            dve.wait_ge(ranks_full, 1)
            link(nc.vector.tensor_scalar(need[:], ps[:, 5, 256:256 + E1], -1.0, float(CAP), ALU.mult, ALU.add))
            link(nc.vector.tensor_tensor(picked[:, 0], ps[:, 5, 0:256].rearrange("p (e i) -> p e i", e=E1),
                                         over_i(need[:]), ALU.is_lt))
            link(nc.vector.tensor_tensor(picked[:, 1], picked[:, 0], even[:], ALU.mult))
            link(nc.vector.tensor_tensor(picked[:, 0], picked[:, 1], picked[:, 2], ALU.add))
            link(nc.vector.tensor_copy(picked_b[:], picked[:, 0]))
            runs(picked_b[:], 0)
            nc.vector.tensor_tensor(run_b[:, 0], run[:, 0], picked_b[:], ALU.subtract).then_inc(runs_done, 1)
            dve.wait_ge(ranks_full, 2)
            link(nc.vector.tensor_copy(slot_i[:, 0], ps[:, 6, 256:512].rearrange("p (e i) -> p e i", e=E1)))
            nc.vector.tensor_single_scalar(slot_i[:, 1], slot_i[:, 0], 3, ALU.arith_shift_right)
            link(nc.vector.tensor_single_scalar(slot_i[:, 2], slot_i[:, 0], B1 - 1, ALU.bitwise_and))
            nc.vector.scalar_tensor_tensor(slot_b[:, 0], slot_i[:, 1], 1.0, picked[:, 0], ALU.add, ALU.mult)
            link(nc.vector.tensor_copy(slot_b[:, 1], slot_i[:, 2]))
            nc.vector.tensor_tensor(
                hot_b[:], bi_sb[:].rearrange("p (o b) -> p o b", o=1).to_broadcast([P, E1 * NT, B1]),
                slot_b[:, 1].rearrange("p e (i o) -> p (e i) o", o=1).to_broadcast([P, E1 * NT, B1]),
                ALU.is_equal).then_inc(hot_done, 1)
            dve.wait_ge(hot_done, 1)
            nc.vector.tensor_tensor(val_b[:].rearrange("p e i k b -> p (e i) k b")[:, :, 1, :], hot_b[:], tile_sb[:],
                                    ALU.mult)
            for g in range(2):
                part = slice(g * B1, (g + 1) * B1)
                nc.vector.tensor_tensor(
                    hot_a[:, :, part].rearrange("p i e a -> p e i a"),
                    ai_sb[:].rearrange("p (o u a) -> p o u a", o=1, u=1).to_broadcast([P, B1, NT, A1]),
                    slot_b[:, 0, part].rearrange("p e (i o) -> p e i o", o=1).to_broadcast([P, B1, NT, A1]),
                    ALU.is_equal).then_inc(hot_done, 1)
            for g in range(2):
                dve.wait_ge(idx_full, g + 1)
                link(nc.vector.tensor_tensor(
                    diag[:], ps[:, 5 + 2 * g, 0:P].rearrange("p (e k) -> p e k", e=B1),
                    own_sb[:].rearrange("p (e o) -> p e o", o=1).to_broadcast([P, B1, 2 * B1]), ALU.mult))
                link(nc.vector.tensor_reduce(idx_v[:, g, :], diag[:].rearrange("p e k -> p k e"), AX.X, ALU.add))
                link(nc.vector.scalar_tensor_tensor(idx_f[:, g, :], idx_v[:, g, B1:], float(P), idx_v[:, g, 0:B1],
                                                    ALU.mult, ALU.add))
                nc.vector.tensor_tensor(
                    idx_x[:, g], idx_f[:, g, :].rearrange("p (o b) -> p o b", o=1).to_broadcast([P, A1, B1]),
                    own_a_sb[:].rearrange("p (a o) -> p a o", o=1).to_broadcast([P, A1, B1]),
                    ALU.mult).then_inc(idx_spread, 1)
            for g in range(2):
                dve.wait_ge(idx_turned, g + 1)
                nc.vector.tensor_copy(idx_t[:, g * B1:(g + 1) * B1], ps[:, 5 + 2 * g, 256:256 + B1]
                                      ).then_inc(idx_done, 1)

            def expert_bias(e):
                dve.wait_ge(eh_full, e + 1)
                if e >= 2:
                    dve.wait_ge(eh_done, e - 1)
                nc.vector.tensor_tensor(pre[:, e % 2], ps[:, 1 + e % 2, :].rearrange("p (c n) -> p c n", c=HC),
                                        b1_sb[:, e, :].rearrange("p (c o) -> p c o", o=1).to_broadcast([P, HC, P]),
                                        ALU.add).then_inc(pre_done, 1)

            expert_bias(0)
            for e in range(E1):
                if e + 1 < E1:
                    expert_bias(e + 1)
                dve.wait_ge(ey_full, e + 1)
                nc.vector.tensor_scalar(routed[:, e, :], ps[:, 3 + 2 * (e % 2), 0:P],
                                        rows[:, e, D + e:D + e + 1], None, ALU.mult).then_inc(routed_done, 1)

        @block.tensor
        def _(pe):
            mm, tr = nc.tensor.matmul, nc.tensor.transpose
            pe.wait_ge(const_in, 32)
            def turn(b):
                pe.wait_ge(ln_done, b + 1)
                if b >= 2:
                    pe.wait_ge(xT_done, b - 1)
                for i in range(TB):
                    ins = tr(ps[:, 6 + b % 2, tile_cols(i)], xn[:, b * TB + i, :], id_f[:])
                ins.then_inc(turned, 1)

            def project(b):
                if b == 0:
                    pe.wait_ge(proj_in, 128)
                if b >= 2:
                    pe.wait_ge(part_cast, 3)
                    pe.wait_ge(v_read, b - 1)
                    pe.wait_ge(cb_rows, 1)
                pe.wait_ge(xT_done, b + 1)
                cols = slice(b * N, (b + 1) * N)
                mm(ps[:, QKV_BANK[b], :], wq_sb[:], xT[:, cols], start=True, stop=True)
                mm(ps[:, QKV_BANK[b] + 1, :], wk_sb[:], xT[:, cols], start=True, stop=True)
                for i in range(TB):
                    ins = mm(ps[:, QKV_BANK[b] + 2, tile_cols(i)], xT[:, b * N + i * P:b * N + (i + 1) * P], wv_sb[:],
                             start=True, stop=True)
                ins.then_inc(qkv_full, 1)

            turn(0)
            turn(1)
            project(0)
            project(1)
            turn(2)
            turn(3)
            pe.wait_ge(cb_parts, 1)
            pe.wait_ge(xT_done, B)
            tr(ps[0:3 * H * TB, 7, 0:P // 2].bitcast(BF16), cb_part[:].rearrange("p j h t -> p (j h t)"),
               id_b[:]).then_inc(cb_turned, 1)
            pe.wait_ge(cb_in, 16 * 3)
            pe.wait_ge(row_in, 32)
            pe.wait_ge(minus_half_set, 2)
            pe.wait_ge(cb_rows, 1)
            pe.wait_ge(part_cast, 1)
            for now in SLOTS:
                for piece in now:
                    kind, k, j = piece
                    if kind in BANK_USES:
                        use = BANK_USE[piece]
                        if use:
                            pe.wait_ge(bank_read, use)
                    if kind == "score":
                        b, hh, n = k // H, k % H, TB * k + j
                        if hh == 0 and j == 0:
                            pe.wait_ge(stack_in[b], 16 * STACK_LOADS)
                        if n >= 2:
                            pe.wait_ge(scores_read, n - 1)
                        mm(ps[:, n % 2, :], q_stack[0:ROWS_A, b % 3, hh, tile_cols(j)],
                           k_stack[0:ROWS_A, b % 3, hh, :], start=True, stop=True).then_inc(scores_full, 1)
                    if kind == "qkv":
                        project(k)
                    if kind == "turn_max":
                        pe.wait_ge(max_parts, k + 1)
                        pe.wait_ge(v_read, B)
                        tr(ps[0:3 * G * TB, 7, 0:P // 2].bitcast(BF16),
                           nmax_part[:, k % 2].rearrange("p j m -> p (j m)"), id_b[:]).then_inc(bank_full, 1)
                    if kind == "prob":
                        b, hh, g, n = k // H, k % H, k // G, 2 * k + j
                        if n < 2:
                            pe.wait_ge(part_cast, 2 * B)
                        if k % G == 0 and j == 0:
                            pe.wait_ge(max_in[g % 2], 16 * (g // 2 + 1))
                        if n >= 2:
                            pe.wait_ge(expo_read, n - 1)
                        for t in range(2 * j, 2 * j + 2):
                            ins = mm(ps[:, 2 + t, :], k_stack[0:ROWS_B, b % 3, hh, tile_cols(t)],
                                     q_stack[0:ROWS_B, b % 3, hh, :], start=True, stop=True)
                        ins.then_inc(expo_full, 1)
                    if kind == "pv":
                        b, g = k // NG, k % NG
                        pe.wait_ge(expo_read, 2 * G * (k + 1) - (1 if j < 2 else 0))
                        if k and j == 0:
                            pe.wait_ge(pv_read, k)
                        for i in range(G):
                            ins = mm(ps[32 * i:32 * i + 32, 6, :], v_aug[:, b * TB + j, g * G + i, :],
                                     probs[:, k % 2, i, j, :], start=(j == 0), stop=(j == TB - 1))
                        if j == TB - 1:
                            ins.then_inc(pv_full, 1)
                    if kind == "turn_out":
                        pe.wait_ge(pv_read, k + 1)
                        for t in range(TB):
                            ins = tr(ps[:, 7, tile_cols(t)], oT[:, k % 2, tile_cols(t)], id_f[:])
                        ins.then_inc(bank_full, 1)
                    if kind == "turn_back":
                        for t in range(TB):
                            ins = tr(ps[:, 7, tile_cols(t)], o_nat[:, t].rearrange("p h e -> p (h e)"), id_f[:])
                        ins.then_inc(bank_full, 1)
                    if kind == "project":
                        for t in range(TB):
                            mm(ps[:, 7, tile_cols(t)], ones_f[0:1, :], ob_sb[:], start=True, stop=False)
                            ins = mm(ps[:, 7, tile_cols(t)], onT[:, tile_cols(t)], wo_sb[:], start=False, stop=True)
                        ins.then_inc(bank_full, 1)
                    if kind == "norm":
                        pe.wait_ge(ln_done, NORMED["normalise", k, 0])
                        for t in range(TB):
                            ins = tr(ps[:, 7, tile_cols(t)], xn[:, k * TB + t, :], id_f[:])
                        ins.then_inc(bank_full, 1)
                    if kind == "gate":
                        pe.wait_ge(bank_read, BANK_USE["norm", 2 * k + 1, 0] + 1)
                        pe.wait_ge(ffn_in, 32)
                        if k:
                            pe.wait_ge(pv_read, UNITS // G)
                        mm(ps[0:2, 6 * k, 0:EXPERTS0], pooled[:, 2 * k:2 * k + 2], wg_sb[:], start=True,
                           stop=True).then_inc(gate_full, 1)
                    if kind == "pick":
                        pe.wait_ge(gate_diag, k + 1)
                        mm(ps[:, 6 * k, 32:36], ones_f[0:2, :], small[:, 0:4], start=True, stop=True
                           ).then_inc(gate_rows, 1)
                    if kind == "select":
                        pe.wait_ge(sel_done, k + 1)
                        if k >= 2:
                            pe.wait_ge(xT3_done, k - 1)
                        for t in range(TB):
                            ins = mm(ps[:, k % 2, tile_cols(t)], xT[:, k * N + t * P:k * N + (t + 1) * P],
                                     w_sel[:, 1, k, :], start=True, stop=True)
                        ins.then_inc(y0_full, 1)
                    if kind == "renorm":
                        pe.wait_ge(ln_done, NORMED[piece])
                        for t in range(TB):
                            ins = tr(ps[:, k % 2, tile_cols(t)], xn[:, k * TB + t, :], id_f[:])
                        ins.then_inc(turned3, 1)
                    if kind == "expand":
                        pe.wait_ge(xT3_done, k + 1)
                        if k == 0:
                            pe.wait_ge(mamba_in, 16 * 12)
                            pe.wait_ge(expo_read, 2 * UNITS)
                        for n in range(4):
                            if k:
                                pe.wait_ge(xi_done if n < 2 else z_done, k)
                            ins = mm(ps[:, 2 + n, :], win_sb[:, tile_cols(n)], xT[:, k * N:(k + 1) * N], start=True,
                                     stop=True)
                            if n % 2:
                                ins.then_inc(xz_full, 1)

            def project_x(b):
                pe.wait_ge(xc_done, NH * (b + 1))
                for half in range(NH):
                    ins = mm(ps[:, b, :], wx_sb[:, half, :], xc[:, half, b * N:(b + 1) * N],
                             start=(half == 0), stop=(half == NH - 1))
                ins.then_inc(dbl_full, 1)

            def project_dt(b):
                pe.wait_ge(dbl_done, b + 1)
                for half in range(NH):
                    k = NH * b + half
                    if k >= 4:
                        pe.wait_ge(dt_relu, k - 3)
                    mm(ps[:, 4 + k % 4, :], wdt_sb[:, tile_cols(half)], dbl[0:DR, b * N:(b + 1) * N],
                       start=True, stop=True).then_inc(dt_full, 1)

            pe.wait_ge(z_done, B)
            project_x(0)
            project_x(1)
            project_dt(0)
            project_dt(1)
            project_x(2)
            project_x(3)
            project_dt(2)
            project_dt(3)
            pe.wait_ge(diag_done, 1)
            pe.sem_inc(y_added, 4)
            def spread_c(q, state, bank):
                for b in range(2):
                    ins = mm(ps[:, bank + b, :], pick_sb[:, state, :].rearrange("p o m -> p (o m)"),
                             c_stack[:, q * SPAN + b * N:q * SPAN + (b + 1) * N], start=True, stop=True)
                ins.then_inc(c_full, 1)

            def start_y(q):
                for half in range(NH):
                    if q:
                        pe.wait_ge(y_done, NH * (q - 1) + half + 1)
                    for b in range(2):
                        mm(ps[:, 2 * half + b, :], d_diag[:, half, :],
                           xc[:, half, q * SPAN + b * N:q * SPAN + (b + 1) * N], start=True, stop=True)

            for q in range(NSPAN):
                if q == 0:
                    pe.wait_ge(c_cast, B)
                    pe.wait_ge(c_rest_done, B)
                    start_y(0)
                    pe.wait_ge(c_done, 4)
                    pe.wait_ge(dt_abs, NH * B)
                    pe.wait_ge(dt_relu, NH * B)
                    pe.wait_ge(read_full, NH)
                    spread_c(0, slice(0, 1), 4)
                else:
                    pe.wait_ge(read_full, NH * q * DS)
                    pe.wait_ge(late_c_done, B - 2)
                    pe.wait_ge(late_mid_done, 2 * (B - 2))
                    spread_c(q, slice(0, 1), 4)
                    start_y(q)
                with pe.Fori(0, DS // SU) as i:
                    for j in range(SU):
                        pe.wait_ge(read_full, i * (NH * SU) + NH * (q * DS + j + 1))
                        spread_c(q, bass.ds(i * SU + (j + 1), 1), 4 + 2 * ((j + 1) % 2))
                        for half in range(NH):
                            pe.wait_ge(read_full, i * (NH * SU) + (q * NH * DS + NH * j + half + 1 + NH))
                            for b in range(2):
                                ins = mm(ps[:, 2 * half + b, :], id_f[:],
                                         read_out[:, (NH * j + half) % 4, b * N:(b + 1) * N],
                                         start=False, stop=True, skip_group_check=True)
                            ins.then_inc(y_added, 1)
                pe.wait_ge(y_added, (q + 1) * 2 * DS + 4)
                pe.sem_inc(y_full, 1)
            pe.wait_ge(read_full, NH + NH * NSPAN * DS)
            for b in range(B):
                pe.wait_ge(y_done, NH * (b // 2 + 1))
                for t in range(TB):
                    cols = slice(b * N + t * P, b * N + (t + 1) * P)
                    for half in range(NH):
                        ins = mm(ps[:, 4 + b, tile_cols(t)], sz[:, half, cols], wout_sb[:, half, :],
                                 start=(half == 0), stop=(half == NH - 1))
                ins.then_inc(out1_full, 1)
            pe.wait_ge(moe_in, 16 * 17)
            for b in range(B + 1):
                if b < B:
                    pe.wait_ge(ln_done, 3 * B + LAST_NORMS.index(("next", b)) + 1)
                    for t in range(TB):
                        ins = tr(ps[:, b, tile_cols(t)], xn[:, b * TB + t, :], id_f[:])
                    ins.then_inc(turned4, 1)
                if b:
                    pe.wait_ge(xT4_done, b)
                    if b == 1:
                        pe.wait_ge(out1_read, 1)
                    for t in range((b - 1) * TB, b * TB):
                        ins = mm(ps[:, 4, t * E1:(t + 1) * E1], xT[:, tile_cols(t)], gw_sb[:], start=True, stop=True)
            ins.then_inc(logits_full, 1)
            pe.wait_ge(probs_done, 1)
            for k in range(2):
                ins = tr(ps[:, 5, tile_cols(k)], prob[:, k * 8:(k + 1) * 8, :].rearrange("p i e -> p (i e)"), id_f[:])
            ins.then_inc(probs_turned, 1)
            pe.wait_ge(shifted, 1)
            pe.wait_ge(prob_x_done, 1)
            pe.sem_inc(sy_full, 1)

            def sum_and_shared(i, step, search=True, last=False):
                if search:
                    pe.wait_ge(counted, i * 4 + (step + 1))
                    mm(ps[:, 6, 0:3], same_sb[:], count[:], start=True, stop=True).then_inc(summed, 1)
                if last:
                    pe.wait_ge(thr_ready, 1)
                    tr(ps[:, 6, P:2 * P], thr_b[:], id_f[:]).then_inc(thr_turned, 1)
                for k in range(2 * (step % 2), 2 * (step % 2) + 2):
                    if step < 2:
                        pe.wait_ge(shid_done, i * HC + (k + 1))
                        mm(ps[:, k, :], sw1_sb[:, tile_cols(k)], xT[:, bass.ds(i * N, N)], start=True,
                           stop=True).then_inc(shid_full, 1)
                    else:
                        if k == 0:
                            pe.wait_ge(shid_done, i * HC + 2 * HC)
                            pe.wait_ge(shared_done, i + 1)
                        for c in range(HC):
                            ins = mm(ps[:, 7, tile_cols(k)], shid[:, c, tile_cols(k)], sw2_sb[:, c, :],
                                     start=(c == 0), stop=(c == HC - 1))
                        if k == TB - 1:
                            ins.then_inc(sy_full, 1)

            with pe.Fori(0, B - 1) as i:
                for step in range(4):
                    sum_and_shared(i, step)
            for step in range(4):
                n = 4 * (B - 1) + step
                sum_and_shared(B - 1, step, n < STEPS, n == STEPS - 1)
            pe.wait_ge(runs_done, 1)
            mm(ps[:, 5, 0:256], before_sb[:], even[:].rearrange("p e i -> p (e i)"), start=True, stop=False)
            mm(ps[:, 5, 0:256], onesb_sb[:], run_b[:, 1].rearrange("p e i -> p (e i)"), start=False, stop=True)
            mm(ps[:, 5, 256:256 + E1], onesb_sb[:], run_b[:, 0, :, NT - 1], start=True,
               stop=True).then_inc(ranks_full, 1)
            pe.wait_ge(runs_done, 2)
            mm(ps[:, 6, 256:512], before_sb[:], picked_b[:].rearrange("p e i -> p (e i)"), start=True, stop=False)
            mm(ps[:, 6, 256:512], onesb_sb[:], run_b[:, 0].rearrange("p e i -> p (e i)"), start=False,
               stop=True).then_inc(ranks_full, 1)
            pe.wait_ge(val_done, 1)
            for g in range(2):
                pe.wait_ge(hot_done, g + 2)
                if g:
                    pe.wait_ge(shared_done, B + 1)
                for t in range(NT):
                    ins = mm(ps[:, 5 + 2 * g, 0:P], hot_a[:, t, g * B1:(g + 1) * B1, :].rearrange("p e a -> p (e a)"),
                             val_b[:, g * B1:(g + 1) * B1, t].rearrange("p e k b -> p e (k b)"),
                             start=(t == 0), stop=(t == NT - 1))
                ins.then_inc(idx_full, 1)
            for g in range(2):
                pe.wait_ge(idx_spread, g + 1)
                mm(ps[:, 5 + 2 * g, 256:256 + B1], idx_x[:, g].rearrange("p a b -> p (a b)"), own_sb[:], start=True,
                   stop=True).then_inc(idx_turned, 1)
            pe.wait_ge(idx_done, 2)
            pe.wait_ge(moe_w_in, 16 * 8)

            def expert_in(e):
                pe.wait_ge(rows_in[e % AHEAD], 16 * (e // AHEAD + 1))
                if e >= 2:
                    pe.wait_ge(rowsT_done, e - 1)
                tr(ps[:, 4 * (e % 2), 0:P], rows[:, e, 0:D], id_f[:]).then_inc(rows_turned, 1)

            def expert_hidden(e):
                pe.wait_ge(rowsT_done, e + 1)
                if e >= 2:
                    pe.wait_ge(pre_done, e - 1)
                for c in range(HC):
                    ins = mm(ps[:, 1 + e % 2, tile_cols(c)], w1_sb[:, e, tile_cols(c)], rowsT[:, e % 2, :],
                             start=True, stop=True)
                ins.then_inc(eh_full, 1)

            def expert_out(e):
                pe.wait_ge(eh_done, e + 1)
                if e >= 2:
                    pe.wait_ge(routed_done, e - 1)
                o = ps[:, 3 + 2 * (e % 2), 0:P]
                mm(o, ones_f[0:1, :], b2_sb[:, e, :], start=True, stop=False)
                for c in range(HC):
                    ins = mm(o, hid[:, e % 2, c, :], w2_sb[:, e, c, :], start=False, stop=(c == HC - 1))
                ins.then_inc(ey_full, 1)

            expert_in(0)
            expert_in(1)
            expert_hidden(0)
            for e in range(E1):
                if e + 2 < E1:
                    expert_in(e + 2)
                if e + 1 < E1:
                    expert_hidden(e + 1)
                expert_out(e)


def _layout(x, L0_tok_W_emb, L0_tok_W_pos, L0_attn_edge_index, L0_attn_edge_attr, L0_attn_q_w, L0_attn_q_b,
            L0_attn_k_w, L0_attn_k_b, L0_attn_v_w, L0_attn_v_b, L0_attn_o_w, L0_attn_o_b, L0_attn_eb_w,
            L0_attn_eb_b, L0_ffn_Wg, L0_ffn_bg, L0_ffn_We, L0_ffn_be, L1_attn_W_in, L1_attn_conv_w, L1_attn_conv_b,
            L1_attn_W_xproj, L1_attn_W_dt, L1_attn_b_dt, L1_attn_A_log, L1_attn_D, L1_attn_W_out, L1_attn_gamma,
            L1_attn_beta, L1_ffn_gate_w, L1_ffn_w1, L1_ffn_b1, L1_ffn_w2, L1_ffn_b2, L1_ffn_sw1, L1_ffn_sb1,
            L1_ffn_sw2, L1_ffn_sb2):
    c = np.ascontiguousarray
    rows = lambda a: np.broadcast_to(a, (P,) + a.shape)
    wanted = np.full((P, 8), 2 * FAR, np.float32) + np.arange(8, dtype=np.float32)
    wanted[:, 0:TB] = np.arange(P)[:, None] + P * np.arange(TB)
    bf16 = mybir.dt.np(BF16)

    def halves(a):
        return c(a.reshape((NH, P) + a.shape[1:]).swapaxes(0, 1))

    by_dim = np.arange(P).reshape(H, HD).T.reshape(P)
    wx = np.zeros((DI, P), np.float32)
    wx[:, 0:DR] = L1_attn_W_xproj[:, 0:DR]
    wx[:, 16:16 + DS] = L1_attn_W_xproj[:, DR:DR + DS]
    pick = np.zeros((P, DS + 1, P), np.float32)
    for row in (32, 64, 96):
        wx[:, row:row + DS] = L1_attn_W_xproj[:, DR + DS:]
        pick[row + np.arange(DS), np.arange(DS)] = 1.0
    k = np.arange(P)
    steps = np.zeros((STEPS + 1, 4), np.int32)
    steps[0:STEPS] = np.arange(4) << np.arange(BITS - 2, -1, -2)[:, None]
    return {
        "ids": c(x.reshape(NT, P).T.astype(np.int32)),
        "emb": c(L0_tok_W_emb.T),
        "pos": c(L0_tok_W_pos.reshape(TB, P, D).transpose(1, 0, 2)),
        "edges": c(L0_attn_edge_index[:, ::-1].reshape(2, P, EDGES // P).transpose(1, 0, 2).astype(np.int32)),
        "wanted": wanted, "absent": wanted.astype(np.float16),
        "attrs": c(L0_attn_edge_attr[::-1]),
        "ebw": c(rows(np.concatenate([L0_attn_eb_w.T, L0_attn_eb_b[None]]))),
        "ident": np.eye(P, dtype=np.float32),
        "identb": np.eye(P, dtype=np.float32).astype(bf16),
        "ones": np.ones((3, 3, H, N), bf16),
        "wq": c(L0_attn_q_w.T[:, by_dim]), "wk": c(L0_attn_k_w.T[:, by_dim]), "wv": c(L0_attn_v_w.T),
        "wo": c(L0_attn_o_w.T),
        "qb": c(L0_attn_q_b[by_dim, None]), "kb": c(L0_attn_k_b[by_dim, None]),
        "vb": c(rows(L0_attn_v_b)), "ob": c(L0_attn_o_b[None]),
        "lane": np.arange(P, dtype=np.float32)[:, None],
        "wg0": L0_ffn_Wg, "bg0": c(np.broadcast_to(L0_ffn_bg, (B, EXPERTS0))),
        "we0": c(L0_ffn_We.reshape(EXPERTS0 * D, D)), "be0": L0_ffn_be,
        "w_in": L1_attn_W_in, "conv_w": halves(L1_attn_conv_w), "conv_b": halves(L1_attn_conv_b),
        "w_x": halves(wx), "c_pick": pick.astype(bf16), "w_dt": L1_attn_W_dt, "b_dt": halves(L1_attn_b_dt),
        "a_log": halves(L1_attn_A_log), "d_skip": halves(L1_attn_D), "w_out": halves(L1_attn_W_out),
        "gamma": c(rows(L1_attn_gamma)), "beta": c(rows(L1_attn_beta)),
        "gate_w": L1_ffn_gate_w, "w1": c(L1_ffn_w1.transpose(1, 0, 2)),
        "b1": c(L1_ffn_b1.reshape(E1, HC, P).transpose(2, 0, 1)),
        "w2": c(L1_ffn_w2.reshape(E1, HC, P, D).transpose(2, 0, 1, 3)), "b2": c(L1_ffn_b2[None]),
        "sw1": L1_ffn_sw1, "sb1": c(L1_ffn_sb1.reshape(HC, P).T),
        "sw2": c(L1_ffn_sw2.reshape(HC, P, D).transpose(1, 0, 2)), "sb2": c(rows(L1_ffn_sb2)),
        "same_expert": (k[:, None] % E1 == k[None] % E1).astype(np.float32),
        "bit_values": c(np.broadcast_to(steps, (P, STEPS + 1, 4)).astype(np.int32)),
        "before": (k[:, None] < k[None]).astype(bf16), "onesb": np.ones((P, P), bf16),
        "run_start": c(rows((np.arange(E1 * NT) % NT != 0).astype(np.float32))),
        "a_iota": c(rows(np.arange(1, A1 + 1)).astype(bf16)), "b_iota": c(rows(np.arange(B1)).astype(bf16)),
        "tile_of": c(np.broadcast_to((np.arange(E1 * NT) % NT)[:, None], (P, E1 * NT, B1)).astype(bf16)),
        "own_expert": (k[:, None] // A1 == np.arange(B1)[None]).astype(np.float32),
        "own_a": (k[:, None] % A1 == np.arange(A1)[None]).astype(np.float32),
    }


def kernel(**inputs):
    import concourse.bacc as bacc
    from concourse.bass_utils import run_bass_kernel_spmd

    arrays = _layout(**{k: np.asarray(v) for k, v in inputs.items()})
    nc = bacc.Bacc("TRN2", target_bir_lowering=False, num_devices=1)
    args = [nc.dram_tensor(name, a.shape, mybir.dt.from_np(a.dtype), kind="ExternalInput").ap()
            for name, a in arrays.items()]
    out = nc.dram_tensor("out", (T, D), F32, kind="ExternalOutput").ap()
    tower_kernel(nc, **dict(zip(arrays, args)), out=out)
    r = run_bass_kernel_spmd(nc, [arrays], core_ids=[0])
    return r.results[0]["out"].reshape(B, N, D)
```
